# Optimizing a Trainium2 kernel written in Bass

```python
import numpy as np
import jax
import jax.numpy as jnp

def _softmax(x, axis=-1):
    return jax.nn.softmax(x, axis=axis)

def _gelu(x):
    return jax.nn.gelu(x, approximate=True)

def _silu(x):
    return jax.nn.silu(x)

def _sigmoid(x):
    return jax.nn.sigmoid(x)

def _layernorm(x, axis=-1, eps=1e-05):
    m = jnp.mean(x, axis=axis, keepdims=True)
    v = jnp.var(x, axis=axis, keepdims=True)
    return (x - m) / jnp.sqrt(v + eps)

def _scatter_add(tgt, idx, src, axis=0):
    return tgt.at[idx].add(src)

def _segment_sum(src, seg, n):
    return jax.ops.segment_sum(src, seg, n)
kernel_name = 'mk_flamingo_gated_d1_seqx_r4_702775'

def setup_inputs(seed: int=0):
    np.random.seed(seed)
    _w = jnp.asarray

    def _rec_inputs():
        import jax
        import jax.numpy as jnp
        _rk = jax.random.key(seed)
        x = -7.109e-05 + 0.9999 * jax.random.normal(jax.random.fold_in(_rk, 1), (1, 2048, 256), jnp.float32)
        _lenS = 2048 - jax.random.randint(jax.random.fold_in(_rk, 7), (1,), 0, max(1, 2048 // 4) + 1, jnp.int32)
        _lenS2 = 1601 - jax.random.randint(jax.random.fold_in(_rk, 8), (1,), 0, max(1, 1601 // 4) + 1, jnp.int32)
        _ctx_768P = jax.random.normal(jax.random.fold_in(_rk, 11), (1, 16, 192), jnp.float32)
        _ctx_768c = jax.random.dirichlet(jax.random.fold_in(_rk, 511), 0.3 * jnp.ones((16,), jnp.float32), (1, 1601))
        _ctx_768t = jnp.einsum('bsk,bkd->bsd', _ctx_768c, _ctx_768P)
        _ctx_768t = _ctx_768t * jax.lax.rsqrt(jnp.mean(jnp.square(_ctx_768t)) + 1e-12) * 0.953939
        ctx_768 = 0.000486113 + 1.00014 * (_ctx_768t + 0.3 * jax.random.normal(jax.random.fold_in(_rk, 611), (1, 1601, 192), jnp.float32))
        _g = jax.random.normal(jax.random.fold_in(_rk, 9001), (2, 1), jnp.float32)
        _g = jnp.sign(_g) * jnp.maximum(jnp.abs(_g), 1.0) + (_g == 0) * 1.0
        g_xattn = _g[0]
        g_ffn = _g[1]
        return (x, ctx_768, g_xattn, g_ffn)
    x, ctx_768, g_xattn, g_ffn = _rec_inputs()

    def _L0_xattn_setup():
        import jax, jax.numpy as jnp
        import numpy as np
        N_HEADS = 8
        D_EMBED = 256
        D_CROSS = 192
        D_HEAD = D_EMBED // N_HEADS
        key = jax.random.key(seed)
        ks = jax.random.split(key, 10)
        B, Lq, Lkv = (16, 1024, 77)
        s_e = 1.0 / np.sqrt(D_EMBED)
        s_c = 1.0 / np.sqrt(D_CROSS)
        return {'x': jax.random.normal(ks[0], (B, Lq, D_EMBED), jnp.float32), 'y': jax.random.normal(ks[1], (B, Lkv, D_CROSS), jnp.float32), 'Wq': jax.random.normal(ks[2], (D_EMBED, D_EMBED), jnp.float32) * s_e, 'bq': jnp.zeros((D_EMBED,), jnp.float32), 'Wk': jax.random.normal(ks[3], (D_CROSS, D_EMBED), jnp.float32) * s_c, 'bk': jnp.zeros((D_EMBED,), jnp.float32), 'Wv': jax.random.normal(ks[4], (D_CROSS, D_EMBED), jnp.float32) * s_c, 'bv': jnp.zeros((D_EMBED,), jnp.float32), 'Wo': jax.random.normal(ks[5], (D_EMBED, D_EMBED), jnp.float32) * s_e, 'bo': jnp.zeros((D_EMBED,), jnp.float32)}
    _L0_xattn_all = _L0_xattn_setup()
    _L0_xattn_in = {k: v for k, v in _L0_xattn_all.items() if k in ('Wq', 'bq', 'Wk', 'bk', 'Wv', 'bv', 'Wo', 'bo')}
    del _L0_xattn_all

    def _L0_ffn_setup():
        import jax, jax.numpy as jnp
        import numpy as np
        H, I, E, NS, C = (256, 256, 6, 2, 2)
        TOPK = 2
        TEMP = 1.0
        EPS = 1e-06
        key = jax.random.key(seed)
        ks = jax.random.split(key, 20)
        sd = 0.02
        inp = {'x': jax.random.normal(ks[0], (4, 512, H), jnp.float32), 'router_W': jax.random.normal(ks[1], (C, H, E), jnp.float32) * sd, 'router_b': jax.random.normal(ks[2], (C, E), jnp.float32) * sd, 'gate_bias': jax.random.normal(ks[3], (C, E), jnp.float32) * sd, 'exp_Wup': jax.random.normal(ks[4], (E, H, I), jnp.float32) * sd, 'exp_bup': jnp.zeros((E, I), jnp.float32), 'exp_Wg': jax.random.normal(ks[5], (E, I, I), jnp.float32) * sd, 'exp_bg': jnp.zeros((E, I), jnp.float32), 'exp_Wdown': jax.random.normal(ks[6], (E, I, H), jnp.float32) * sd, 'exp_bdown': jnp.zeros((E, H), jnp.float32), 'share_Wup': jax.random.normal(ks[7], (H, NS * I), jnp.float32) * sd, 'share_bup': jnp.zeros((NS * I,), jnp.float32), 'share_Wg': jax.random.normal(ks[8], (I, I), jnp.float32) * sd, 'share_bg': jnp.zeros((I,), jnp.float32), 'share_Wdown': jax.random.normal(ks[9], (I, H), jnp.float32) * sd, 'share_bdown': jnp.zeros((H,), jnp.float32), 'norm_w': jnp.ones((C, H), jnp.float32)}
        return inp
    _L0_ffn_all = _L0_ffn_setup()
    _L0_ffn_in = {k: v for k, v in _L0_ffn_all.items() if k in ('router_W', 'router_b', 'gate_bias', 'exp_Wup', 'exp_bup', 'exp_Wg', 'exp_bg', 'exp_Wdown', 'exp_bdown', 'share_Wup', 'share_bup', 'share_Wg', 'share_bg', 'share_Wdown', 'share_bdown', 'norm_w')}
    del _L0_ffn_all
    return {'x': x, 'ctx_768': ctx_768, 'g_xattn': g_xattn, 'g_ffn': g_ffn, 'L0_xattn_Wq': _L0_xattn_in['Wq'], 'L0_xattn_bq': _L0_xattn_in['bq'], 'L0_xattn_Wk': _L0_xattn_in['Wk'], 'L0_xattn_bk': _L0_xattn_in['bk'], 'L0_xattn_Wv': _L0_xattn_in['Wv'], 'L0_xattn_bv': _L0_xattn_in['bv'], 'L0_xattn_Wo': _L0_xattn_in['Wo'], 'L0_xattn_bo': _L0_xattn_in['bo'], 'L0_ffn_router_W': _L0_ffn_in['router_W'], 'L0_ffn_router_b': _L0_ffn_in['router_b'], 'L0_ffn_gate_bias': _L0_ffn_in['gate_bias'], 'L0_ffn_exp_Wup': _L0_ffn_in['exp_Wup'], 'L0_ffn_exp_bup': _L0_ffn_in['exp_bup'], 'L0_ffn_exp_Wg': _L0_ffn_in['exp_Wg'], 'L0_ffn_exp_bg': _L0_ffn_in['exp_bg'], 'L0_ffn_exp_Wdown': _L0_ffn_in['exp_Wdown'], 'L0_ffn_exp_bdown': _L0_ffn_in['exp_bdown'], 'L0_ffn_share_Wup': _L0_ffn_in['share_Wup'], 'L0_ffn_share_bup': _L0_ffn_in['share_bup'], 'L0_ffn_share_Wg': _L0_ffn_in['share_Wg'], 'L0_ffn_share_bg': _L0_ffn_in['share_bg'], 'L0_ffn_share_Wdown': _L0_ffn_in['share_Wdown'], 'L0_ffn_share_bdown': _L0_ffn_in['share_bdown'], 'L0_ffn_norm_w': _L0_ffn_in['norm_w']}

def reference(x, ctx_768, g_xattn, g_ffn, L0_xattn_Wq, L0_xattn_bq, L0_xattn_Wk, L0_xattn_bk, L0_xattn_Wv, L0_xattn_bv, L0_xattn_Wo, L0_xattn_bo, L0_ffn_router_W, L0_ffn_router_b, L0_ffn_gate_bias, L0_ffn_exp_Wup, L0_ffn_exp_bup, L0_ffn_exp_Wg, L0_ffn_exp_bg, L0_ffn_exp_Wdown, L0_ffn_exp_bdown, L0_ffn_share_Wup, L0_ffn_share_bup, L0_ffn_share_Wg, L0_ffn_share_bg, L0_ffn_share_Wdown, L0_ffn_share_bdown, L0_ffn_norm_w):
    import jax
    import jax.numpy as jnp

    def _L0_xattn_ref(x, y, Wq, bq, Wk, bk, Wv, bv, Wo, bo):
        import jax, jax.numpy as jnp
        import numpy as np
        N_HEADS = 8
        D_EMBED = 256
        D_CROSS = 192
        D_HEAD = D_EMBED // N_HEADS
        q = jnp.einsum('bqd,de->bqe', x, Wq) + bq
        k = jnp.einsum('bkc,ce->bke', y, Wk) + bk
        v = jnp.einsum('bkc,ce->bke', y, Wv) + bv
        scale = 1.0 / np.sqrt(D_HEAD)
        scores = jnp.einsum('bqe,bke->bqk', q, k) * scale
        attn = jax.nn.softmax(scores, axis=-1)
        out = jnp.einsum('bqk,bke->bqe', attn, v)
        return jnp.einsum('bqe,ef->bqf', out, Wo) + bo

    def _L0_ffn_ref(x, router_W, router_b, gate_bias, exp_Wup, exp_bup, exp_Wg, exp_bg, exp_Wdown, exp_bdown, share_Wup, share_bup, share_Wg, share_bg, share_Wdown, share_bdown, norm_w):
        import jax, jax.numpy as jnp
        import numpy as np
        H, I, E, NS, C = (256, 256, 6, 2, 2)
        TOPK = 2
        TEMP = 1.0
        EPS = 1e-06
        B, S, Hd = x.shape
        xf = x.reshape(-1, Hd)
        for j in range(C):
            residual = xf
            gate = (xf @ router_W[j] + router_b[j]) / TEMP
            biased = gate + gate_bias[j]
            _, ids = jax.lax.top_k(biased, TOPK)
            sel = (ids[:, :, None] == jnp.arange(E)[None, None, :]).any(axis=1)
            weights = jax.nn.softmax(jnp.where(sel, gate, -jnp.inf), axis=-1)
            h = jnp.einsum('nh,ehi->eni', xf, exp_Wup) + exp_bup[:, None, :]
            h = jax.nn.silu(jnp.einsum('eni,eij->enj', h, exp_Wg) + exp_bg[:, None, :]) * h
            eo = jnp.einsum('eni,eih->enh', h, exp_Wdown) + exp_bdown[:, None, :]
            combined = jnp.einsum('ne,enh->nh', weights, eo)
            s = (xf @ share_Wup + share_bup).reshape(-1, NS, I)
            s = jax.nn.silu(s @ share_Wg + share_bg) * s
            share_out = (s @ share_Wdown + share_bdown).sum(axis=1)
            z = combined + share_out
            y = residual + z
            y = y * jax.lax.rsqrt(jnp.mean(y * y, axis=-1, keepdims=True) + EPS) * norm_w[j]
            xf = y
        return xf.reshape(B, S, Hd)
    x = x + jnp.tanh(g_xattn[0]) * _L0_xattn_ref(_layernorm(x, axis=-1), ctx_768, L0_xattn_Wq, L0_xattn_bq, L0_xattn_Wk, L0_xattn_bk, L0_xattn_Wv, L0_xattn_bv, L0_xattn_Wo, L0_xattn_bo)
    x = x + jnp.tanh(g_ffn[0]) * _L0_ffn_ref(_layernorm(x, axis=-1), L0_ffn_router_W, L0_ffn_router_b, L0_ffn_gate_bias, L0_ffn_exp_Wup, L0_ffn_exp_bup, L0_ffn_exp_Wg, L0_ffn_exp_bg, L0_ffn_exp_Wdown, L0_ffn_exp_bdown, L0_ffn_share_Wup, L0_ffn_share_bup, L0_ffn_share_Wg, L0_ffn_share_bg, L0_ffn_share_Wdown, L0_ffn_share_bdown, L0_ffn_norm_w)
    return x

_drawn_inputs = setup_inputs


def setup_inputs(seed=0):
    import zlib

    import numpy as np

    out = dict(_drawn_inputs(seed))
    spreads = {'L0_xattn_bq': (0.0, 0.1),
     'L0_xattn_bk': (0.0, 0.8),
     'L0_xattn_bv': (0.0, 0.1),
     'L0_xattn_bo': (0.0, 0.1),
     'L0_ffn_exp_bup': (0.0, 0.8),
     'L0_ffn_exp_bg': (0.0, 0.618),
     'L0_ffn_exp_bdown': (0.0, 0.1),
     'L0_ffn_share_bup': (0.0, 0.521),
     'L0_ffn_share_bg': (0.0, 0.298),
     'L0_ffn_share_bdown': (0.0, 0.1),
     'L0_ffn_norm_w': (1.0, 0.2)}
    factors = {'L0_ffn_exp_Wup': 3.448, 'L0_ffn_exp_Wg': 4.693, 'L0_ffn_exp_Wdown': 3.391}
    for name, (base, spread) in spreads.items():
        noise = np.random.default_rng([zlib.crc32(name.encode()), seed]).standard_normal(out[name].shape)
        drawn = base * np.exp(spread * noise) if base else spread * noise
        out[name] = jnp.asarray(drawn.astype(out[name].dtype))
    for name, factor in factors.items():
        out[name] = (out[name] * factor).astype(out[name].dtype)
    return out
```

```python
from contextlib import ExitStack

import numpy as np

import concourse.bass as bass
from concourse import mybir

F32 = mybir.dt.float32
F32R = mybir.dt.float32r
ALU = mybir.AluOpType
ACT = mybir.ActivationFunctionType
AX = mybir.AxisListType

P = 128
D = 256
C = D // P
NTOK = 2048
TILES = NTOK // P
GROUP = 512
NG = NTOK // GROUP
TG = GROUP // P
DC = 192
HC = DC // 2
KEYS = 1601
KPAD = KEYS + 1
KB = (KEYS + P - 1) // P
KROWS = [min(P, KEYS - b * P) for b in range(KB)]
SB = [(0, 512), (512, 1024), (1024, 1536), (1536, KPAD)]
TGRP = [range(0, 4), range(4, 8), range(8, 12), range(12, 13)]
NE = 6
ROUNDS = 2
UNITS = 2 + NE
GROUPS = ROUNDS * NG
SCALE = 1.0 / float(np.sqrt(D // 8))
LN_EPS = 1e-5
RMS_EPS = 1e-6
NW = 22

BQ, BK, BV, BU = 0, 2, 4, 6
BG = BU + 2 * UNITS
BDN = BG + 2 * UNITS
NWC = BDN + 2
NCOL = NWC + 2 * GROUPS
R_BO, R_RB = 0, D
R_GB = R_RB + NE * GROUPS
R_G = R_GB + NE * GROUPS
NROW = R_G + 2

W_HI, W_LO, W_HI2 = 0, 32, 64
R_HI = 96


def up_index(k):
    return k if k < 2 else 4 + 3 * (k - 2)


def gate_index(k):
    return 2 if k < 2 else 5 + 3 * (k - 2)


def down_index(k):
    return 3 if k < 2 else 6 + 3 * (k - 2)


def wait(eng, sem, value):
    if isinstance(value, int) and value <= 0:
        return
    eng.wait_ge(sem, value)


def build(nc, x, ctxT, w_att, w_ffn, cols, rows, w_router, b_down, out):
    with ExitStack() as ctx:
        base = nc.sbuf_base
        place = [(base + 31) // 32 * 32]

        def at(name, shape, dt, offset):
            return nc.alloc_sbuf_tensor_at(name, shape, dt, offset=offset)

        def sb(name, shape, dt=F32):
            size = 4 * int(np.prod(shape[1:]))
            t = at(name, shape, dt, place[0])
            place[0] += (size + 31) // 32 * 32
            return t

        sems = {}

        def sem(name):
            sems[name] = ctx.enter_context(nc.semaphore(name))
            return sems[name]

        colp = sb("colp", [P, NCOL])
        rowp = sb("rowp", [P, NROW])
        ident = sb("ident", [P, P])
        pick = sb("pick", [P, NE + 1, P], F32R)
        ones2 = sb("ones2", [P, 2], F32R)
        tanh_g = sb("tanh_g", [P, 2])
        bdn2 = sb("bdn2", [P, 2])
        bd = sb("bd", [P, D], F32R)
        wr_hi = sb("wr_hi", [P, GROUPS, C, NE], F32R)
        wr_lo = sb("wr_lo", [P, GROUPS, C, NE], F32R)
        half = sb("half", [P, 1])
        tri = sb("tri", [P, NE, NE])
        wp = sb("wp", [P, TG, P])
        x2 = sb("x2", [P, TILES, D])
        state = sb("state", [P, C, NTOK])
        rsum = sb("rsum", [P, TILES])
        rinv = sb("rinv", [P, TILES])
        bmax = sb("bmax", [P, 4])
        negm = sb("negm", [P, 1])
        bn6 = sb("bn6", [P, TILES, 6])
        mv = sb("mv", [P, TILES, 2])
        var = sb("var", [P, TILES])
        rstd = sb("rstd", [P, TILES])
        rt_g = sb("rt_g", [P, TG, NE])
        rt_b = sb("rt_b", [P, TG, NE])
        rt_gt = sb("rt_gt", [P, TG, NE, NE])
        rt_eq = sb("rt_eq", [P, TG, NE, NE])
        rt_c = sb("rt_c", [P, TG, NE])
        rt_s = sb("rt_s", [P, TG])
        rt_w = sb("rt_w", [P, TG, NE])
        rt_h = sb("rt_h", [P, TG, NE], F32R)

        region_a = place[0]
        k_hi = sb("k_hi", [P, C, KPAD], F32R)
        k_lo = sb("k_lo", [P, C, KPAD], F32R)
        v_hi = sb("v_hi", [P, KB, D], F32R)
        v_lo = sb("v_lo", [P, KB, D], F32R)
        stage = sb("stage", [P, 2 * D])
        region_b = place[0]
        prob = sb("prob", [P, KEYS + 7])
        pT_hi = sb("pT_hi", [P, KB * P], F32R)
        pT_lo = sb("pT_lo", [P, KB * P], F32R)
        q_hi = sb("q_hi", [P, C, P], F32R)
        q_lo = sb("q_lo", [P, C, P], F32R)
        o_row = sb("o_row", [P, D])
        end_a = place[0]
        place[0] = region_b
        ln_xn = sb("ln_xn", [P, TG, D])
        ln_hi = sb("ln_hi", [P, C, GROUP], F32R)
        ln_lo = sb("ln_lo", [P, C, GROUP], F32R)
        vo = sb("vo", [P, 2, D])
        wr_raw = sb("wr_raw", [P, GROUPS * C * NE])
        bd_raw = sb("bd_raw", [P, D])
        bd_hi = sb("bd_hi", [P, D], F32R)
        assert place[0] <= end_a
        place[0] = region_c = end_a
        w_hi = sb("w_hi", [P, NW, 2 * D], F32R)
        w_lo = sb("w_lo", [P, NW, 2 * D], F32R)
        end_c = place[0]
        assert end_c <= nc.sbuf_usable_end, (end_c, nc.sbuf_usable_end)
        place[0] = region_c
        y_raw = sb("y_raw", [HC, C, KPAD])
        y_hi = sb("y_hi", [HC, C, KPAD], F32R)
        y_lo = sb("y_lo", [HC, C, KPAD], F32R)
        vT_hi = sb("vT_hi", [P, C, KPAD], F32R)
        vT_lo = sb("vT_lo", [P, C, KPAD], F32R)
        wa_raw = sb("wa_raw", [P, 4, 2 * D])
        wa_hi = sb("wa_hi", [P, 4, 2 * D], F32R)
        wa_lo = sb("wa_lo", [P, 4, 2 * D], F32R)
        assert place[0] <= end_c, (place[0], end_c)
        place[0] = region_a
        xs_hi = sb("xs_hi", [P, C, GROUP], F32R)
        xs_lo = sb("xs_lo", [P, C, GROUP], F32R)
        h32 = sb("h32", [P, 2, C, GROUP])
        h_hi = sb("h_hi", [P, 2, C, GROUP], F32R)
        h_lo = sb("h_lo", [P, 2, C, GROUP], F32R)
        sg = sb("sg", [P, C, GROUP])
        aa = sb("aa", [P, C, GROUP])
        as0 = sb("as0", [P, C, GROUP])
        a_hi = sb("a_hi", [P, 2, C, GROUP], F32R)
        a_lo = sb("a_lo", [P, 2, C, GROUP], F32R)
        msum = sb("msum", [P, TG])
        root = sb("root", [P, TG])
        root_h = sb("root_h", [P, TG], F32R)
        rT = sb("rT", [P, GROUP], F32R)
        wT = sb("wT", [P, GROUP], F32R)
        sq = sb("sq", [P, GROUP])
        sq_hi = sb("sq_hi", [P, GROUP], F32R)
        sq_lo = sb("sq_lo", [P, GROUP], F32R)
        assert place[0] <= end_a, (place[0], end_a)
        ps = ctx.enter_context(nc.psum_tensor("ps", [P, 8, 512], F32))

        ld_cols, ld_rows, ld_wa, ld_small = sem("ld_cols"), sem("ld_rows"), sem("ld_wa"), sem("ld_small")
        ld_y = [sem(f"ld_y{b}") for b in range(4)]
        ld_x = [sem(f"ld_x{g}") for g in range(NG)]
        ld_w, out_done = sem("ld_w"), sem("out_done")
        zeroed, const, tg_done, ones_done = sem("zeroed"), sem("const"), sem("tg_done"), sem("ones_done")
        wa_split_hi, wa_split_lo = sem("wa_split_hi"), sem("wa_split_lo")
        y_split_hi, y_split_lo = sem("y_split_hi"), sem("y_split_lo")
        kv_mm, kv_act, kv_dve = sem("kv_mm"), sem("kv_act"), sem("kv_dve")
        ln_st, ln_ag, ln_var, ln_rs, ln_done = sem("ln_st"), sem("ln_ag"), sem("ln_var"), sem("ln_rs"), sem("ln_done")
        lnT_mm, lnT_act, lnT_dve = sem("lnT_mm"), sem("lnT_act"), sem("lnT_dve")
        q_mm, q_act = sem("q_mm"), sem("q_act")
        vo_mm, vo_add, vo_hi, vo_lo = sem("vo_mm"), sem("vo_add"), sem("vo_hi"), sem("vo_lo")
        w_done, wh_done = sem("w_done"), sem("wh_done")
        qs_hi, qs_lo = sem("qs_hi"), sem("qs_lo")
        s_mm, s_max, s_neg, s_max4, s_exp = sem("s_mm"), sem("s_max"), sem("s_neg"), sem("s_max4"), sem("s_exp")
        t_mm, t_act, t_dve = sem("t_mm"), sem("t_act"), sem("t_dve")
        o_mm, o_inv, o_sc, o_x2, o_keep, o_bn, o_ag, o_var, o_rs, o_n = (sem(n) for n in (
            "o_mm", "o_inv", "o_sc", "o_x2", "o_keep", "o_bn", "o_ag", "o_var", "o_rs", "o_n"))
        n_mm, n_act = sem("n_mm"), sem("n_act")
        xs_act, xs_pool = sem("xs_act"), sem("xs_pool")
        u_mm, u_act, u_dve = sem("u_mm"), sem("u_act"), sem("u_dve")
        g_mm, g_act = sem("g_mm"), sem("g_act")
        a_mul, a_fin, a_split_hi, a_split_lo = sem("a_mul"), sem("a_fin"), sem("a_split_hi"), sem("a_split_lo")
        b_mm, d_mm = sem("b_mm"), sem("d_mm")
        r_mm, r_dve, r_tanh, r_chain, r_ready, wT_mm, wT_act = (sem(n) for n in (
            "r_mm", "r_dve", "r_tanh", "r_chain", "r_ready", "wT_mm", "wT_act"))
        y_dve, sq_act, sqh_act, sq_pool, ss_mm, ms_dve, ms_pool, y_norm, ms_sum, rh_dve, rr_dve, rT_mm, rT_act, rb_mm = (sem(n) for n in (
            "y_dve", "sq_act", "sqh_act", "sq_pool", "ss_mm", "ms_dve", "ms_pool", "y_norm", "ms_sum", "rh_dve", "rr_dve", "rT_mm",
            "rT_act", "rb_mm"))
        f_mm, f_dve = sem("f_mm"), sem("f_dve")

        def f(ap):
            return ap.bitcast(F32)

        SCORE = [0, 1, 2, 3]
        TBANK = [4, 5]
        OBANK, XBANK = 6, 7
        HB, GB, YB, BB, RB = [0, 1], [2, 3], [4, 5], 6, 7

        kv_jobs = [(e, b) for e in range(C) for b in range(4)]
        KV = 2 * len(kv_jobs)

        users = [[] for _ in range(8)]
        order = {}
        n = 0
        for j in range(KV):
            order["kv", j] = n; users[n % 8].append((n, kv_dve, j + 1)); n += 1
        for g in range(NG):
            for c in range(C):
                order["T", g, c] = n; users[n % 8].append((n, lnT_dve, 2 * g + c + 1)); n += 1
            for e in range(C):
                order["Q", g, e] = n; users[n % 8].append((n, q_act, 2 * g + e + 1)); n += 1
        for b in range(KB):
            order["V", b] = n; users[n % 8].append((n, vo_add, b + 1)); n += 1

        def bank_of(*job):
            return order[job] % 8

        def bank_free(eng, *job):
            before = [u for u in users[order[job] % 8] if u[0] < order[job]]
            if before:
                eng.wait_ge(before[-1][1], before[-1][2])

        block = ctx.enter_context(nc.Block())

        @block.sync
        def _(sp):
            sp.dma_start(wa_raw[:], w_att).then_inc(ld_wa, 16)
            for b, (lo, hi) in enumerate(SB):
                hi = min(hi, KEYS)
                sp.dma_start(y_raw[:, :, lo:hi], ctxT[:, :, lo:hi]).then_inc(ld_y[b], 16)
            sp.dma_start(colp[:], cols).then_inc(ld_cols, 16)
            xt = x.rearrange("(t p) d -> p t d", p=P)
            for g in range(NG):
                sp.dma_start(x2[:, TG * g:TG * g + TG, :], xt[:, TG * g:TG * g + TG, :]).then_inc(ld_x[g], 16)
            sp.dma_start(rowp[:], rows.broadcast_to([P, NROW])).then_inc(ld_rows, 16)
            sp.dma_start(wr_raw[:], w_router).then_inc(ld_small, 16)
            sp.wait_ge(zeroed, 1)
            for p0 in (W_HI, W_LO, W_HI2):
                sp.dma_start(bd_raw[p0:p0 + NE, :], b_down).then_inc(ld_small, 16)
            sp.dma_start(stage[:], w_ffn[:, 0, :]).then_inc(ld_w, 16)
            with sp.Fori(1, NW) as m:
                sp.wait_ge(w_done, m)
                sp.dma_start(stage[:], w_ffn[:, bass.ds(m, 1), :].rearrange("p a n -> p (a n)")).then_inc(ld_w, 16)
            ot = out.rearrange("(t p) d -> p t d", p=P)
            for g in range(NG):
                sp.wait_ge(f_dve, TG * (g + 1))
                sp.dma_start(ot[:, TG * g:TG * g + TG, :], x2[:, TG * g:TG * g + TG, :]).then_inc(out_done, 16)
            sp.wait_ge(out_done, 16 * NG)

        @block.gpsimd
        def _(pool):
            nc.gpsimd.memset(bd_raw[:], 0.0).then_inc(zeroed, 1)
            nc.gpsimd.memset(y_raw[:, :, KEYS:KPAD], 0.0).then_inc(zeroed, 1)
            nc.gpsimd.memset(ident[:], 0.0).then_inc(zeroed, 1)
            nc.gpsimd.memset(tri[:], 0.0).then_inc(zeroed, 1)
            nc.gpsimd.memset(wp[:], 0.0).then_inc(zeroed, 1)
            nc.gpsimd.memset(half[:], -0.5).then_inc(const, 1)
            pool.wait_ge(zeroed, 5)
            nc.gpsimd.affine_select(out=ident[:], in_=ident[:], compare_op=ALU.not_equal, fill=1.0,
                                    base=0, pattern=[[-1, P]], channel_multiplier=1).then_inc(const, 1)
            nc.gpsimd.affine_select(out=tri[:], in_=tri[:], compare_op=ALU.is_ge, fill=1.0,
                                    base=0, pattern=[[-1, NE], [1, NE]], channel_multiplier=0).then_inc(const, 1)
            pool.wait_ge(ld_wa, 16)
            for m in (2, 3):
                nc.gpsimd.tensor_copy(wa_hi[:, m, :], wa_raw[:, m, :]).then_inc(wh_done, 1)
                pool.wait_ge(wh_done, m - 1)
                nc.gpsimd.tensor_tensor(wa_lo[:, m, :], wa_raw[:, m, :], f(wa_hi[:, m, :]), ALU.subtract).then_inc(wa_split_lo, 1)
            pool.wait_ge(const, 1)
            for g in range(NG):
                pool.wait_ge(ln_var, g + 1)
                t = slice(TG * g, TG * g + TG)
                nc.gpsimd.tensor_tensor(rstd[:, t], var[:, t], half[:].broadcast_to([P, TG]), ALU.pow).then_inc(ln_rs, 1)
            pool.wait_ge(ld_small, 64)
            wr = "p u c e -> p (u c e)"
            nc.gpsimd.tensor_copy(wr_hi[:].rearrange(wr), wr_raw[:]).then_inc(wh_done, 1)
            nc.gpsimd.tensor_copy(bd_hi[:], bd_raw[:]).then_inc(wh_done, 1)
            pool.wait_ge(wh_done, 4)
            nc.gpsimd.tensor_tensor(wr_lo[:].rearrange(wr), wr_raw[:], f(wr_hi[:]).rearrange(wr), ALU.subtract).then_inc(const, 1)
            nc.gpsimd.tensor_copy(bd[0:W_HI2, :], f(bd_hi[0:W_HI2, :])).then_inc(const, 1)
            pool.wait_ge(const, 5)
            nc.gpsimd.tensor_tensor(bd[W_HI2:P, :], bd_raw[W_HI2:P, :], f(bd_hi[W_HI2:P, :]), ALU.subtract).then_inc(const, 1)
            pool.wait_ge(const, 6)
            pool.wait_ge(vo_mm, KB)

            def attention_rstd(t):
                pool.wait_ge(o_var, t + 1)
                nc.gpsimd.tensor_tensor(rstd[:, bass.ds(t, 1)], var[:, bass.ds(t, 1)], half[:], ALU.pow).then_inc(o_rs, 1)

            def split_weight(m):
                pool.wait_ge(ld_w, 16 * (m + 1))
                nc.gpsimd.tensor_copy(w_hi[:, bass.ds(m, 1), :].rearrange("p a n -> p (a n)"), stage[:]).then_inc(wh_done, 1)
                pool.wait_ge(wh_done, m + 5)
                nc.gpsimd.tensor_tensor(w_lo[:, bass.ds(m, 1), :].rearrange("p a n -> p (a n)"), stage[:],
                                        f(w_hi[:, bass.ds(m, 1), :]).rearrange("p a n -> p (a n)"),
                                        ALU.subtract).then_inc(w_done, 1)

            for m in range(NW - TILES):
                split_weight(m)
            with pool.Fori(0, TILES) as t:
                split_weight(t + (NW - TILES))
                attention_rstd(t)

            def split_input(u):
                lo = (u % NG) * GROUP
                pool.wait_ge(xs_act, u + 1)
                nc.gpsimd.tensor_tensor(xs_lo[:], state[:, :, bass.ds(lo, GROUP)], f(xs_hi[:]),
                                        ALU.subtract).then_inc(xs_pool, 1)

            def norm(u):
                for c in range(C):
                    pool.wait_ge(sqh_act, C * u + c + 1)
                    nc.gpsimd.tensor_tensor(sq_lo[:], sq[:], f(sq_hi[:]), ALU.subtract).then_inc(sq_pool, 1)
                pool.wait_ge(ms_dve, u + 1)
                nc.gpsimd.tensor_tensor(root[:], msum[:], half[:].broadcast_to([P, TG]), ALU.pow).then_inc(ms_pool, 1)

            split_input(0)
            split_input(1)
            with pool.Fori(1, GROUPS - 1) as u:
                norm(u - 1)
                split_input(u + 1)
            norm(GROUPS - 2)
            norm(GROUPS - 1)

        @block.scalar
        def _(act):
            act.wait_ge(ld_wa, 16)
            for m in (0, 1):
                nc.scalar.copy(wa_hi[0:HC, m, :], wa_raw[0:HC, m, :]).then_inc(wa_split_hi, 1)
            act.wait_ge(zeroed, 2)
            for b, (lo, hi) in enumerate(SB):
                act.wait_ge(ld_y[b], 16)
                nc.scalar.copy(y_hi[:, :, lo:hi], y_raw[:, :, lo:hi]).then_inc(y_split_hi, 1)
            act.wait_ge(ld_rows, 16)
            nc.scalar.activation(tanh_g[:], rowp[:, R_G:R_G + 2], ACT.Tanh).then_inc(tg_done, 1)
            act.wait_ge(ld_cols, 16)
            nc.scalar.activation(bdn2[:], colp[:, BDN:BDN + 2], ACT.Copy, scale=2.0).then_inc(tg_done, 1)
            for which, dst, bias in ((0, k_hi, BK), (1, vT_hi, BV)):
                for j, (e, b) in enumerate(kv_jobs):
                    j += which * len(kv_jobs)
                    lo, hi = SB[b]
                    act.wait_ge(kv_mm, j + 1)
                    nc.scalar.activation(dst[:, e, lo:hi], ps[:, bank_of("kv", j), 0:hi - lo], ACT.Identity,
                                         bias=colp[:, bias + e:bias + e + 1]).then_inc(kv_act, 1)
            for g in range(NG):
                for c in range(C):
                    act.wait_ge(lnT_mm, C * g + c + 1)
                    nc.scalar.copy(ln_hi[:, c, :], ps[:, bank_of("T", g, c), :]).then_inc(lnT_act, 1)
                for e in range(C):
                    act.wait_ge(q_mm, C * g + e + 1)
                    nc.scalar.activation(state[:, e, GROUP * g:GROUP * g + GROUP], ps[:, bank_of("Q", g, e), :],
                                         ACT.Identity, bias=colp[:, BQ + e:BQ + e + 1]).then_inc(q_act, 1)

            def exponent(t):
                act.wait_ge(s_neg, t + 1)
                wait(act, t_mm, 4 * t)
                nc.scalar.activation(prob[:, 0:KEYS], ps[:, 0:4, :].rearrange("p b n -> p (b n)")[:, 0:KEYS], ACT.Exp,
                                     bias=negm[:, 0:1], scale=SCALE,
                                     accum_out=rsum[:, bass.ds(t, 1)]).then_inc(s_exp, 1)

            def high_halves(t):
                for i, grp in enumerate(TGRP):
                    act.wait_ge(t_mm, 4 * t + i + 1)
                    n, k0 = len(grp) * P, grp[0] * P
                    rows = KROWS[grp[0]]
                    nc.scalar.copy(pT_hi[0:rows, k0:k0 + n], ps[0:rows, TBANK[i % 2], 0:n]).then_inc(t_act, 1)

            def to_state(t):
                act.wait_ge(n_mm, t + 1)
                nc.scalar.copy(state[:, :, bass.ds(t * P, P)],
                               ps[:, XBANK, 0:D].rearrange("p (c n) -> p c n", c=C)).then_inc(n_act, 1)

            act.wait_ge(vo_mm, KB)
            act.wait_ge(vo_lo, KB)
            act.wait_ge(const, 6)
            exponent(0)
            high_halves(0)
            exponent(1)
            with act.Fori(1, TILES - 1) as t:
                high_halves(t)
                to_state(t - 1)
                exponent(t + 1)
            high_halves(TILES - 1)
            to_state(TILES - 2)
            to_state(TILES - 1)

            def input_high(u):
                wait(act, u_mm, 2 * UNITS * u)
                wait(act, d_mm, (UNITS - 1) * (u - 1))
                nc.scalar.copy(xs_hi[:], state[:, :, bass.ds((u % NG) * GROUP, GROUP)]).then_inc(xs_act, 1)

            def after_up(u, k):
                for c in range(C):
                    n = 2 * UNITS * u + 2 * k + c
                    act.wait_ge(u_mm, n + 1)
                    wait(act, a_mul, n + 1 - 4)
                    wait(act, g_mm, 2 * UNITS * u + 2 * (k - 2) + 2)
                    bias = colp[:, BU + 2 * k + c:BU + 2 * k + c + 1]
                    nc.scalar.activation(h32[:, k % 2, c, :], ps[:, HB[c], :], ACT.Identity, bias=bias).then_inc(u_act, 1)
                    nc.scalar.activation(h_hi[:, k % 2, c, :], ps[:, HB[c], :], ACT.Identity, bias=bias).then_inc(u_act, 1)

            def after_gate(u, k):
                for c in range(C):
                    n = 2 * UNITS * u + 2 * k + c
                    act.wait_ge(g_mm, n + 1)
                    wait(act, a_mul, n + 1 - 2)
                    nc.scalar.activation(sg[:, c, :], ps[:, GB[c], :], ACT.Silu,
                                         bias=colp[:, BG + 2 * k + c:BG + 2 * k + c + 1]).then_inc(g_act, 1)

            def square(u, c):
                act.wait_ge(y_dve, C * u + c + 1)
                if c:
                    act.wait_ge(ss_mm, C * u + c)
                nc.scalar.activation(sq[:], state[:, c, bass.ds((u % NG) * GROUP, GROUP)], ACT.Square).then_inc(sq_act, 1)
                act.wait_ge(sq_act, C * u + c + 1)
                nc.scalar.copy(sq_hi[:], sq[:]).then_inc(sqh_act, 1)

            def root_transposed(u):
                act.wait_ge(rT_mm, u + 1)
                nc.scalar.copy(rT[:], ps[:, RB, :]).then_inc(rT_act, 1)

            def group(u, first=False, last=False):
                for k in range(UNITS):
                    if k < UNITS - 1:
                        after_up(u, k + 1)
                    elif not last:
                        after_up(u + 1, 0)
                    after_gate(u, k)
                    if k == 0:
                        act.wait_ge(r_tanh, 2 * u + 1)
                        nc.scalar.activation(rt_w[:], rt_w[:], ACT.Tanh, scale=0.5).then_inc(r_tanh, 1)
                    if k == 1:
                        act.wait_ge(wT_mm, u + 1)
                        wait(act, d_mm, 7 * u)
                        nc.scalar.copy(wT[:], ps[:, RB, :]).then_inc(wT_act, 1)
                    if k in (1, 2) and not first:
                        square(u - 1, k - 1)
                    if k == 6 and not first:
                        root_transposed(u - 1)
                    if k == UNITS - 2 and not last:
                        input_high(u + 1)

            act.wait_ge(o_mm, TILES)
            act.wait_ge(n_mm, TILES)
            act.wait_ge(w_done, NW)
            input_high(0)
            after_up(0, 0)
            group(0, first=True)
            with act.Fori(1, GROUPS - 1) as u:
                group(u)
            group(GROUPS - 1, last=True)
            for c in range(C):
                square(GROUPS - 1, c)
            root_transposed(GROUPS - 1)

        @block.vector
        def _(dve):
            dve.wait_ge(const, 3)
            dve.wait_ge(zeroed, 5)
            nc.vector.tensor_scalar(ones2[:], wp[:, 0, 0:2], 1.0, None, ALU.add).then_inc(ones_done, 1)
            nc.vector.tensor_scalar(pick[:, NE, :], wp[:, 0, :], ident[:, R_HI:R_HI + 1], ident[:, R_HI + 1:R_HI + 2],
                                    ALU.add, ALU.add).then_inc(ones_done, 1)
            for e in range(NE):
                nc.vector.tensor_scalar(pick[:, e, :], wp[:, 0, :], ident[:, W_HI + e:W_HI + e + 1],
                                        ident[:, W_LO + e:W_LO + e + 1], ALU.add, ALU.add).then_inc(ones_done, 1)
            for m in (0, 1):
                dve.wait_ge(wa_split_hi, m + 1)
                nc.vector.tensor_tensor(wa_lo[0:HC, m, :], wa_raw[0:HC, m, :], f(wa_hi[0:HC, m, :]),
                                        ALU.subtract).then_inc(wa_split_lo, 1)
            for b, (lo, hi) in enumerate(SB):
                dve.wait_ge(y_split_hi, b + 1)
                nc.vector.tensor_tensor(y_lo[:, :, lo:hi], y_raw[:, :, lo:hi], f(y_hi[:, :, lo:hi]),
                                        ALU.subtract).then_inc(y_split_lo, 1)

            def stats(g):
                dve.wait_ge(ld_x[g], 16)
                for t in range(TG * g, TG * g + TG):
                    nc.vector.bn_stats(bn6[:, t, :], x2[:, t, :]).then_inc(ln_st, 1)
                dve.wait_ge(ln_st, TG * (g + 1))
                for t in range(TG * g, TG * g + TG):
                    nc.vector.bn_aggr(mv[:, t, :], bn6[:, t, :]).then_inc(ln_ag, 1)
                dve.wait_ge(ln_ag, TG * (g + 1))
                nc.vector.tensor_scalar(var[:, TG * g:TG * g + TG], mv[:, TG * g:TG * g + TG, 1], LN_EPS, None,
                                        ALU.add).then_inc(ln_var, 1)

            def kv_low(which, dst, src_hi, bias):
                for j, (e, b) in enumerate(kv_jobs):
                    j += which * len(kv_jobs)
                    lo, hi = SB[b]
                    dve.wait_ge(kv_act, j + 1)
                    nc.vector.scalar_tensor_tensor(out=dst[:, e, lo:hi], in0=ps[:, bank_of("kv", j), 0:hi - lo],
                                                   scalar=colp[:, bias + e:bias + e + 1], in1=f(src_hi[:, e, lo:hi]),
                                                   op0=ALU.add, op1=ALU.subtract).then_inc(kv_dve, 1)

            dve.wait_ge(ld_cols, 16)
            kv_low(0, k_lo, k_hi, BK)
            stats(0)
            kv_low(1, vT_lo, vT_hi, BV)
            stats(1)
            stats(2)
            stats(3)
            for g in range(NG):
                dve.wait_ge(ln_rs, g + 1)
                wait(dve, lnT_mm, C * g)
                for i in range(TG):
                    t = TG * g + i
                    nc.vector.tensor_scalar(ln_xn[:, i, :], x2[:, t, :], mv[:, t, 0:1], rstd[:, t:t + 1],
                                            ALU.subtract, ALU.mult).then_inc(ln_done, 1)
                for c in range(C):
                    dve.wait_ge(lnT_act, C * g + c + 1)
                    nc.vector.tensor_tensor(ln_lo[:, c, :], ps[:, bank_of("T", g, c), :], f(ln_hi[:, c, :]),
                                            ALU.subtract).then_inc(lnT_dve, 1)
            dve.wait_ge(ld_rows, 16)
            for b in range(KB):
                r = KROWS[b]
                dve.wait_ge(vo_mm, b + 1)
                wait(dve, vo_lo, b - 1)
                nc.vector.tensor_tensor(vo[0:r, b % 2, :], ps[0:r, bank_of("V", b), 0:D], rowp[0:r, R_BO:R_BO + D],
                                        ALU.add).then_inc(vo_add, 1)
                dve.wait_ge(vo_add, b + 1)
                nc.vector.tensor_copy(v_hi[0:r, b, :], vo[0:r, b % 2, :]).then_inc(vo_hi, 1)
                dve.wait_ge(vo_hi, b + 1)
                nc.vector.tensor_tensor(v_lo[0:r, b, :], vo[0:r, b % 2, :], f(v_hi[0:r, b, :]),
                                        ALU.subtract).then_inc(vo_lo, 1)

            def split_q(t):
                wait(dve, s_mm, 4 * t)
                nc.vector.tensor_copy(q_hi[:], state[:, :, bass.ds(t * P, P)]).then_inc(qs_hi, 1)
                dve.wait_ge(qs_hi, t + 1)
                nc.vector.tensor_tensor(q_lo[:], state[:, :, bass.ds(t * P, P)], f(q_hi[:]),
                                        ALU.subtract).then_inc(qs_lo, 1)

            def bank_max(t, b):
                lo, hi = SB[b]
                dve.wait_ge(s_mm, 4 * t + b + 1)
                nc.vector.tensor_reduce(bmax[:, b:b + 1], ps[:, SCORE[b], 0:min(hi, KEYS) - lo], AX.X,
                                        ALU.max).then_inc(s_max, 1)

            def neg_max(t):
                dve.wait_ge(s_max, 4 * t + 4)
                nc.vector.tensor_reduce(bmax[:, 0:1], bmax[:, 0:4], AX.X, ALU.max).then_inc(s_max4, 1)
                dve.wait_ge(s_max4, t + 1)
                nc.vector.tensor_scalar(negm[:], bmax[:, 0:1], -SCALE, None, ALU.mult).then_inc(s_neg, 1)

            def low_half(t, i):
                grp = TGRP[i]
                n, k0, rows = len(grp) * P, grp[0] * P, KROWS[grp[0]]
                dve.wait_ge(t_act, 4 * t + i + 1)
                nc.vector.tensor_tensor(pT_lo[0:rows, k0:k0 + n], ps[0:rows, TBANK[i % 2], 0:n],
                                        f(pT_hi[0:rows, k0:k0 + n]), ALU.subtract).then_inc(t_dve, 1)

            def residual(t):
                one = bass.ds(t, 1)
                dve.wait_ge(s_exp, t + 1)
                nc.vector.reciprocal(rinv[:, one], rsum[:, one]).then_inc(o_inv, 1)
                dve.wait_ge(o_inv, t + 1)
                nc.vector.tensor_tensor(rinv[:, one], rinv[:, one], tanh_g[:, 0:1], ALU.mult).then_inc(o_sc, 1)
                dve.wait_ge(o_sc, t + 1)
                dve.wait_ge(o_mm, t + 1)
                row = x2[:, one, :].rearrange("p a n -> p (a n)")
                nc.vector.scalar_tensor_tensor(out=o_row[:], in0=ps[:, OBANK, 0:D], scalar=rinv[:, one], in1=row,
                                               op0=ALU.mult, op1=ALU.add).then_inc(o_x2, 1)
                dve.wait_ge(o_x2, t + 1)
                nc.vector.bn_stats(bn6[:, 0, :], o_row[:]).then_inc(o_bn, 1)
                dve.wait_ge(o_bn, t + 1)
                nc.vector.tensor_scalar(row, o_row[:], 1.0, None, ALU.mult).then_inc(o_keep, 1)
                nc.vector.bn_aggr(mv[:, 0, :], bn6[:, 0, :]).then_inc(o_ag, 1)
                dve.wait_ge(o_ag, t + 1)
                nc.vector.tensor_scalar(var[:, one], mv[:, 0, 1:2], LN_EPS, None, ALU.add).then_inc(o_var, 1)

            def normed(t):
                one = bass.ds(t, 1)
                dve.wait_ge(o_rs, t + 1)
                nc.vector.tensor_scalar(o_row[:], o_row[:], mv[:, 0, 0:1],
                                        rstd[:, one], ALU.subtract, ALU.mult).then_inc(o_n, 1)

            dve.wait_ge(tg_done, 2)
            dve.wait_ge(q_act, C * NG)
            split_q(0)
            for b in range(4):
                bank_max(0, b)
            neg_max(0)
            split_q(1)

            def attention_tile(t, first=False, last=False):
                low_half(t, 0)
                if not first:
                    residual(t - 1)
                low_half(t, 1)
                if not last:
                    bank_max(t + 1, 0)
                low_half(t, 2)
                if not first:
                    normed(t - 1)
                low_half(t, 3)
                if not last:
                    for b in range(1, 4):
                        bank_max(t + 1, b)
                    neg_max(t + 1)

            attention_tile(0, first=True)
            split_q(2)
            with dve.Fori(1, TILES - 2) as t:
                attention_tile(t)
                split_q(t + 2)
            attention_tile(TILES - 2)
            attention_tile(TILES - 1, last=True)
            residual(TILES - 1)
            normed(TILES - 1)

            def h_low(u, k):
                for c in range(C):
                    n = 2 * UNITS * u + 2 * k + c
                    dve.wait_ge(u_act, 2 * n + 2)
                    nc.vector.tensor_tensor(h_lo[:, k % 2, c, :], h32[:, k % 2, c, :], f(h_hi[:, k % 2, c, :]),
                                            ALU.subtract).then_inc(u_dve, 1)

            def activated(u, k):
                for c in range(C):
                    n = 2 * UNITS * u + 2 * k + c
                    m = 2 * (UNITS - 1) * u + 2 * (k - 1) + c
                    dve.wait_ge(g_act, n + 1)
                    if k == 0:
                        nc.vector.tensor_tensor(as0[:, c, :], sg[:, c, :], h32[:, 0, c, :], ALU.mult).then_inc(a_mul, 1)
                        continue
                    nc.vector.tensor_tensor(aa[:, c, :], sg[:, c, :], h32[:, k % 2, c, :], ALU.mult).then_inc(a_mul, 1)
                    dve.wait_ge(a_mul, n + 1)
                    if k == 1:
                        nc.vector.tensor_tensor(aa[:, c, :], aa[:, c, :], as0[:, c, :], ALU.add).then_inc(a_fin, 1)
                    else:
                        dve.wait_ge(b_mm, NE * u + k - 1)
                        nc.vector.tensor_tensor(aa[:, c, :], ps[:, BB, :], aa[:, c, :], ALU.mult).then_inc(a_fin, 1)
                    dve.wait_ge(a_fin, m + 1)
                    wait(dve, d_mm, (UNITS - 1) * u + (k - 2 if k > 2 else 0))
                    nc.vector.tensor_copy(a_hi[:, k % 2, c, :], aa[:, c, :]).then_inc(a_split_hi, 1)
                    dve.wait_ge(a_split_hi, m + 1)
                    nc.vector.tensor_tensor(a_lo[:, k % 2, c, :], aa[:, c, :], f(a_hi[:, k % 2, c, :]),
                                            ALU.subtract).then_inc(a_split_lo, 1)

            CHAIN = 12

            def route_a(u):
                step = [0]

                def link(instruction):
                    step[0] += 1
                    instruction.then_inc(r_chain, 1)
                    dve.wait_ge(r_chain, CHAIN * u + step[0])

                def per_tile(row):
                    return rowp[:, bass.ds(row + u * NE, NE)].unsqueeze(1).broadcast_to([P, TG, NE])

                dve.wait_ge(r_mm, u + 1)
                link(nc.vector.tensor_tensor(rt_g[:], ps[:, RB, 0:TG * P].rearrange("p (t n) -> p t n", t=TG)[:, :, 0:NE],
                                             per_tile(R_RB), ALU.add))
                link(nc.vector.tensor_tensor(rt_b[:], rt_g[:], per_tile(R_GB), ALU.add))
                mine = rt_b[:].unsqueeze(3).broadcast_to([P, TG, NE, NE])
                other = rt_b[:].unsqueeze(2).broadcast_to([P, TG, NE, NE])
                nc.vector.tensor_tensor(rt_gt[:], other, mine, ALU.is_gt).then_inc(r_dve, 1)
                link(nc.vector.tensor_tensor(rt_eq[:], other, mine, ALU.is_equal))
                link(nc.vector.tensor_tensor(rt_eq[:], rt_eq[:], tri[:].unsqueeze(1).broadcast_to([P, TG, NE, NE]), ALU.mult))
                dve.wait_ge(r_dve, 2 * u + 1)
                link(nc.vector.tensor_tensor(rt_gt[:], rt_gt[:], rt_eq[:], ALU.add))
                link(nc.vector.tensor_reduce(rt_c[:], rt_gt[:], AX.X, ALU.add))
                link(nc.vector.tensor_scalar(rt_c[:], rt_c[:], 2.0, None, ALU.is_lt))
                link(nc.vector.tensor_tensor(rt_w[:], rt_g[:], rt_c[:], ALU.mult))
                link(nc.vector.tensor_reduce(rt_s[:], rt_w[:], AX.X, ALU.add))
                link(nc.vector.tensor_scalar(rt_w[:], rt_g[:], 2.0, None, ALU.mult))
                nc.vector.tensor_tensor(rt_w[:], rt_w[:], rt_s[:].unsqueeze(2).broadcast_to([P, TG, NE]),
                                        ALU.subtract).then_inc(r_tanh, 1)

            def route_b(u):
                dve.wait_ge(r_tanh, 2 * u + 2)
                nc.vector.tensor_scalar(rt_w[:], rt_w[:], 0.5, 0.5, ALU.mult, ALU.add).then_inc(r_chain, 1)
                dve.wait_ge(r_chain, CHAIN * u + CHAIN - 1)
                nc.vector.tensor_tensor(rt_w[:], rt_w[:], rt_c[:], ALU.mult).then_inc(r_chain, 1)
                dve.wait_ge(r_chain, CHAIN * u + CHAIN)
                nc.vector.tensor_copy(rt_h[:], rt_w[:]).then_inc(r_dve, 1)
                dve.wait_ge(r_dve, 2 * u + 2)
                nc.vector.tensor_copy(wp[:, :, W_HI:W_HI + NE], f(rt_h[:])).then_inc(r_ready, 1)
                nc.vector.tensor_copy(wp[:, :, W_HI2:W_HI2 + NE], f(rt_h[:])).then_inc(r_ready, 1)
                nc.vector.tensor_tensor(wp[:, :, W_LO:W_LO + NE], rt_w[:], f(rt_h[:]), ALU.subtract).then_inc(r_ready, 1)

            def group_columns(u):
                return bass.ds((u % NG) * GROUP, GROUP)

            def y_out(u):
                dve.wait_ge(d_mm, (UNITS - 1) * (u + 1))
                for c in range(C):
                    s = state[:, c, group_columns(u)]
                    nc.vector.scalar_tensor_tensor(out=s, in0=ps[:, YB[c], :], scalar=bdn2[:, c:c + 1], in1=s,
                                                   op0=ALU.add, op1=ALU.add).then_inc(y_dve, 1)

            def mean_square(u):
                dve.wait_ge(ss_mm, C * u + C)
                nc.vector.tensor_reduce(msum[:], ps[:, RB, 0:2 * TG * C].rearrange("p (c i n) -> p n i c", c=C, n=2)[:, 0, :, :],
                                        AX.X, ALU.add).then_inc(ms_sum, 1)
                dve.wait_ge(ms_sum, u + 1)
                nc.vector.tensor_scalar(msum[:], msum[:], 1.0 / D, RMS_EPS, ALU.mult, ALU.add).then_inc(ms_dve, 1)

            def root_halves(u):
                dve.wait_ge(ms_pool, u + 1)
                nc.vector.tensor_copy(root_h[:], root[:]).then_inc(rh_dve, 1)
                dve.wait_ge(rh_dve, u + 1)
                nc.vector.tensor_copy(wp[:, :, R_HI:R_HI + 1], f(root_h[:]).unsqueeze(2)).then_inc(rr_dve, 1)
                nc.vector.tensor_tensor(wp[:, :, R_HI + 1:R_HI + 2], root[:].unsqueeze(2), f(root_h[:]).unsqueeze(2),
                                        ALU.subtract).then_inc(rr_dve, 1)

            def rms(u):
                dve.wait_ge(rb_mm, u + 1)
                for c in range(C):
                    s = state[:, c, group_columns(u)]
                    nc.vector.scalar_tensor_tensor(out=s, in0=s, scalar=colp[:, bass.ds(NWC + c + u * C, 1)],
                                                   in1=ps[:, RB, :], op0=ALU.mult, op1=ALU.mult).then_inc(y_norm, 1)

            def group(u, first=False, last=False):
                for k in range(UNITS):
                    if k == 0:
                        route_a(u)
                    if k == UNITS - 1 and not first:
                        rms(u - 1)
                    if k < UNITS - 1:
                        h_low(u, k + 1)
                    elif not last:
                        h_low(u + 1, 0)
                    if k == 4 and not first:
                        mean_square(u - 1)
                    if k == 5 and not first:
                        root_halves(u - 1)
                    activated(u, k)
                    if k == 0:
                        route_b(u)
                        if not first:
                            y_out(u - 1)

            dve.wait_ge(o_mm, TILES)
            dve.wait_ge(w_done, NW)
            dve.wait_ge(n_mm, TILES)
            h_low(0, 0)
            group(0, first=True)
            with dve.Fori(1, GROUPS - 1) as u:
                group(u)
            group(GROUPS - 1, last=True)
            y_out(GROUPS - 1)
            mean_square(GROUPS - 1)
            root_halves(GROUPS - 1)
            rms(GROUPS - 1)

            for t in range(TILES):
                dve.wait_ge(f_mm, t + 1)
                nc.vector.scalar_tensor_tensor(out=x2[:, t, :], in0=ps[:, t % 8, 0:D], scalar=tanh_g[:, 1:2],
                                               in1=x2[:, t, :], op0=ALU.mult, op1=ALU.add).then_inc(f_dve, 1)

        @block.tensor
        def _(pe):
            def product(dst, terms):
                last = None
                n = 3 * len(terms)
                i = 0
                for wh, wl, xh, xl in terms:
                    for w, v in ((wh, xh), (wh, xl), (wl, xh)):
                        last = nc.tensor.matmul(dst, w, v, start=(i == 0), stop=(i == n - 1))
                        i += 1
                return last

            def wa(m, c, e, rows=P):
                return (wa_hi[0:rows, m, c * D + e * P:c * D + e * P + P], wa_lo[0:rows, m, c * D + e * P:c * D + e * P + P])

            for which in (0, 1):
                for j, (e, b) in enumerate(kv_jobs):
                    j += which * len(kv_jobs)
                    lo, hi = SB[b]
                    if j < 4:
                        pe.wait_ge(y_split_lo, b + 1)
                        pe.wait_ge(y_split_hi, b + 1)
                    if j == 0:
                        pe.wait_ge(wa_split_lo, 4)
                        pe.wait_ge(wh_done, 2)
                    bank_free(pe, "kv", j)
                    product(ps[:, bank_of("kv", j), 0:hi - lo],
                            [wa(which, c, e, HC) + (y_hi[:, c, lo:hi], y_lo[:, c, lo:hi]) for c in range(C)]).then_inc(kv_mm, 1)
            pe.wait_ge(const, 3)
            for g in range(NG):
                pe.wait_ge(ln_done, TG * (g + 1))
                for c in range(C):
                    bank_free(pe, "T", g, c)
                    for i in range(TG):
                        m = nc.tensor.transpose(ps[:, bank_of("T", g, c), i * P:i * P + P], ln_xn[:, i, c * P:c * P + P], ident[:])
                    m.then_inc(lnT_mm, 1)
                pe.wait_ge(lnT_dve, C * (g + 1))
                for e in range(C):
                    bank_free(pe, "Q", g, e)
                    product(ps[:, bank_of("Q", g, e), :],
                            [wa(2, c, e) + (ln_hi[:, c, :], ln_lo[:, c, :]) for c in range(C)]).then_inc(q_mm, 1)
            pe.wait_ge(kv_dve, KV)
            for b in range(KB):
                r = KROWS[b]
                bank_free(pe, "V", b)
                product(ps[0:r, bank_of("V", b), 0:D],
                        [(vT_hi[:, c, b * P:b * P + r], vT_lo[:, c, b * P:b * P + r],
                          wa_hi[:, 3, c * D:c * D + D], wa_lo[:, 3, c * D:c * D + D]) for c in range(C)]).then_inc(vo_mm, 1)

            def scores(t, b):
                lo, hi = SB[b]
                if b == 0:
                    pe.wait_ge(qs_lo, t + 1)
                    wait(pe, s_exp, t)
                product(ps[:, SCORE[b], 0:hi - lo],
                        [(q_hi[:, c, :], q_lo[:, c, :], k_hi[:, c, lo:hi], k_lo[:, c, lo:hi]) for c in range(C)]).then_inc(s_mm, 1)

            def transposes(t, i):
                if i == 0:
                    pe.wait_ge(s_exp, t + 1)
                wait(pe, t_dve, 4 * t + i - 1)
                for n, kb in enumerate(TGRP[i]):
                    r = KROWS[kb]
                    m = nc.tensor.transpose(ps[0:r, TBANK[i % 2], n * P:n * P + P], prob[:, kb * P:kb * P + r], ident[:])
                m.then_inc(t_mm, 1)

            def values(t):
                wait(pe, o_x2, t)
                for i, grp in enumerate(TGRP):
                    pe.wait_ge(t_dve, 4 * t + i + 1)
                    for kb in grp:
                        r = KROWS[kb]
                        ph, pl = pT_hi[0:r, kb * P:kb * P + P], pT_lo[0:r, kb * P:kb * P + P]
                        for n, (p, v) in enumerate(((ph, v_hi), (ph, v_lo), (pl, v_hi))):
                            m = nc.tensor.matmul(ps[:, OBANK, 0:D], p, v[0:r, kb, :], start=(kb == 0 and n == 0),
                                                 stop=(kb == KB - 1 and n == 2))
                m.then_inc(o_mm, 1)

            def normed_transposes(t):
                pe.wait_ge(o_n, t + 1)
                for c in range(C):
                    m = nc.tensor.transpose(ps[:, XBANK, c * P:c * P + P], o_row[:, c * P:c * P + P], ident[:])
                m.then_inc(n_mm, 1)

            def attention_tile(t, first=False, last=False):
                transposes(t, 0)
                transposes(t, 1)
                if not last:
                    scores(t + 1, 0)
                transposes(t, 2)
                if not last:
                    scores(t + 1, 1)
                transposes(t, 3)
                if not last:
                    scores(t + 1, 2)
                if not first:
                    normed_transposes(t - 1)
                if not last:
                    scores(t + 1, 3)
                values(t)

            pe.wait_ge(vo_lo, KB)
            for b in range(4):
                scores(0, b)
            attention_tile(0, first=True)
            with pe.Fori(1, TILES - 1) as t:
                attention_tile(t)
            attention_tile(TILES - 1, last=True)
            pe.wait_ge(n_act, TILES - 1)
            normed_transposes(TILES - 1)

            def w(m, c, e):
                return w_hi[:, m, c * D + e * P:c * D + e * P + P], w_lo[:, m, c * D + e * P:c * D + e * P + P]

            def up(u, k):
                if k == 0:
                    pe.wait_ge(xs_pool, u + 1)
                for e in range(C):
                    n = 2 * UNITS * u + 2 * k + e
                    wait(pe, u_act, 2 * (n - 1))
                    product(ps[:, HB[e], :], [w(up_index(k), c, e) + (xs_hi[:, c, :], xs_lo[:, c, :])
                                              for c in range(C)]).then_inc(u_mm, 1)

            def gate(u, k):
                pe.wait_ge(u_dve, 2 * UNITS * u + 2 * k + 2)
                for e in range(C):
                    n = 2 * UNITS * u + 2 * k + e
                    wait(pe, g_act, n - 1)
                    product(ps[:, GB[e], :], [w(gate_index(k), c, e) + (h_hi[:, k % 2, c, :], h_lo[:, k % 2, c, :])
                                              for c in range(C)]).then_inc(g_mm, 1)

            def down(u, k):
                pe.wait_ge(a_split_lo, 2 * (UNITS - 1) * u + 2 * k)
                if k == 1:
                    wait(pe, y_dve, C * u)
                for e in range(C):
                    i = 0
                    for c in range(C):
                        wh, wl = w(down_index(k), c, e)
                        ah, al = a_hi[:, k % 2, c, :], a_lo[:, k % 2, c, :]
                        for ww, a in ((wh, ah), (wh, al), (wl, ah)):
                            m = nc.tensor.matmul(ps[:, YB[e], :], ww, a, start=(k == 1 and i == 0),
                                                 stop=(k == UNITS - 1 and i == 5))
                            i += 1
                m.then_inc(d_mm, 1)

            def down_biases(u):
                pe.wait_ge(wT_act, u + 1)
                for e in range(C):
                    nc.tensor.matmul(ps[:, YB[e], :], bd[:, e * P:e * P + P], wT[:], start=False, stop=False)

            def expert_weights(u, k):
                pe.wait_ge(wT_act, u + 1)
                wait(pe, a_fin, 2 * (UNITS - 1) * u + 2 * (k - 1))
                nc.tensor.matmul(ps[:, BB, :], pick[:, k - 2, :], wT[:], start=True, stop=True).then_inc(b_mm, 1)

            def router_weights(u):
                pe.wait_ge(r_ready, 3 * u + 3)
                for i in range(TG):
                    m = nc.tensor.transpose(ps[:, RB, i * P:i * P + P], wp[:, i, :], ident[:])
                m.then_inc(wT_mm, 1)

            def squares(u, c):
                pe.wait_ge(sq_pool, C * u + c + 1)
                for i in range(TG):
                    col = 2 * (c * TG + i)
                    nc.tensor.matmul(ps[:, RB, col:col + 2], sq_hi[:, i * P:i * P + P], ones2[:], start=True, stop=False)
                    m = nc.tensor.matmul(ps[:, RB, col:col + 2], sq_lo[:, i * P:i * P + P], ones2[:], start=False, stop=True)
                m.then_inc(ss_mm, 1)

            def root_transposes(u):
                pe.wait_ge(rr_dve, 2 * u + 2)
                for i in range(TG):
                    m = nc.tensor.transpose(ps[:, RB, i * P:i * P + P], wp[:, i, :], ident[:])
                m.then_inc(rT_mm, 1)

            def root_broadcast(u):
                pe.wait_ge(rT_act, u + 1)
                nc.tensor.matmul(ps[:, RB, :], pick[:, NE, :], rT[:], start=True, stop=True).then_inc(rb_mm, 1)

            def group(u, first=False, last=False):
                for k in range(UNITS):
                    if k < UNITS - 1:
                        up(u, k + 1)
                    elif not last:
                        up(u + 1, 0)
                        router_gates(u + 1)
                    gate(u, k)
                    if k >= 2:
                        expert_weights(u, k)
                        down(u, k - 1)
                    if k == 0 and not first:
                        down(u - 1, UNITS - 1)
                    if k == 1:
                        router_weights(u)
                    if k == 2:
                        down_biases(u)
                        if not first:
                            squares(u - 1, 0)
                    if k == 3 and not first:
                        squares(u - 1, 1)
                    if k == 5 and not first:
                        root_transposes(u - 1)
                    if k == 6 and not first:
                        root_broadcast(u - 1)

            def router_gates(u):
                wait(pe, y_norm, C * (u - 1))
                for i in range(TG):
                    n = 0
                    for c in range(C):
                        xh, xl = xs_hi[:, c, i * P:i * P + P], xs_lo[:, c, i * P:i * P + P]
                        rh = wr_hi[:, bass.ds(u, 1), c, :].rearrange("p a e -> p (a e)")
                        rl = wr_lo[:, bass.ds(u, 1), c, :].rearrange("p a e -> p (a e)")
                        for a, b in ((xh, rh), (xh, rl), (xl, rh)):
                            m = nc.tensor.matmul(ps[:, RB, i * P:i * P + NE], a, b, start=(n == 0), stop=(n == 5))
                            n += 1
                m.then_inc(r_mm, 1)

            pe.wait_ge(w_done, NW)
            pe.wait_ge(n_act, TILES)
            up(0, 0)
            router_gates(0)
            pe.wait_ge(ones_done, 2 + NE)
            group(0, first=True)
            with pe.Fori(1, GROUPS - 1) as u:
                group(u)
            group(GROUPS - 1, last=True)
            down(GROUPS - 1, UNITS - 1)
            for c in range(C):
                squares(GROUPS - 1, c)
            root_transposes(GROUPS - 1)
            root_broadcast(GROUPS - 1)

            pe.wait_ge(y_norm, C * GROUPS)
            for t in range(TILES):
                g = t // TG
                pe.wait_ge(y_norm, C * (NG + g + 1))
                wait(pe, f_dve, t - 7)
                for c in range(C):
                    m = nc.tensor.transpose(ps[:, t % 8, c * P:c * P + P], state[:, c, t * P:t * P + P], ident[:])
                m.then_inc(f_mm, 1)


def kernel(**inputs):
    import concourse.bacc as bacc
    from concourse.bass_utils import run_bass_kernel_spmd as run

    a = {k: np.asarray(v) for k, v in inputs.items()}

    def rows_by_partition(w, p):
        k = w.shape[0] // p
        return w.reshape(k, p, w.shape[1]).transpose(1, 0, 2).reshape(p, k * w.shape[1])

    def columns(v):
        return v.reshape(-1, C, P).transpose(2, 0, 1).reshape(P, -1)

    ctxT = a["ctx_768"][0].T.reshape(C, HC, KEYS).transpose(1, 0, 2)
    w_att = np.zeros((P, 4, 2 * D), np.float32)
    w_att[0:HC, 0] = rows_by_partition(a["L0_xattn_Wk"], HC)
    w_att[0:HC, 1] = rows_by_partition(a["L0_xattn_Wv"], HC)
    w_att[:, 2] = rows_by_partition(a["L0_xattn_Wq"], P)
    w_att[:, 3] = rows_by_partition(a["L0_xattn_Wo"], P)
    ws = [a["L0_ffn_share_Wup"][:, 0:D], a["L0_ffn_share_Wup"][:, D:2 * D], a["L0_ffn_share_Wg"], a["L0_ffn_share_Wdown"]]
    for e in range(NE):
        ws += [a["L0_ffn_exp_Wup"][e], a["L0_ffn_exp_Wg"][e], a["L0_ffn_exp_Wdown"][e]]
    w_ffn = np.stack([rows_by_partition(m, P) for m in ws], axis=1)
    sbg = a["L0_ffn_share_bg"]
    cols = np.concatenate([columns(v) for v in (
        a["L0_xattn_bq"], a["L0_xattn_bk"], a["L0_xattn_bv"], a["L0_ffn_share_bup"], a["L0_ffn_exp_bup"],
        sbg, sbg, a["L0_ffn_exp_bg"], a["L0_ffn_share_bdown"], np.repeat(a["L0_ffn_norm_w"], NG, axis=0))], axis=1)
    rows = np.concatenate([a["L0_xattn_bo"], np.repeat(a["L0_ffn_router_b"], NG, axis=0).reshape(-1),
                           np.repeat(a["L0_ffn_gate_bias"], NG, axis=0).reshape(-1), a["g_xattn"], a["g_ffn"]])[None, :]
    w_router = np.repeat(a["L0_ffn_router_W"].reshape(ROUNDS, C, P, NE).transpose(2, 0, 1, 3), NG, axis=1).reshape(P, -1)
    arrays = {"x": a["x"][0], "ctxT": ctxT, "w_att": w_att, "w_ffn": w_ffn, "cols": cols, "rows": rows,
              "w_router": w_router, "b_down": a["L0_ffn_exp_bdown"]}
    arrays = {k: np.ascontiguousarray(v) for k, v in arrays.items()}
    assert arrays["cols"].shape == (P, NCOL) and arrays["rows"].shape == (1, NROW)

    nc = bacc.Bacc("TRN2", target_bir_lowering=False, num_devices=1)
    args = [nc.dram_tensor(k, v.shape, mybir.dt.from_np(v.dtype), kind="ExternalInput").ap() for k, v in arrays.items()]
    o = nc.dram_tensor("out", (NTOK, D), F32, kind="ExternalOutput").ap()
    build(nc, *args, o)
    r = run(nc, [arrays], core_ids=[0])
    return r.results[0]["out"].reshape(1, NTOK, D)
```

```python
from contextlib import ExitStack

import numpy as np

import concourse.bass as bass
from concourse import mybir

F32 = mybir.dt.float32
F32R = mybir.dt.float32r
ALU = mybir.AluOpType
ACT = mybir.ActivationFunctionType
AX = mybir.AxisListType

P = 128
D = 256
C = D // P
NTOK = 2048
TILES = NTOK // P
GROUP = 512
NG = NTOK // GROUP
TG = GROUP // P
DC = 192
DR = DC - P
A, B, E, A_LO = 0, 1, 2, 3
Y, Y_LO, YB, YE = 0, 1, 2, 3
PASSES = ((A, Y), (A, Y_LO), (A_LO, Y), (B, YB), (E, YE))
ONE_HI, ONE_LO = 64, 96
KEYS = 1601
KPAD = KEYS + 1
KB = (KEYS + P - 1) // P
KROWS = [min(P, KEYS - b * P) for b in range(KB)]
SB = [(0, 512), (512, 1024), (1024, 1536), (1536, KPAD)]
TGRP = [range(0, 4), range(4, 8), range(8, 12), range(12, 13)]
NE = 6
ROUNDS = 2
UNITS = 2 + NE
GROUPS = ROUNDS * NG
SCALE = 1.0 / float(np.sqrt(D // 8))
LN_EPS = 1e-5
RMS_EPS = 1e-6
WQ, WK, WV, WO = 0, C * D, C * D + C * 3 * P, C * D + 2 * C * 3 * P
WA = WO + C * D
NW = 22
WCHUNK = NW * 2 * D // TILES

BQ, BU = 0, 2
BG = BU + 2 * UNITS
BDN = BG + 2 * UNITS
NWC = BDN + 2
NCOL = NWC + 2 * GROUPS
R_RB = 0
R_GB = R_RB + NE * GROUPS
R_G = R_GB + NE * GROUPS
NROW = R_G + 2

W_HI, W_LO, W_HI2 = 0, 32, 64
R_HI = 96


def up_index(k):
    return k if k < 2 else 4 + 3 * (k - 2)


def gate_index(k):
    return 2 if k < 2 else 5 + 3 * (k - 2)


def down_index(k):
    return 3 if k < 2 else 6 + 3 * (k - 2)


def wait(eng, sem, value):
    if isinstance(value, int) and value <= 0:
        return
    eng.wait_ge(sem, value)


def build(nc, x, ctxT, w_att, b_o, w_ffn, cols, rows, w_router, b_down, norm_row, out):
    with ExitStack() as ctx:
        base = nc.sbuf_base
        place = [(base + 31) // 32 * 32]

        def at(name, shape, dt, offset):
            return nc.alloc_sbuf_tensor_at(name, shape, dt, offset=offset)

        def sb(name, shape, dt=F32):
            size = 4 * int(np.prod(shape[1:]))
            t = at(name, shape, dt, place[0])
            place[0] += (size + 31) // 32 * 32
            return t

        sems = {}

        def sem(name):
            sems[name] = ctx.enter_context(nc.semaphore(name))
            return sems[name]

        colp = sb("colp", [P, NCOL])
        rowp = sb("rowp", [P, NROW])
        ident = sb("ident", [P, P])
        pick = sb("pick", [P, NE + 1, P], F32R)
        ones_col = sb("ones_col", [P, 1])
        ones2 = sb("ones2", [P, 2], F32R)
        tanh_g = sb("tanh_g", [P, 2])
        bdn2 = sb("bdn2", [P, 2])
        bd = sb("bd", [P, D], F32R)
        wr = sb("wr", [P, GROUPS, C, 2, NE], F32R)
        half = sb("half", [P, 1])
        tri = sb("tri", [P, NE, NE])
        wp = sb("wp", [P, TG, P])
        x2 = sb("x2", [P, TILES, D])
        state = sb("state", [P, C, NTOK])
        rsum = sb("rsum", [P, TILES])
        rinv = sb("rinv", [P, TILES])
        bmax = sb("bmax", [P, 4])
        negm = sb("negm", [P, 1])
        bn6 = sb("bn6", [P, TILES, 6])
        mv = sb("mv", [P, TILES, 2])
        var = sb("var", [P, TILES])
        rstd = sb("rstd", [P, TILES])

        region_a = place[0]
        yk = sb("yk", [P, 4, KPAD], F32R)
        v_hi = sb("v_hi", [P, KB, D], F32R)
        v_lo = sb("v_lo", [P, KB, D], F32R)
        stage = sb("stage", [P, WCHUNK])
        region_b = place[0]
        prob = sb("prob", [P, KEYS + 7])
        pT_hi = sb("pT_hi", [P, KB * P], F32R)
        pT_lo = sb("pT_lo", [P, KB * P], F32R)
        o_row = sb("o_row", [P, D])
        end_b = place[0]
        zt = sb("zt", [P, 4, P], F32R)
        z32 = sb("z32", [P, 3, P])
        end_a = place[0]
        place[0] = region_b
        ln_xn = sb("ln_xn", [P, TG, D])
        ln_hi = sb("ln_hi", [P, 2, C, GROUP], F32R)
        ln_lo = sb("ln_lo", [P, 2, C, GROUP], F32R)
        assert place[0] <= end_b
        place[0] = region_c = end_a
        w_hi = sb("w_hi", [P, NW * 2 * D], F32R)
        w_lo = sb("w_lo", [P, NW * 2 * D], F32R)
        end_c = place[0]
        z_e = at("z_e", [P, NTOK], F32, end_c - 4 * NTOK)
        assert end_c <= nc.sbuf_usable_end, (end_c, nc.sbuf_usable_end)
        place[0] = region_c
        y_raw = sb("y_raw", [P, 2, KPAD])
        wr_raw = sb("wr_raw", [P, GROUPS * C * NE])
        bd_raw = sb("bd_raw", [P, D])
        bd_hi = sb("bd_hi", [P, D], F32R)
        wa_raw = sb("wa_raw", [P, WA])
        wa_hi = sb("wa_hi", [P, WA], F32R)
        wa_lo = sb("wa_lo", [P, WA], F32R)
        wqk_hi = sb("wqk_hi", [P, C, 3 * P], F32R)
        wqk_lo = sb("wqk_lo", [P, C, 3 * P], F32R)
        wvo = sb("wvo", [P, 4, D], F32R)
        bo_rows = sb("bo_rows", [P, D])
        vo = sb("vo", [P, D])
        bq2 = sb("bq2", [P, C, 2], F32R)
        zbias = sb("zbias", [P, 3])
        assert place[0] <= end_c - 4 * NTOK, (place[0], end_c)
        place[0] = region_a
        xs_hi = sb("xs_hi", [P, C, GROUP], F32R)
        xs_lo = sb("xs_lo", [P, C, GROUP], F32R)
        h32 = sb("h32", [P, 2, C, GROUP])
        h_hi = sb("h_hi", [P, 2, C, GROUP], F32R)
        h_lo = sb("h_lo", [P, 2, C, GROUP], F32R)
        sg = sb("sg", [P, C, GROUP])
        aa = sb("aa", [P, C, GROUP])
        as0 = sb("as0", [P, C, GROUP])
        a_hi = sb("a_hi", [P, 2, C, GROUP], F32R)
        a_lo = sb("a_lo", [P, 2, C, GROUP], F32R)
        rt_g = sb("rt_g", [P, TG, NE])
        rt_b = sb("rt_b", [P, TG, NE])
        rt_gt = sb("rt_gt", [P, TG, NE, NE])
        rt_eq = sb("rt_eq", [P, TG, NE, NE])
        rt_c = sb("rt_c", [P, TG, NE])
        rt_s = sb("rt_s", [P, TG])
        rt_w = sb("rt_w", [P, TG, NE])
        rt_h = sb("rt_h", [P, TG, NE], F32R)
        msum = sb("msum", [P, TG])
        e_sums = sb("e_sums", [P, TG])
        root = sb("root", [P, TG])
        root_h = sb("root_h", [P, TG], F32R)
        rT = sb("rT", [P, GROUP], F32R)
        wT = sb("wT", [P, GROUP], F32R)
        sq = sb("sq", [P, C, GROUP])
        sq_sum = sb("sq_sum", [P, GROUP])
        sq_hi = sb("sq_hi", [P, GROUP], F32R)
        sq_lo = sb("sq_lo", [P, GROUP], F32R)
        w_row = sb("w_row", [P, D])
        assert place[0] <= end_a, (place[0], end_a)
        ps = ctx.enter_context(nc.psum_tensor("ps", [P, 8, 512], F32))

        ld_cols, ld_rows, ld_small, ld_bo = sem("ld_cols"), sem("ld_rows"), sem("ld_small"), sem("ld_bo")
        ld_wqk, ld_wvo = sem("ld_wqk"), sem("ld_wvo")
        ld_y = [sem(f"ld_y{b}") for b in range(4)]
        ld_x = [sem(f"ld_x{g}") for g in range(NG)]
        ld_w, out_done = sem("ld_w"), sem("out_done")
        zeroed, const, tg_done, ones_done = sem("zeroed"), sem("const"), sem("tg_done"), sem("ones_done")
        wa_split_hi, wa_split_lo = sem("wa_split_hi"), sem("wa_split_lo")
        y_split_hi, y_split_lo = sem("y_split_hi"), sem("y_split_lo")
        wqk_mm, wqk_act, wqk_dve = sem("wqk_mm"), sem("wqk_act"), sem("wqk_dve")
        zb_mm, zb_dve, bq_hi, bq_lo = sem("zb_mm"), sem("zb_dve"), sem("bq_hi"), sem("bq_lo")
        wvo_mm, wvo_act, wvo_dve, wvo_sum, wvo_e = (sem(n) for n in ("wvo_mm", "wvo_act", "wvo_dve", "wvo_sum", "wvo_e"))
        ye_low, ye_one, y_ones = sem("ye_low"), sem("ye_one"), sem("y_ones")
        ln_st, ln_ag, ln_var, ln_rs, ln_done = sem("ln_st"), sem("ln_ag"), sem("ln_var"), sem("ln_rs"), sem("ln_done")
        lnT_mm, lnT_act, lnT_dve = sem("lnT_mm"), sem("lnT_act"), sem("lnT_dve")
        z_mm, z_act = sem("z_mm"), sem("z_act")
        v_mm, v_act, v_dve = sem("v_mm"), sem("v_act"), sem("v_dve")
        w_done, wh_act, wh_done = sem("w_done"), sem("wh_act"), sem("wh_done")
        zs_32, zs_hi, zs_lo = sem("zs_32"), sem("zs_hi"), sem("zs_lo")
        s_mm, s_max, s_neg, s_max4, s_exp = sem("s_mm"), sem("s_max"), sem("s_neg"), sem("s_max4"), sem("s_exp")
        t_mm, t_act, t_dve = sem("t_mm"), sem("t_act"), sem("t_dve")
        o_mm, o_inv, o_sc, o_x2, o_keep, o_bn, o_ag, o_var, o_rs, o_n = (sem(n) for n in (
            "o_mm", "o_inv", "o_sc", "o_x2", "o_keep", "o_bn", "o_ag", "o_var", "o_rs", "o_n"))
        n_mm, n_act = sem("n_mm"), sem("n_act")
        xs_act, xs_pool = sem("xs_act"), sem("xs_pool")
        u_mm, u_act, u_dve = sem("u_mm"), sem("u_act"), sem("u_dve")
        g_mm, g_act = sem("g_mm"), sem("g_act")
        a_mul, a_fin, a_split_hi, a_split_lo = sem("a_mul"), sem("a_fin"), sem("a_split_hi"), sem("a_split_lo")
        b_mm, d_mm = sem("b_mm"), sem("d_mm")
        r_mm, r_dve, r_tanh, r_chain, r_ready, wT_mm, wT_act = (sem(n) for n in (
            "r_mm", "r_dve", "r_tanh", "r_chain", "r_ready", "wT_mm", "wT_act"))
        y_dve, sq_act, sqs_pool, sqh_act, sq_pool, ss_mm, ms_dve, ms_pool, y_norm, rh_dve, rr_dve, rT_mm, rT_act, rb_mm = (sem(n) for n in (
            "y_dve", "sq_act", "sqs_pool", "sqh_act", "sq_pool", "ss_mm", "ms_dve", "ms_pool", "y_norm", "rh_dve", "rr_dve", "rT_mm",
            "rT_act", "rb_mm"))
        f_mm, f_dve = sem("f_mm"), sem("f_dve")
        ld_row, e_w, e_sum, e_mean, e_root, e_scale = (sem(n) for n in ("ld_row", "e_w", "e_sum", "e_mean", "e_root", "e_scale"))

        def f(ap):
            return ap.bitcast(F32)

        SCORE = [0, 1, 2, 3]
        TBANK = [4, 5]
        OBANK, XBANK = 6, 7
        HB, GB, DB, BB, RB = [0, 1], [2, 3], [4, 5], 6, 7

        jobs = [("wqk", 0), ("wqk", 1), ("zb", 0)]
        jobs += [("T", 0, c) for c in range(C)]
        jobs += [("wvo", part) for part in (A, B, E)]
        jobs += [("T", 1, c) for c in range(C)]
        V_AFTER = {1: range(0, 7), 2: range(7, KB)}
        for g in range(NG):
            jobs += [("z", g, part) for part in (A, B, E)]
            jobs += [("V", b) for b in V_AFTER.get(g, ())]
            if g + 2 < NG:
                jobs += [("T", g + 2, c) for c in range(C)]

        freed = {"wqk": lambda m: (wqk_dve, m + 1), "zb": lambda m: (zb_dve, 1), "wvo": lambda part: (wvo_dve, part + 1),
                 "T": lambda g, c: (lnT_dve, C * g + c + 1), "z": lambda g, part: (z_act, 3 * g + part + 1),
                 "V": lambda b: (v_dve, b + 1)}

        def bank_of(*job):
            return jobs.index(job) % 8

        def bank_free(eng, *job):
            before = jobs.index(job) - 8
            if before >= 0:
                kind, *which = jobs[before]
                eng.wait_ge(*freed[kind](*which))

        OUT_PAIRS = (TILES - TG) // 2

        def out_bank(p):
            return p if p < 4 else BB + p - 4

        block = ctx.enter_context(nc.Block())

        @block.sync
        def _(sp):
            xt = x.rearrange("(t p) d -> p t d", p=P)

            def load_x(g):
                sp.dma_start(x2[:, TG * g:TG * g + TG, :], xt[:, TG * g:TG * g + TG, :]).then_inc(ld_x[g], 16)

            sp.dma_start(wa_raw[:, 0:WV], w_att[:, 0:WV]).then_inc(ld_wqk, 16)
            load_x(0)
            sp.dma_start(colp[:], cols).then_inc(ld_cols, 16)
            sp.dma_start(wa_raw[:, WV:WA], w_att[:, WV:WA]).then_inc(ld_wvo, 16)
            sp.dma_start(bo_rows[:], b_o).then_inc(ld_bo, 16)
            load_x(1)
            for b, (lo, hi) in enumerate(SB):
                hi = min(hi, KEYS)
                sp.dma_start(y_raw[:, :, lo:hi], ctxT[:, :, lo:hi]).then_inc(ld_y[b], 16)
            load_x(2)
            load_x(3)
            sp.dma_start(rowp[:], rows.broadcast_to([P, NROW])).then_inc(ld_rows, 16)
            sp.dma_start(wr_raw[:], w_router).then_inc(ld_small, 16)
            sp.wait_ge(zeroed, 1)
            for p0 in (W_HI, W_LO, W_HI2):
                sp.dma_start(bd_raw[p0:p0 + NE, :], b_down).then_inc(ld_small, 16)
            sp.dma_start(stage[:], w_ffn[:, 0:WCHUNK]).then_inc(ld_w, 16)
            with sp.Fori(1, TILES) as m:
                sp.wait_ge(w_done, m)
                sp.dma_start(stage[:], w_ffn[:, bass.ds(m * WCHUNK, WCHUNK)]).then_inc(ld_w, 16)
            ot = out.rearrange("(t p) d -> p t d", p=P)
            sp.wait_ge(o_mm, TILES)
            sp.dma_start(w_row[:], norm_row.broadcast_to([P, D])).then_inc(ld_row, 16)
            for p in range(TILES // 2):
                sp.wait_ge(f_dve, p + 1)
                sp.dma_start(ot[:, 2 * p:2 * p + 2, :], x2[:, 2 * p:2 * p + 2, :]).then_inc(out_done, 16)
            sp.wait_ge(out_done, 16 * (TILES // 2))

        @block.gpsimd
        def _(pool):
            nc.gpsimd.memset(bd_raw[:], 0.0).then_inc(zeroed, 1)
            nc.gpsimd.memset(y_raw[:, :, KEYS:KPAD], 0.0).then_inc(zeroed, 1)
            nc.gpsimd.memset(ident[:], 0.0).then_inc(zeroed, 1)
            nc.gpsimd.memset(tri[:], 0.0).then_inc(zeroed, 1)
            nc.gpsimd.memset(wp[:], 0.0).then_inc(zeroed, 1)
            nc.gpsimd.memset(half[:], -0.5).then_inc(const, 1)
            pool.wait_ge(zeroed, 5)
            nc.gpsimd.affine_select(out=ident[:], in_=ident[:], compare_op=ALU.not_equal, fill=1.0,
                                    base=0, pattern=[[-1, P]], channel_multiplier=1).then_inc(const, 1)
            nc.gpsimd.affine_select(out=tri[:], in_=tri[:], compare_op=ALU.is_ge, fill=1.0,
                                    base=0, pattern=[[-1, NE], [1, NE]], channel_multiplier=0).then_inc(const, 1)
            def ln_root(g):
                pool.wait_ge(ln_var, g + 1)
                t = slice(TG * g, TG * g + TG)
                nc.gpsimd.tensor_tensor(rstd[:, t], var[:, t], half[:].broadcast_to([P, TG]), ALU.pow).then_inc(ln_rs, 1)

            pool.wait_ge(const, 2)
            nc.gpsimd.tensor_tensor(ones_col[:], ident[:, ONE_HI:ONE_HI + 1], ident[:, ONE_LO:ONE_LO + 1], ALU.add).then_inc(ye_one, 1)
            ln_root(0)
            pool.wait_ge(ye_one, 1)
            pool.wait_ge(ln_rs, 1)
            nc.gpsimd.tensor_copy(yk[DR:P, YE, :], ones_col[DR:P, :].broadcast_to([DR, KPAD])).then_inc(y_ones, 1)
            pool.wait_ge(y_ones, 1)
            for g in range(1, NG):
                ln_root(g)
                if g == 1:
                    pool.wait_ge(ln_rs, 2)
                    for b, (lo, hi) in enumerate(SB):
                        pool.wait_ge(y_split_hi, 2 * b + 2)
                        wait(pool, ye_low, b)
                        nc.gpsimd.tensor_tensor(yk[0:DR, YE, lo:hi], y_raw[0:DR, 1, lo:hi], f(yk[0:DR, YB, lo:hi]),
                                                ALU.subtract).then_inc(ye_low, 1)
                    pool.wait_ge(ye_low, len(SB))
            def attention_rstd(t):
                pool.wait_ge(o_var, t + 1)
                nc.gpsimd.tensor_tensor(rstd[:, bass.ds(t, 1)], var[:, bass.ds(t, 1)], half[:], ALU.pow).then_inc(o_rs, 1)

            def split_z(t):
                nc.gpsimd.tensor_copy(z32[:, A:B + 1, :], state[:, :, bass.ds(t * P, P)]).then_inc(zs_32, 1)
                nc.gpsimd.tensor_copy(z32[:, E, :], z_e[:, bass.ds(t * P, P)]).then_inc(zs_32, 1)
                pool.wait_ge(zs_32, 2 * t + 2)
                pool.wait_ge(zs_hi, 2 * t + 2)
                nc.gpsimd.tensor_tensor(zt[:, A_LO, :], z32[:, A, :], f(zt[:, A, :]), ALU.subtract).then_inc(zs_lo, 1)
                pool.wait_ge(zs_lo, 3 * t + 1)
                nc.gpsimd.tensor_tensor(zt[DR:P, B, :], z32[DR:P, B, :], f(zt[DR:P, B, :]), ALU.subtract).then_inc(zs_lo, 1)
                pool.wait_ge(zs_lo, 3 * t + 2)
                row = slice(ONE_LO, ONE_LO + 1)
                nc.gpsimd.tensor_tensor(zt[row, E, :], z32[row, E, :], f(zt[row, E, :]), ALU.subtract).then_inc(zs_lo, 1)
                pool.wait_ge(zs_lo, 3 * t + 3)

            pool.wait_ge(z_act, 3)
            split_z(0)
            pool.wait_ge(ld_small, 64)
            by_half = wr[:].rearrange("p u c h e -> p h (u c) e")
            raw = wr_raw[:].rearrange("p (n e) -> p n e", e=NE)
            nc.gpsimd.tensor_copy(by_half[:, 0], raw).then_inc(wh_done, 1)
            nc.gpsimd.tensor_copy(bd_hi[:], bd_raw[:]).then_inc(wh_done, 1)
            pool.wait_ge(wh_done, 2)
            nc.gpsimd.tensor_tensor(by_half[:, 1], raw, f(wr[:]).rearrange("p u c h e -> p h (u c) e")[:, 0],
                                    ALU.subtract).then_inc(const, 1)
            nc.gpsimd.tensor_copy(bd[0:W_HI2, :], f(bd_hi[0:W_HI2, :])).then_inc(const, 1)
            pool.wait_ge(const, 5)
            nc.gpsimd.tensor_tensor(bd[W_HI2:P, :], bd_raw[W_HI2:P, :], f(bd_hi[W_HI2:P, :]), ALU.subtract).then_inc(const, 1)
            pool.wait_ge(const, 6)
            pool.wait_ge(z_act, 3 * NG)
            split_z(1)
            split_z(2)
            with pool.Fori(1, TILES - 2) as t:
                attention_rstd(t - 1)
                split_z(t + 2)
            for t in range(TILES - 3, TILES - 1):
                attention_rstd(t)

            def split_input(u):
                lo = (u % NG) * GROUP
                pool.wait_ge(xs_act, u + 1)
                nc.gpsimd.tensor_tensor(xs_lo[:], state[:, :, bass.ds(lo, GROUP)], f(xs_hi[:]),
                                        ALU.subtract).then_inc(xs_pool, 1)

            def norm(u):
                pool.wait_ge(sq_act, C * u + C)
                nc.gpsimd.tensor_tensor(sq_sum[:], sq[:, 0, :], sq[:, 1, :], ALU.add).then_inc(sqs_pool, 1)
                pool.wait_ge(sqh_act, u + 1)
                nc.gpsimd.tensor_tensor(sq_lo[:], sq_sum[:], f(sq_hi[:]), ALU.subtract).then_inc(sq_pool, 1)
                pool.wait_ge(ms_dve, u + 1)
                nc.gpsimd.tensor_tensor(root[:], msum[:], half[:].broadcast_to([P, TG]), ALU.pow).then_inc(ms_pool, 1)

            split_input(0)
            attention_rstd(TILES - 1)
            split_input(1)
            with pool.Fori(1, GROUPS - 1) as u:
                norm(u - 1)
                split_input(u + 1)
            norm(GROUPS - 2)
            pool.wait_ge(e_mean, 1)
            nc.gpsimd.tensor_tensor(root[:], msum[:], half[:].broadcast_to([P, TG]), ALU.pow).then_inc(e_root, 1)

        @block.scalar
        def _(act):
            for n, part in enumerate((slice(WQ, WK), slice(WK, WV), slice(WV, WO), slice(WO, WA))):
                act.wait_ge(ld_wqk if n < 2 else ld_wvo, 16)
                nc.scalar.copy(wa_hi[:, part], wa_raw[:, part]).then_inc(wa_split_hi, 1)
            for m in range(C):
                act.wait_ge(wqk_mm, m + 1)
                nc.scalar.copy(wqk_hi[:, m, :], ps[:, bank_of("wqk", m), 0:3 * P]).then_inc(wqk_act, 1)

            def ln_high(g):
                for c in range(C):
                    act.wait_ge(lnT_mm, C * g + c + 1)
                    nc.scalar.copy(ln_hi[:, g % 2, c, :], ps[:, bank_of("T", g, c), :]).then_inc(lnT_act, 1)

            def z_out(g):
                for part in (A, B, E):
                    act.wait_ge(z_mm, 3 * g + part + 1)
                    columns = slice(GROUP * g, GROUP * g + GROUP)
                    nc.scalar.activation(z_e[:, columns] if part == E else state[:, part, columns], ps[:, bank_of("z", g, part), :],
                                         ACT.Identity, bias=zbias[:, part:part + 1]).then_inc(z_act, 1)

            def y_high(b):
                lo, hi = SB[b]
                act.wait_ge(ld_y[b], 16)
                nc.scalar.copy(yk[:, Y, lo:hi], y_raw[:, 0, lo:hi]).then_inc(y_split_hi, 1)
                nc.scalar.copy(yk[:, YB, lo:hi], y_raw[:, 1, lo:hi]).then_inc(y_split_hi, 1)

            def z_high(t):
                wait(act, s_mm, 4 * t)
                wait(act, zs_lo, 3 * t)
                nc.scalar.copy(zt[:, A:B + 1, :], state[:, :, bass.ds(t * P, P)]).then_inc(zs_hi, 1)
                nc.scalar.copy(zt[:, E, :], z_e[:, bass.ds(t * P, P)]).then_inc(zs_hi, 1)

            act.wait_ge(zeroed, 2)
            y_high(0)
            y_high(1)
            ln_high(0)
            y_high(2)
            y_high(3)
            for part in (A, B):
                act.wait_ge(wvo_mm, part + 1)
                nc.scalar.copy(wvo[:, part, :], ps[:, bank_of("wvo", part), 0:D]).then_inc(wvo_act, 1)
            ln_high(1)
            act.wait_ge(zb_dve, 1)
            for g in range(NG):
                z_out(g)
                if g == 0:
                    act.wait_ge(z_act, 3)
                    z_high(0)
                for b in V_AFTER.get(g, ()):
                    r = KROWS[b]
                    act.wait_ge(v_mm, b + 1)
                    nc.scalar.copy(v_hi[0:r, b, :], ps[0:r, bank_of("V", b), 0:D]).then_inc(v_act, 1)
                if g + 2 < NG:
                    ln_high(g + 2)
                if g == 1:
                    act.wait_ge(ld_rows, 16)
                    nc.scalar.activation(tanh_g[:], rowp[:, R_G:R_G + 2], ACT.Tanh).then_inc(tg_done, 1)
                    act.wait_ge(ld_cols, 16)
                    nc.scalar.activation(bdn2[:], colp[:, BDN:BDN + 2], ACT.Copy, scale=2.0).then_inc(tg_done, 1)

            def exponent(t):
                act.wait_ge(s_neg, t + 1)
                wait(act, t_mm, 4 * t)
                nc.scalar.activation(prob[:, 0:KEYS], ps[:, 0:4, :].rearrange("p b n -> p (b n)")[:, 0:KEYS], ACT.Exp,
                                     bias=negm[:, 0:1], scale=SCALE,
                                     accum_out=rsum[:, bass.ds(t, 1)]).then_inc(s_exp, 1)

            def high_halves(t):
                for i, grp in enumerate(TGRP):
                    act.wait_ge(t_mm, 4 * t + i + 1)
                    n, k0 = len(grp) * P, grp[0] * P
                    rows = KROWS[grp[0]]
                    nc.scalar.copy(pT_hi[0:rows, k0:k0 + n], ps[0:rows, TBANK[i % 2], 0:n]).then_inc(t_act, 1)

            def to_state(t):
                act.wait_ge(n_mm, t + 1)
                nc.scalar.copy(state[:, :, bass.ds(t * P, P)],
                               ps[:, XBANK, 0:D].rearrange("p (c n) -> p c n", c=C)).then_inc(n_act, 1)

            def weights_high(t):
                act.wait_ge(ld_w, 16 * (t + 1))
                nc.scalar.copy(w_hi[:, bass.ds(t * WCHUNK, WCHUNK)], stage[:]).then_inc(wh_act, 1)

            act.wait_ge(v_dve, KB)
            act.wait_ge(z_act, 3 * NG)
            act.wait_ge(const, 6)
            exponent(0)
            z_high(1)
            high_halves(0)
            weights_high(0)
            z_high(2)
            exponent(1)
            with act.Fori(1, TILES - 2) as t:
                high_halves(t)
                weights_high(t)
                z_high(t + 2)
                exponent(t + 1)
                to_state(t - 1)
            high_halves(TILES - 2)
            weights_high(TILES - 2)
            exponent(TILES - 1)
            to_state(TILES - 3)
            high_halves(TILES - 1)
            weights_high(TILES - 1)

            def input_high(u):
                wait(act, u_mm, 2 * UNITS * u)
                wait(act, d_mm, (UNITS - 1) * (u - 1))
                nc.scalar.copy(xs_hi[:], state[:, :, bass.ds((u % NG) * GROUP, GROUP)]).then_inc(xs_act, 1)

            input_high(0)

            def after_up(u, k):
                for c in range(C):
                    n = 2 * UNITS * u + 2 * k + c
                    act.wait_ge(u_mm, n + 1)
                    wait(act, a_mul, n + 1 - 4)
                    wait(act, g_mm, 2 * UNITS * u + 2 * (k - 2) + 2)
                    bias = colp[:, BU + 2 * k + c:BU + 2 * k + c + 1]
                    nc.scalar.activation(h32[:, k % 2, c, :], ps[:, HB[c], :], ACT.Identity, bias=bias).then_inc(u_act, 1)
                    nc.scalar.activation(h_hi[:, k % 2, c, :], ps[:, HB[c], :], ACT.Identity, bias=bias).then_inc(u_act, 1)

            def after_gate(u, k):
                for c in range(C):
                    n = 2 * UNITS * u + 2 * k + c
                    act.wait_ge(g_mm, n + 1)
                    wait(act, a_mul, n + 1 - 2)
                    nc.scalar.activation(sg[:, c, :], ps[:, GB[c], :], ACT.Silu,
                                         bias=colp[:, BG + 2 * k + c:BG + 2 * k + c + 1]).then_inc(g_act, 1)

            def square(u, c):
                act.wait_ge(y_dve, C * u + c + 1)
                nc.scalar.activation(sq[:, c, :], state[:, c, bass.ds((u % NG) * GROUP, GROUP)], ACT.Square).then_inc(sq_act, 1)

            def squares_high(u):
                act.wait_ge(sqs_pool, u + 1)
                nc.scalar.copy(sq_hi[:], sq_sum[:]).then_inc(sqh_act, 1)

            def root_transposed(u):
                act.wait_ge(rT_mm, u + 1)
                nc.scalar.copy(rT[:], ps[:, RB, :]).then_inc(rT_act, 1)

            def group(u, first=False, last=False):
                for k in range(UNITS):
                    if k == UNITS - 2 and not last:
                        input_high(u + 1)
                    if k < UNITS - 1:
                        after_up(u, k + 1)
                    elif not last:
                        after_up(u + 1, 0)
                    after_gate(u, k)
                    if k == 0 and first:
                        to_state(TILES - 1)
                    if k == 0:
                        act.wait_ge(r_tanh, 2 * u + 1)
                        nc.scalar.activation(rt_w[:], rt_w[:], ACT.Tanh, scale=0.5).then_inc(r_tanh, 1)
                    if k == 1:
                        act.wait_ge(wT_mm, u + 1)
                        wait(act, d_mm, 7 * u)
                        nc.scalar.copy(wT[:], ps[:, RB, :]).then_inc(wT_act, 1)
                    if k == 1 and not first:
                        square(u - 1, 0)
                        square(u - 1, 1)
                    if k == 2 and not first:
                        squares_high(u - 1)
                    if k == 6 and not first:
                        root_transposed(u - 1)

            act.wait_ge(o_mm, TILES)
            act.wait_ge(w_done, TILES)
            to_state(TILES - 2)
            after_up(0, 0)
            group(0, first=True)
            with act.Fori(1, GROUPS - 1) as u:
                group(u)
            group(GROUPS - 1, last=True)
            for i in range(TG):
                act.wait_ge(f_mm, OUT_PAIRS + i // 2 + 1)
                wait(act, e_sum, i)
                nc.scalar.activation(sq[:, 0, 0:D], ps[:, i // 2, (i % 2) * D:(i % 2) * D + D], ACT.Square,
                                     accum_out=e_sums[:, i:i + 1]).then_inc(e_sum, 1)

        @block.vector
        def _(dve):
            dve.wait_ge(const, 3)
            dve.wait_ge(zeroed, 5)
            nc.vector.tensor_scalar(ones2[:], wp[:, 0, 0:2], 1.0, None, ALU.add).then_inc(ones_done, 1)
            nc.vector.tensor_scalar(pick[:, NE, :], wp[:, 0, :], ident[:, R_HI:R_HI + 1], ident[:, R_HI + 1:R_HI + 2],
                                    ALU.add, ALU.add).then_inc(ones_done, 1)
            for e in range(NE):
                nc.vector.tensor_scalar(pick[:, e, :], wp[:, 0, :], ident[:, W_HI + e:W_HI + e + 1],
                                        ident[:, W_LO + e:W_LO + e + 1], ALU.add, ALU.add).then_inc(ones_done, 1)
            def weights_low_att(parts):
                for n, part in parts:
                    dve.wait_ge(wa_split_hi, n + 1)
                    nc.vector.tensor_tensor(wa_lo[:, part], wa_raw[:, part], f(wa_hi[:, part]), ALU.subtract).then_inc(wa_split_lo, 1)

            weights_low_att(((0, slice(WQ, WK)), (1, slice(WK, WV))))

            def stats(g):
                dve.wait_ge(ld_x[g], 16)
                for t in range(TG * g, TG * g + TG):
                    nc.vector.bn_stats(bn6[:, t, :], x2[:, t, :]).then_inc(ln_st, 1)
                dve.wait_ge(ln_st, TG * (g + 1))
                for t in range(TG * g, TG * g + TG):
                    nc.vector.bn_aggr(mv[:, t, :], bn6[:, t, :]).then_inc(ln_ag, 1)
                dve.wait_ge(ln_ag, TG * (g + 1))
                nc.vector.tensor_scalar(var[:, TG * g:TG * g + TG], mv[:, TG * g:TG * g + TG, 1], LN_EPS, None,
                                        ALU.add).then_inc(ln_var, 1)

            def normalize(g):
                dve.wait_ge(ln_rs, g + 1)
                wait(dve, lnT_mm, C * g)
                for i in range(TG):
                    t = TG * g + i
                    nc.vector.tensor_scalar(ln_xn[:, i, :], x2[:, t, :], mv[:, t, 0:1], rstd[:, t:t + 1],
                                            ALU.subtract, ALU.mult).then_inc(ln_done, 1)

            def ln_low(g):
                for c in range(C):
                    dve.wait_ge(lnT_act, C * g + c + 1)
                    nc.vector.tensor_tensor(ln_lo[:, g % 2, c, :], ps[:, bank_of("T", g, c), :], f(ln_hi[:, g % 2, c, :]),
                                            ALU.subtract).then_inc(lnT_dve, 1)

            dve.wait_ge(ld_cols, 16)
            bq = colp[:, BQ:BQ + C].unsqueeze(2)
            nc.vector.tensor_copy(bq2[:, :, 0:1], bq).then_inc(bq_hi, 1)
            dve.wait_ge(bq_hi, 1)
            nc.vector.tensor_tensor(bq2[:, :, 1:2], bq, f(bq2[:, :, 0:1]), ALU.subtract).then_inc(bq_lo, 1)
            stats(0)
            for m in range(C):
                dve.wait_ge(wqk_act, m + 1)
                nc.vector.tensor_tensor(wqk_lo[:, m, :], ps[:, bank_of("wqk", m), 0:3 * P], f(wqk_hi[:, m, :]),
                                        ALU.subtract).then_inc(wqk_dve, 1)
            normalize(0)
            dve.wait_ge(zb_mm, 1)
            nc.vector.tensor_reduce(zbias[:], ps[:, bank_of("zb", 0), 0:6].rearrange("p (s n) -> p s n", n=2), AX.X,
                                    ALU.add).then_inc(zb_dve, 1)
            weights_low_att(((2, slice(WV, WO)), (3, slice(WO, WA))))
            stats(1)
            ln_low(0)

            def y_low(b):
                lo, hi = SB[b]
                dve.wait_ge(y_split_hi, 2 * b + 1)
                nc.vector.tensor_tensor(yk[:, Y_LO, lo:hi], y_raw[:, 0, lo:hi], f(yk[:, Y, lo:hi]),
                                        ALU.subtract).then_inc(y_split_lo, 1)

            normalize(1)
            y_low(0)
            dve.wait_ge(wvo_act, 1)
            nc.vector.tensor_tensor(wvo[:, A_LO, :], ps[:, bank_of("wvo", A), 0:D], f(wvo[:, A, :]), ALU.subtract).then_inc(wvo_dve, 1)
            dve.wait_ge(wvo_act, 2)
            nc.vector.tensor_tensor(wvo[DR:P, B, :], ps[DR:P, bank_of("wvo", B), 0:D], f(wvo[DR:P, B, :]),
                                    ALU.subtract).then_inc(wvo_dve, 1)
            dve.wait_ge(wvo_mm, 3)
            dve.wait_ge(ld_bo, 16)
            nc.vector.tensor_tensor(vo[:], ps[:, bank_of("wvo", E), 0:D], bo_rows[:], ALU.add).then_inc(wvo_sum, 1)
            dve.wait_ge(wvo_sum, 1)
            nc.vector.tensor_copy(wvo[:, E, :], vo[:]).then_inc(wvo_e, 1)
            dve.wait_ge(wvo_e, 1)
            row = slice(ONE_LO, ONE_LO + 1)
            nc.vector.tensor_tensor(wvo[row, E, :], vo[row, :], f(wvo[row, E, :]), ALU.subtract).then_inc(wvo_dve, 1)
            ln_low(1)
            stats(2)
            normalize(2)
            for b in range(1, len(SB)):
                y_low(b)
            stats(3)
            for g in range(1, NG):
                if g > 1:
                    for b in V_AFTER.get(g - 1, ()):
                        r = KROWS[b]
                        dve.wait_ge(v_act, b + 1)
                        nc.vector.tensor_tensor(v_lo[0:r, b, :], ps[0:r, bank_of("V", b), 0:D], f(v_hi[0:r, b, :]),
                                                ALU.subtract).then_inc(v_dve, 1)
                if g + 1 < NG:
                    ln_low(g + 1)
                if g + 2 < NG:
                    normalize(g + 2)

            def weights_low(t):
                part = bass.ds(t * WCHUNK, WCHUNK)
                dve.wait_ge(wh_act, t + 1)
                nc.vector.tensor_tensor(w_lo[:, part], stage[:], f(w_hi[:, part]), ALU.subtract).then_inc(w_done, 1)

            def bank_max(t, b):
                lo, hi = SB[b]
                dve.wait_ge(s_mm, 4 * t + b + 1)
                nc.vector.tensor_reduce(bmax[:, b:b + 1], ps[:, SCORE[b], 0:min(hi, KEYS) - lo], AX.X,
                                        ALU.max).then_inc(s_max, 1)

            def neg_max(t):
                dve.wait_ge(s_max, 4 * t + 4)
                nc.vector.tensor_reduce(bmax[:, 0:1], bmax[:, 0:4], AX.X, ALU.max).then_inc(s_max4, 1)
                dve.wait_ge(s_max4, t + 1)
                nc.vector.tensor_scalar(negm[:], bmax[:, 0:1], -SCALE, None, ALU.mult).then_inc(s_neg, 1)

            def low_half(t, i):
                grp = TGRP[i]
                n, k0, rows = len(grp) * P, grp[0] * P, KROWS[grp[0]]
                dve.wait_ge(t_act, 4 * t + i + 1)
                nc.vector.tensor_tensor(pT_lo[0:rows, k0:k0 + n], ps[0:rows, TBANK[i % 2], 0:n],
                                        f(pT_hi[0:rows, k0:k0 + n]), ALU.subtract).then_inc(t_dve, 1)

            def residual(t):
                one = bass.ds(t, 1)
                dve.wait_ge(s_exp, t + 1)
                nc.vector.reciprocal(rinv[:, one], rsum[:, one]).then_inc(o_inv, 1)
                dve.wait_ge(o_inv, t + 1)
                nc.vector.tensor_tensor(rinv[:, one], rinv[:, one], tanh_g[:, 0:1], ALU.mult).then_inc(o_sc, 1)
                dve.wait_ge(o_sc, t + 1)
                dve.wait_ge(o_mm, t + 1)
                wait(dve, n_mm, t)
                row = x2[:, one, :].rearrange("p a n -> p (a n)")
                nc.vector.scalar_tensor_tensor(out=o_row[:], in0=ps[:, OBANK, 0:D], scalar=rinv[:, one], in1=row,
                                               op0=ALU.mult, op1=ALU.add).then_inc(o_x2, 1)
                dve.wait_ge(o_x2, t + 1)
                nc.vector.bn_stats(bn6[:, 0, :], o_row[:]).then_inc(o_bn, 1)
                dve.wait_ge(o_bn, t + 1)
                nc.vector.tensor_scalar(row, o_row[:], 1.0, None, ALU.mult).then_inc(o_keep, 1)
                nc.vector.bn_aggr(mv[:, 0, :], bn6[:, 0, :]).then_inc(o_ag, 1)
                dve.wait_ge(o_ag, t + 1)
                nc.vector.tensor_scalar(var[:, one], mv[:, 0, 1:2], LN_EPS, None, ALU.add).then_inc(o_var, 1)

            def normed(t):
                one = bass.ds(t, 1)
                dve.wait_ge(o_rs, t + 1)
                nc.vector.tensor_scalar(o_row[:], o_row[:], mv[:, 0, 0:1],
                                        rstd[:, one], ALU.subtract, ALU.mult).then_inc(o_n, 1)

            dve.wait_ge(tg_done, 2)
            for b in range(4):
                bank_max(0, b)
            neg_max(0)

            def attention_tile(t, first=False, last=False):
                low_half(t, 0)
                low_half(t, 1)
                if not last:
                    bank_max(t + 1, 0)
                low_half(t, 2)
                if not first:
                    residual(t - 1)
                low_half(t, 3)
                if not last:
                    for b in range(1, 4):
                        bank_max(t + 1, b)
                    neg_max(t + 1)
                if not first:
                    normed(t - 1)
                weights_low(t)

            attention_tile(0, first=True)
            with dve.Fori(1, TILES - 1) as t:
                attention_tile(t)
            attention_tile(TILES - 1, last=True)
            residual(TILES - 1)
            normed(TILES - 1)

            def h_low(u, k):
                for c in range(C):
                    n = 2 * UNITS * u + 2 * k + c
                    dve.wait_ge(u_act, 2 * n + 2)
                    nc.vector.tensor_tensor(h_lo[:, k % 2, c, :], h32[:, k % 2, c, :], f(h_hi[:, k % 2, c, :]),
                                            ALU.subtract).then_inc(u_dve, 1)

            def activated(u, k):
                for c in range(C):
                    n = 2 * UNITS * u + 2 * k + c
                    m = 2 * (UNITS - 1) * u + 2 * (k - 1) + c
                    dve.wait_ge(g_act, n + 1)
                    if k == 0:
                        nc.vector.tensor_tensor(as0[:, c, :], sg[:, c, :], h32[:, 0, c, :], ALU.mult).then_inc(a_mul, 1)
                        continue
                    nc.vector.tensor_tensor(aa[:, c, :], sg[:, c, :], h32[:, k % 2, c, :], ALU.mult).then_inc(a_mul, 1)
                    dve.wait_ge(a_mul, n + 1)
                    if k == 1:
                        nc.vector.tensor_tensor(aa[:, c, :], aa[:, c, :], as0[:, c, :], ALU.add).then_inc(a_fin, 1)
                    else:
                        dve.wait_ge(b_mm, NE * u + k - 1)
                        nc.vector.tensor_tensor(aa[:, c, :], ps[:, BB, :], aa[:, c, :], ALU.mult).then_inc(a_fin, 1)
                    dve.wait_ge(a_fin, m + 1)
                    wait(dve, d_mm, (UNITS - 1) * u + (k - 2 if k > 2 else 0))
                    nc.vector.tensor_copy(a_hi[:, k % 2, c, :], aa[:, c, :]).then_inc(a_split_hi, 1)
                    dve.wait_ge(a_split_hi, m + 1)
                    nc.vector.tensor_tensor(a_lo[:, k % 2, c, :], aa[:, c, :], f(a_hi[:, k % 2, c, :]),
                                            ALU.subtract).then_inc(a_split_lo, 1)

            CHAIN = 13

            def route_a(u):
                step = [0]

                def link(instruction):
                    step[0] += 1
                    instruction.then_inc(r_chain, 1)
                    dve.wait_ge(r_chain, CHAIN * u + step[0])

                def per_tile(row):
                    return rowp[:, bass.ds(row + u * NE, NE)].unsqueeze(1).broadcast_to([P, TG, NE])

                dve.wait_ge(r_mm, u + 1)
                gates = ps[:, RB, 0:TG * P].rearrange("p (t n) -> p t n", t=TG)
                link(nc.vector.tensor_tensor(rt_g[:], gates[:, :, 0:NE], per_tile(R_RB), ALU.add))
                link(nc.vector.tensor_tensor(rt_g[:], gates[:, :, NE:2 * NE], rt_g[:], ALU.add))
                link(nc.vector.tensor_tensor(rt_b[:], rt_g[:], per_tile(R_GB), ALU.add))
                mine = rt_b[:].unsqueeze(3).broadcast_to([P, TG, NE, NE])
                other = rt_b[:].unsqueeze(2).broadcast_to([P, TG, NE, NE])
                nc.vector.tensor_tensor(rt_gt[:], other, mine, ALU.is_gt).then_inc(r_dve, 1)
                link(nc.vector.tensor_tensor(rt_eq[:], other, mine, ALU.is_equal))
                link(nc.vector.tensor_tensor(rt_eq[:], rt_eq[:], tri[:].unsqueeze(1).broadcast_to([P, TG, NE, NE]), ALU.mult))
                dve.wait_ge(r_dve, 2 * u + 1)
                link(nc.vector.tensor_tensor(rt_gt[:], rt_gt[:], rt_eq[:], ALU.add))
                link(nc.vector.tensor_reduce(rt_c[:], rt_gt[:], AX.X, ALU.add))
                link(nc.vector.tensor_scalar(rt_c[:], rt_c[:], 2.0, None, ALU.is_lt))
                link(nc.vector.tensor_tensor(rt_w[:], rt_g[:], rt_c[:], ALU.mult))
                link(nc.vector.tensor_reduce(rt_s[:], rt_w[:], AX.X, ALU.add))
                link(nc.vector.tensor_scalar(rt_w[:], rt_g[:], 2.0, None, ALU.mult))
                nc.vector.tensor_tensor(rt_w[:], rt_w[:], rt_s[:].unsqueeze(2).broadcast_to([P, TG, NE]),
                                        ALU.subtract).then_inc(r_tanh, 1)

            def route_b(u):
                dve.wait_ge(r_tanh, 2 * u + 2)
                nc.vector.tensor_scalar(rt_w[:], rt_w[:], 0.5, 0.5, ALU.mult, ALU.add).then_inc(r_chain, 1)
                dve.wait_ge(r_chain, CHAIN * u + CHAIN - 1)
                nc.vector.tensor_tensor(rt_w[:], rt_w[:], rt_c[:], ALU.mult).then_inc(r_chain, 1)
                dve.wait_ge(r_chain, CHAIN * u + CHAIN)
                nc.vector.tensor_copy(rt_h[:], rt_w[:]).then_inc(r_dve, 1)
                dve.wait_ge(r_dve, 2 * u + 2)
                nc.vector.tensor_copy(wp[:, :, W_HI:W_HI + NE], f(rt_h[:])).then_inc(r_ready, 1)
                nc.vector.tensor_copy(wp[:, :, W_HI2:W_HI2 + NE], f(rt_h[:])).then_inc(r_ready, 1)
                nc.vector.tensor_tensor(wp[:, :, W_LO:W_LO + NE], rt_w[:], f(rt_h[:]), ALU.subtract).then_inc(r_ready, 1)

            def group_columns(u):
                return bass.ds((u % NG) * GROUP, GROUP)

            def y_out(u):
                dve.wait_ge(d_mm, (UNITS - 1) * (u + 1))
                for c in range(C):
                    s = state[:, c, group_columns(u)]
                    nc.vector.scalar_tensor_tensor(out=s, in0=ps[:, DB[c], :], scalar=bdn2[:, c:c + 1], in1=s,
                                                   op0=ALU.add, op1=ALU.add).then_inc(y_dve, 1)

            def mean_square(u):
                dve.wait_ge(ss_mm, u + 1)
                nc.vector.tensor_scalar(msum[:], ps[:, RB, 0:2 * TG].rearrange("p (i n) -> p n i", n=2)[:, 0, :], 1.0 / D, RMS_EPS,
                                        ALU.mult, ALU.add).then_inc(ms_dve, 1)

            def root_halves(u):
                dve.wait_ge(ms_pool, u + 1)
                nc.vector.tensor_copy(root_h[:], root[:]).then_inc(rh_dve, 1)
                dve.wait_ge(rh_dve, u + 1)
                nc.vector.tensor_copy(wp[:, :, R_HI:R_HI + 1], f(root_h[:]).unsqueeze(2)).then_inc(rr_dve, 1)
                nc.vector.tensor_tensor(wp[:, :, R_HI + 1:R_HI + 2], root[:].unsqueeze(2), f(root_h[:]).unsqueeze(2),
                                        ALU.subtract).then_inc(rr_dve, 1)

            def rms(u):
                dve.wait_ge(rb_mm, u + 1)
                for c in range(C):
                    s = state[:, c, group_columns(u)]
                    nc.vector.scalar_tensor_tensor(out=s, in0=s, scalar=colp[:, bass.ds(NWC + c + u * C, 1)],
                                                   in1=ps[:, RB, :], op0=ALU.mult, op1=ALU.mult).then_inc(y_norm, 1)

            def group(u, first=False, last=False):
                for k in range(UNITS):
                    if k == 0:
                        route_a(u)
                    if k == UNITS - 1 and not first:
                        rms(u - 1)
                    if k < UNITS - 1:
                        h_low(u, k + 1)
                    elif not last:
                        h_low(u + 1, 0)
                    if k == 4 and not first:
                        mean_square(u - 1)
                    if k == 5 and not first:
                        root_halves(u - 1)
                    activated(u, k)
                    if k == 0:
                        route_b(u)
                        if not first:
                            y_out(u - 1)

            dve.wait_ge(o_mm, TILES)
            dve.wait_ge(w_done, TILES)
            h_low(0, 0)
            group(0, first=True)
            with dve.Fori(1, GROUPS - 1) as u:
                group(u)
            group(GROUPS - 1, last=True)
            def out_pair(p):
                dve.wait_ge(f_mm, p + 1)
                rows = x2[:, 2 * p:2 * p + 2, :].rearrange("p t d -> p (t d)")
                nc.vector.scalar_tensor_tensor(out=rows, in0=ps[:, out_bank(p), :], scalar=tanh_g[:, 1:2],
                                               in1=rows, op0=ALU.mult, op1=ALU.add).then_inc(f_dve, 1)

            for p in range(4):
                out_pair(p)
            y_out(GROUPS - 1)
            for p in range(4, OUT_PAIRS):
                out_pair(p)
            dve.wait_ge(ld_row, 16)
            dve.wait_ge(a_split_lo, 2 * (UNITS - 1) * GROUPS)
            for i in range(2):
                dve.wait_ge(f_mm, OUT_PAIRS + i + 1)
                dve.wait_ge(e_sum, 2 * i + 2)
                nc.vector.tensor_tensor(aa[:, i, :].rearrange("p (t d) -> p t d", d=D),
                                        ps[:, i, :].rearrange("p (t d) -> p t d", d=D),
                                        w_row[:].unsqueeze(1).broadcast_to([P, 2, D]), ALU.mult).then_inc(e_w, 1)
            dve.wait_ge(e_sum, TG)
            nc.vector.tensor_scalar(msum[:], e_sums[:], 1.0 / D, RMS_EPS, ALU.mult, ALU.add).then_inc(e_mean, 1)
            dve.wait_ge(e_root, 1)
            nc.vector.tensor_scalar(root[:], root[:], tanh_g[:, 1:2], None, ALU.mult).then_inc(e_scale, 1)
            dve.wait_ge(e_scale, 1)
            dve.wait_ge(e_w, 2)
            for i in range(TG):
                row = x2[:, TILES - TG + i, :]
                m = nc.vector.scalar_tensor_tensor(out=row, in0=aa[:, i // 2, (i % 2) * D:(i % 2) * D + D],
                                                   scalar=root[:, i:i + 1], in1=row, op0=ALU.mult, op1=ALU.add)
                if i % 2:
                    m.then_inc(f_dve, 1)

        @block.tensor
        def _(pe):
            def product(dst, terms):
                last = None
                n = 3 * len(terms)
                i = 0
                for wh, wl, xh, xl in terms:
                    for w, v in ((wh, xh), (wh, xl), (wl, xh)):
                        last = nc.tensor.matmul(dst, w, v, start=(i == 0), stop=(i == n - 1))
                        i += 1
                return last

            def halves(start, n):
                return wa_hi[:, start:start + n], wa_lo[:, start:start + n]

            pe.wait_ge(wa_split_lo, 2)
            for m in range(C):
                product(ps[:, bank_of("wqk", m), 0:3 * P],
                        [halves(WQ + c * D + m * P, P) + halves(WK + c * 3 * P, 3 * P) for c in range(C)]).then_inc(wqk_mm, 1)
            pe.wait_ge(bq_lo, 1)
            for part in (A, B, E):
                for c in range(C):
                    for n, w in enumerate(halves(WK + c * 3 * P + part * P, P)):
                        m = nc.tensor.matmul(ps[:, bank_of("zb", 0), 2 * part:2 * part + 2], w, bq2[:, c, :],
                                             start=(c == 0 and n == 0), stop=(c == C - 1 and n == 1))
            m.then_inc(zb_mm, 1)
            pe.wait_ge(const, 3)
            def x_transposes(g):
                pe.wait_ge(ln_done, TG * (g + 1))
                for c in range(C):
                    bank_free(pe, "T", g, c)
                    for i in range(TG):
                        m = nc.tensor.transpose(ps[:, bank_of("T", g, c), i * P:i * P + P], ln_xn[:, i, c * P:c * P + P], ident[:])
                    m.then_inc(lnT_mm, 1)

            x_transposes(0)
            pe.wait_ge(wa_split_lo, 4)
            for part in (A, B, E):
                bank_free(pe, "wvo", part)
                product(ps[:, bank_of("wvo", part), 0:D],
                        [halves(WV + c * 3 * P + part * P, P) + halves(WO + c * D, D) for c in range(C)]).then_inc(wvo_mm, 1)
            x_transposes(1)
            pe.wait_ge(wqk_dve, C)
            for g in range(NG):
                pe.wait_ge(lnT_dve, C * (g + 1))
                for part in (A, B, E):
                    bank_free(pe, "z", g, part)
                    columns = slice(part * P, part * P + P)
                    product(ps[:, bank_of("z", g, part), :],
                            [(wqk_hi[:, c, columns], wqk_lo[:, c, columns], ln_hi[:, g % 2, c, :], ln_lo[:, g % 2, c, :])
                             for c in range(C)]).then_inc(z_mm, 1)
                for b in V_AFTER.get(g, ()):
                    if b == 0:
                        pe.wait_ge(y_split_lo, len(SB))
                        pe.wait_ge(ye_low, len(SB))
                        pe.wait_ge(y_ones, 1)
                        pe.wait_ge(wvo_dve, 3)
                    r = KROWS[b]
                    bank_free(pe, "V", b)
                    for n, (left, right) in enumerate(PASSES):
                        m = nc.tensor.matmul(ps[0:r, bank_of("V", b), 0:D], yk[:, right, b * P:b * P + r], wvo[:, left, :],
                                             start=(n == 0), stop=(n == len(PASSES) - 1))
                    m.then_inc(v_mm, 1)
                if g + 2 < NG:
                    x_transposes(g + 2)

            def scores(t, b):
                lo, hi = SB[b]
                if b == 0:
                    pe.wait_ge(zs_lo, 3 * (t + 1))
                    wait(pe, s_exp, t)
                for n, (left, right) in enumerate(PASSES):
                    m = nc.tensor.matmul(ps[:, SCORE[b], 0:hi - lo], zt[:, left, :], yk[:, right, lo:hi],
                                         start=(n == 0), stop=(n == len(PASSES) - 1))
                m.then_inc(s_mm, 1)

            def transposes(t, i):
                if i == 0:
                    pe.wait_ge(s_exp, t + 1)
                wait(pe, t_dve, 4 * t + i - 1)
                for n, kb in enumerate(TGRP[i]):
                    r = KROWS[kb]
                    m = nc.tensor.transpose(ps[0:r, TBANK[i % 2], n * P:n * P + P], prob[:, kb * P:kb * P + r], ident[:])
                m.then_inc(t_mm, 1)

            def values(t):
                wait(pe, o_x2, t)
                for i, grp in enumerate(TGRP):
                    pe.wait_ge(t_dve, 4 * t + i + 1)
                    for kb in grp:
                        r = KROWS[kb]
                        ph, pl = pT_hi[0:r, kb * P:kb * P + P], pT_lo[0:r, kb * P:kb * P + P]
                        for n, (p, v) in enumerate(((ph, v_hi), (ph, v_lo), (pl, v_hi))):
                            m = nc.tensor.matmul(ps[:, OBANK, 0:D], p, v[0:r, kb, :], start=(kb == 0 and n == 0),
                                                 stop=(kb == KB - 1 and n == 2))
                m.then_inc(o_mm, 1)

            def normed_transposes(t):
                pe.wait_ge(o_n, t + 1)
                for c in range(C):
                    m = nc.tensor.transpose(ps[:, XBANK, c * P:c * P + P], o_row[:, c * P:c * P + P], ident[:])
                m.then_inc(n_mm, 1)

            def attention_tile(t, first=False, last=False):
                transposes(t, 0)
                transposes(t, 1)
                if not last:
                    scores(t + 1, 0)
                transposes(t, 2)
                if not last:
                    scores(t + 1, 1)
                transposes(t, 3)
                if not last:
                    scores(t + 1, 2)
                    scores(t + 1, 3)
                values(t)
                if not first:
                    normed_transposes(t - 1)

            pe.wait_ge(v_dve, KB)
            pe.wait_ge(z_act, 3 * NG)
            for b in range(4):
                scores(0, b)
            attention_tile(0, first=True)
            with pe.Fori(1, TILES - 1) as t:
                attention_tile(t)
            attention_tile(TILES - 1, last=True)

            def w(m, c, e):
                start = (m * C + c) * D + e * P
                return w_hi[:, start:start + P], w_lo[:, start:start + P]

            def up(u, k):
                if k == 0:
                    pe.wait_ge(xs_pool, u + 1)
                for e in range(C):
                    n = 2 * UNITS * u + 2 * k + e
                    wait(pe, u_act, 2 * (n - 1))
                    product(ps[:, HB[e], :], [w(up_index(k), c, e) + (xs_hi[:, c, :], xs_lo[:, c, :])
                                              for c in range(C)]).then_inc(u_mm, 1)

            def gate(u, k):
                pe.wait_ge(u_dve, 2 * UNITS * u + 2 * k + 2)
                for e in range(C):
                    n = 2 * UNITS * u + 2 * k + e
                    wait(pe, g_act, n - 1)
                    product(ps[:, GB[e], :], [w(gate_index(k), c, e) + (h_hi[:, k % 2, c, :], h_lo[:, k % 2, c, :])
                                              for c in range(C)]).then_inc(g_mm, 1)

            def down(u, k):
                pe.wait_ge(a_split_lo, 2 * (UNITS - 1) * u + 2 * k)
                if k == 1:
                    wait(pe, y_dve, C * u)
                for e in range(C):
                    i = 0
                    for c in range(C):
                        wh, wl = w(down_index(k), c, e)
                        ah, al = a_hi[:, k % 2, c, :], a_lo[:, k % 2, c, :]
                        for ww, a in ((wh, ah), (wh, al), (wl, ah)):
                            m = nc.tensor.matmul(ps[:, DB[e], :], ww, a, start=(k == 1 and i == 0),
                                                 stop=(k == UNITS - 1 and i == 5))
                            i += 1
                m.then_inc(d_mm, 1)

            def down_biases(u):
                pe.wait_ge(wT_act, u + 1)
                for e in range(C):
                    nc.tensor.matmul(ps[:, DB[e], :], bd[:, e * P:e * P + P], wT[:], start=False, stop=False)

            def expert_weights(u, k):
                pe.wait_ge(wT_act, u + 1)
                wait(pe, a_fin, 2 * (UNITS - 1) * u + 2 * (k - 1))
                nc.tensor.matmul(ps[:, BB, :], pick[:, k - 2, :], wT[:], start=True, stop=True).then_inc(b_mm, 1)

            def router_weights(u):
                pe.wait_ge(r_ready, 3 * u + 3)
                for i in range(TG):
                    m = nc.tensor.transpose(ps[:, RB, i * P:i * P + P], wp[:, i, :], ident[:])
                m.then_inc(wT_mm, 1)

            def squares(u):
                pe.wait_ge(sq_pool, u + 1)
                for i in range(TG):
                    nc.tensor.matmul(ps[:, RB, 2 * i:2 * i + 2], sq_hi[:, i * P:i * P + P], ones2[:], start=True, stop=False)
                    m = nc.tensor.matmul(ps[:, RB, 2 * i:2 * i + 2], sq_lo[:, i * P:i * P + P], ones2[:], start=False, stop=True)
                m.then_inc(ss_mm, 1)

            def root_transposes(u):
                pe.wait_ge(rr_dve, 2 * u + 2)
                for i in range(TG):
                    m = nc.tensor.transpose(ps[:, RB, i * P:i * P + P], wp[:, i, :], ident[:])
                m.then_inc(rT_mm, 1)

            def root_broadcast(u):
                pe.wait_ge(rT_act, u + 1)
                nc.tensor.matmul(ps[:, RB, :], pick[:, NE, :], rT[:], start=True, stop=True).then_inc(rb_mm, 1)

            def group(u, first=False, last=False):
                for k in range(UNITS):
                    if k < UNITS - 1:
                        up(u, k + 1)
                    elif not last:
                        up(u + 1, 0)
                    gate(u, k)
                    if k == 0 and first:
                        pe.wait_ge(n_act, TILES - 1)
                        normed_transposes(TILES - 1)
                        pe.wait_ge(n_act, TILES)
                        router_gates(0)
                    if k == UNITS - 1 and not last:
                        router_gates(u + 1)
                    if k >= 2:
                        expert_weights(u, k)
                        down(u, k - 1)
                    if k == 0 and not first:
                        down(u - 1, UNITS - 1)
                    if k == 1:
                        router_weights(u)
                    if k == 2:
                        down_biases(u)
                    if k == 3 and not first:
                        squares(u - 1)
                    if k == 5 and not first:
                        root_transposes(u - 1)
                    if k == 6 and not first:
                        root_broadcast(u - 1)

            def router_gates(u):
                wait(pe, y_norm, C * (u - 1))
                for i in range(TG):
                    for c in range(C):
                        xh, xl = xs_hi[:, c, i * P:i * P + P], xs_lo[:, c, i * P:i * P + P]
                        w_both = wr[:, bass.ds(u, 1), c, :, :].rearrange("p a h e -> p (a h e)")
                        w_high = wr[:, bass.ds(u, 1), c, 0, :].rearrange("p a e -> p (a e)")
                        nc.tensor.matmul(ps[:, RB, i * P:i * P + 2 * NE], xh, w_both, start=(c == 0), stop=False)
                        m = nc.tensor.matmul(ps[:, RB, i * P:i * P + NE], xl, w_high, start=False, stop=(c == C - 1))
                m.then_inc(r_mm, 1)

            pe.wait_ge(w_done, TILES)
            up(0, 0)
            pe.wait_ge(ones_done, 2 + NE)
            group(0, first=True)
            with pe.Fori(1, GROUPS - 1) as u:
                group(u)
            group(GROUPS - 1, last=True)

            def out_transposes(p, bank):
                for i in range(2):
                    for c in range(C):
                        t = 2 * p + i
                        m = nc.tensor.transpose(ps[:, bank, i * D + c * P:i * D + c * P + P], state[:, c, t * P:t * P + P], ident[:])
                m.then_inc(f_mm, 1)

            pe.wait_ge(y_norm, C * (GROUPS - 2))
            pe.wait_ge(u_act, 4 * UNITS * GROUPS)
            pe.wait_ge(g_act, 2 * UNITS * GROUPS)
            for p in range(4):
                out_transposes(p, out_bank(p))
            down(GROUPS - 1, UNITS - 1)
            pe.wait_ge(y_norm, C * (GROUPS - 1))
            for p in range(4, OUT_PAIRS):
                out_transposes(p, out_bank(p))
            pe.wait_ge(y_dve, C * GROUPS)
            for i in range(2):
                pe.wait_ge(f_dve, i + 1)
                out_transposes(OUT_PAIRS + i, i)


def kernel(**inputs):
    import concourse.bacc as bacc
    from concourse.bass_utils import run_bass_kernel_spmd as run

    a = {k: np.asarray(v) for k, v in inputs.items()}

    def rows_by_partition(w, p):
        k = w.shape[0] // p
        return w.reshape(k, p, w.shape[1]).transpose(1, 0, 2).reshape(p, k * w.shape[1])

    def columns(v):
        return v.reshape(-1, C, P).transpose(2, 0, 1).reshape(P, -1)

    y = a["ctx_768"][0].T
    ctxT = np.stack([y[:P], np.concatenate([y[P:], y[P:]])], axis=1)

    def parts(w, bias):
        e = np.zeros((D, P), w.dtype)
        e[:, :DR], e[:, ONE_HI], e[:, ONE_LO] = w[:, P:], bias, bias
        return np.concatenate([w[:, :P], w[:, P:], w[:, P:], e], axis=1)

    w_att = np.concatenate([rows_by_partition(w, P) for w in (
        a["L0_xattn_Wq"].T, parts(a["L0_xattn_Wk"].T, a["L0_xattn_bk"]), parts(a["L0_xattn_Wv"].T, a["L0_xattn_bv"]),
        a["L0_xattn_Wo"])], axis=1)
    b_o = np.zeros((P, D), np.float32)
    b_o[[ONE_HI, ONE_LO]] = a["L0_xattn_bo"]
    ws = [a["L0_ffn_share_Wup"][:, 0:D], a["L0_ffn_share_Wup"][:, D:2 * D], a["L0_ffn_share_Wg"], a["L0_ffn_share_Wdown"]]
    for e in range(NE):
        ws += [a["L0_ffn_exp_Wup"][e], a["L0_ffn_exp_Wg"][e], a["L0_ffn_exp_Wdown"][e]]
    w_ffn = np.concatenate([rows_by_partition(m, P) for m in ws], axis=1)
    sbg = a["L0_ffn_share_bg"]
    cols = np.concatenate([columns(v) for v in (
        a["L0_xattn_bq"], a["L0_ffn_share_bup"], a["L0_ffn_exp_bup"],
        sbg, sbg, a["L0_ffn_exp_bg"], a["L0_ffn_share_bdown"], np.repeat(a["L0_ffn_norm_w"], NG, axis=0))], axis=1)
    rows = np.concatenate([np.repeat(a["L0_ffn_router_b"], NG, axis=0).reshape(-1),
                           np.repeat(a["L0_ffn_gate_bias"], NG, axis=0).reshape(-1), a["g_xattn"], a["g_ffn"]])[None, :]
    w_router = np.repeat(a["L0_ffn_router_W"].reshape(ROUNDS, C, P, NE).transpose(2, 0, 1, 3), NG, axis=1).reshape(P, -1)
    arrays = {"x": a["x"][0], "ctxT": ctxT, "w_att": w_att, "b_o": b_o, "w_ffn": w_ffn, "cols": cols, "rows": rows,
              "w_router": w_router, "b_down": a["L0_ffn_exp_bdown"],
              "norm_row": a["L0_ffn_norm_w"][ROUNDS - 1:ROUNDS]}
    arrays = {k: np.ascontiguousarray(v) for k, v in arrays.items()}
    assert arrays["cols"].shape == (P, NCOL) and arrays["rows"].shape == (1, NROW)

    nc = bacc.Bacc("TRN2", target_bir_lowering=False, num_devices=1)
    args = [nc.dram_tensor(k, v.shape, mybir.dt.from_np(v.dtype), kind="ExternalInput").ap() for k, v in arrays.items()]
    o = nc.dram_tensor("out", (NTOK, D), F32, kind="ExternalOutput").ap()
    build(nc, *args, o)
    r = run(nc, [arrays], core_ids=[0])
    return r.results[0]["out"].reshape(1, NTOK, D)
```

```python
from contextlib import ExitStack

import numpy as np

import concourse.bass as bass
from concourse import mybir

F32 = mybir.dt.float32
F32R = mybir.dt.float32r
ALU = mybir.AluOpType
ACT = mybir.ActivationFunctionType
AX = mybir.AxisListType

P = 128
D = 256
C = D // P
NTOK = 2048
TILES = NTOK // P
GROUP = 512
NG = NTOK // GROUP
TG = GROUP // P
DC = 192
DR = DC - P
A, B, E, A_LO = 0, 1, 2, 3
Y, Y_LO, YB, YE = 0, 1, 2, 3
PASSES = ((A, Y), (A, Y_LO), (A_LO, Y), (B, YB), (E, YE))
ONE_HI, ONE_LO = 64, 96
KEYS = 1601
KPAD = KEYS + 1
KB = (KEYS + P - 1) // P
KROWS = [min(P, KEYS - b * P) for b in range(KB)]
SW = KEYS // 4
SB = [(0, SW), (SW, 2 * SW), (2 * SW, 3 * SW), (3 * SW, KPAD)]
TGRP = [range(0, 4), range(4, 8), range(8, 12), range(12, 13)]
NE = 6
ROUNDS = 2
UNITS = 2 + NE
GROUPS = ROUNDS * NG
SCALE = 1.0 / float(np.sqrt(D // 8))
LN_EPS = 1e-5
RMS_EPS = 1e-6
WQ, WK, WV, WO = 0, C * D, C * D + C * 3 * P, C * D + 2 * C * 3 * P
WA = WO + C * D
NW = 22
WCHUNK = NW * 2 * D // TILES

BQ, BU = 0, 2
BG = BU + 2 * UNITS
NCOL = BG + 2 * UNITS
R_RB = 0
R_GB = R_RB + NE * ROUNDS
R_G = R_GB + NE * ROUNDS
NROW = R_G + 2

W_HI, W_LO, W_HI2 = 0, 32, 64
TWO_HI, TWO_LO = 31, 96


def up_index(k):
    return k if k < 2 else 4 + 3 * (k - 2)


def gate_index(k):
    return 2 if k < 2 else 5 + 3 * (k - 2)


def down_index(k):
    return 3 if k < 2 else 6 + 3 * (k - 2)


def wait(eng, sem, value):
    if isinstance(value, int) and value <= 0:
        return
    eng.wait_ge(sem, value)


def build(nc, x, ctxT, w_att, b_o, w_ffn, cols, rows, w_router, b_down, norm_rows, out):
    with ExitStack() as ctx:
        base = nc.sbuf_base
        place = [(base + 31) // 32 * 32]

        def at(name, shape, dt, offset):
            return nc.alloc_sbuf_tensor_at(name, shape, dt, offset=offset)

        def sb(name, shape, dt=F32):
            size = 4 * int(np.prod(shape[1:]))
            t = at(name, shape, dt, place[0])
            place[0] += (size + 31) // 32 * 32
            return t

        sems = {}

        def sem(name):
            sems[name] = ctx.enter_context(nc.semaphore(name))
            return sems[name]

        colp = sb("colp", [P, NCOL])
        rowp = sb("rowp", [P, NROW])
        w_rows = sb("w_rows", [P, ROUNDS * D])
        ident = sb("ident", [P, P])
        ones_col = sb("ones_col", [P, 1])
        tanh_g = sb("tanh_g", [P, 2])
        bd = sb("bd", [P, D], F32R)
        wr = sb("wr", [P, ROUNDS, C, 2, NE], F32R)
        half = sb("half", [P, 1])
        tri = sb("tri", [P, NE, NE])
        wp = sb("wp", [P, TG, P])
        x2 = sb("x2", [P, TILES, D])
        state = sb("state", [P, TILES * D])
        rsum = sb("rsum", [P, TILES])
        rsum2 = sb("rsum2", [P, TILES])
        rinv = sb("rinv", [P, TILES])
        bmax = sb("bmax", [P, 4])
        negm = sb("negm", [P, 1])
        bn6 = sb("bn6", [P, TILES, 6])
        mv = sb("mv", [P, TILES, 2])
        var = sb("var", [P, TILES])
        rstd = sb("rstd", [P, TILES])

        region_a = place[0]
        yk = sb("yk", [P, 4, KPAD], F32R)
        v_hi = sb("v_hi", [P, KB, D], F32R)
        v_lo = sb("v_lo", [P, KB, D], F32R)
        stage = sb("stage", [P, WCHUNK])
        region_b = place[0]
        prob = sb("prob", [P, KEYS + 7])
        pT_hi = sb("pT_hi", [P, KB * P], F32R)
        pT_lo = sb("pT_lo", [P, KB * P], F32R)
        o_row = sb("o_row", [P, D])
        end_b = place[0]
        zt = sb("zt", [P, 4, P], F32R)
        z32 = sb("z32", [P, 3, P])
        end_a = place[0]
        place[0] = region_b
        ln_xn = sb("ln_xn", [P, TG, D])
        ln_hi = sb("ln_hi", [P, 2, C, GROUP], F32R)
        ln_lo = sb("ln_lo", [P, 2, C, GROUP], F32R)
        assert place[0] <= end_b
        place[0] = region_c = end_a
        w_hi = sb("w_hi", [P, NW * 2 * D], F32R)
        w_lo = sb("w_lo", [P, NW * 2 * D], F32R)
        end_c = place[0]
        z_e = at("z_e", [P, NTOK], F32, end_c - 4 * NTOK)
        assert end_c <= nc.sbuf_usable_end, (end_c, nc.sbuf_usable_end)
        place[0] = region_c
        y_raw = sb("y_raw", [P, 2, KPAD])
        wr_raw = sb("wr_raw", [P, ROUNDS * C * NE])
        bd_raw = sb("bd_raw", [P, D])
        bd_hi = sb("bd_hi", [P, D], F32R)
        wa_raw = sb("wa_raw", [P, WA])
        wa_hi = sb("wa_hi", [P, WA], F32R)
        wa_lo = sb("wa_lo", [P, WA], F32R)
        wqk_hi = sb("wqk_hi", [P, C, 3 * P], F32R)
        wqk_lo = sb("wqk_lo", [P, C, 3 * P], F32R)
        wvo = sb("wvo", [P, 4, D], F32R)
        bo_rows = sb("bo_rows", [P, D])
        vo = sb("vo", [P, D])
        bq2 = sb("bq2", [P, C, 2], F32R)
        zbias = sb("zbias", [P, 3])
        assert place[0] <= end_c - 4 * NTOK, (place[0], end_c)
        place[0] = region_a
        xs_hi = sb("xs_hi", [P, C, GROUP], F32R)
        xs_lo = sb("xs_lo", [P, C, GROUP], F32R)
        h32 = sb("h32", [P, 2, C, GROUP])
        h_hi = sb("h_hi", [P, 2, C, GROUP], F32R)
        h_lo = sb("h_lo", [P, 2, C, GROUP], F32R)
        sg = sb("sg", [P, C, GROUP])
        aa = sb("aa", [P, C, GROUP])
        as0 = sb("as0", [P, C, GROUP])
        a_hi = sb("a_hi", [P, 2, C, GROUP], F32R)
        a_lo = sb("a_lo", [P, 2, C, GROUP], F32R)
        rt_g = sb("rt_g", [P, TG, NE])
        rt_b = sb("rt_b", [P, TG, NE])
        rt_gt = sb("rt_gt", [P, TG, NE, NE])
        rt_eq = sb("rt_eq", [P, TG, NE, NE])
        rt_c = sb("rt_c", [P, TG, NE])
        rt_s = sb("rt_s", [P, TG])
        rt_w = sb("rt_w", [P, TG, NE])
        rt_h = sb("rt_h", [P, TG, NE], F32R)
        rt_wf = sb("rt_wf", [P, TG, NE])
        msum = sb("msum", [P, TG])
        sums = sb("sums", [P, TG])
        root = sb("root", [P, TG])
        wT = sb("wT", [P, GROUP], F32R)
        acc = sb("acc", [P, TG, D])
        sq = sb("sq", [P, TG, D])
        x_in = sb("x_in", [P, TG * D])
        assert place[0] <= end_a, (place[0], end_a)
        ps = ctx.enter_context(nc.psum_tensor("ps", [P, 8, 512], F32))

        ld_cols, ld_rows, ld_small, ld_bo = sem("ld_cols"), sem("ld_rows"), sem("ld_small"), sem("ld_bo")
        ld_wq, ld_wk, ld_wvo = sem("ld_wq"), sem("ld_wk"), sem("ld_wvo")
        ld_y = [sem(f"ld_y{b}") for b in range(4)]
        ld_x = [sem(f"ld_x{g}") for g in range(NG)]
        ld_w, out_done = sem("ld_w"), sem("out_done")
        zeroed, const, tg_done, twos = sem("zeroed"), sem("const"), sem("tg_done"), sem("twos")
        wa_split_hi, wa_split_lo, wo_split_lo = sem("wa_split_hi"), sem("wa_split_lo"), sem("wo_split_lo")
        y_split_hi, y_split_lo = sem("y_split_hi"), sem("y_split_lo")
        wqk_mm, wqk_act, wqk_dve = sem("wqk_mm"), sem("wqk_act"), sem("wqk_dve")
        zb_mm, zb_dve, bq_hi, bq_lo = sem("zb_mm"), sem("zb_dve"), sem("bq_hi"), sem("bq_lo")
        wvo_mm, wvo_act, wvo_dve, wvo_sum, wvo_e = (sem(n) for n in ("wvo_mm", "wvo_act", "wvo_dve", "wvo_sum", "wvo_e"))
        ye_low, ye_one, y_ones = sem("ye_low"), sem("ye_one"), sem("y_ones")
        ln_st, ln_ag, ln_var, ln_rs, ln_done = sem("ln_st"), sem("ln_ag"), sem("ln_var"), sem("ln_rs"), sem("ln_done")
        lnT_mm, lnT_act, lnT_dve = sem("lnT_mm"), sem("lnT_act"), sem("lnT_dve")
        z_mm, z_act, z_dve = sem("z_mm"), sem("z_act"), sem("z_dve")
        v_mm, v_act, v_dve = sem("v_mm"), sem("v_act"), sem("v_dve")
        w_done, wh_act, wh_done = sem("w_done"), sem("wh_act"), sem("wh_done")
        zs_32, zs_hi, zs_lo = sem("zs_32"), sem("zs_hi"), sem("zs_lo")
        s_mm, s_max, s_neg, s_max4, s_exp = sem("s_mm"), sem("s_max"), sem("s_neg"), sem("s_max4"), sem("s_exp")
        t_mm, t_act, t_dve = sem("t_mm"), sem("t_act"), sem("t_dve")
        o_sum = sem("o_sum")
        o_mm, o_inv, o_sc, o_x2, o_keep, o_bn, o_ag, o_var, o_rs, o_n = (sem(n) for n in (
            "o_mm", "o_inv", "o_sc", "o_x2", "o_keep", "o_bn", "o_ag", "o_var", "o_rs", "o_n"))
        x_fetch, xT_mm, xs_act, xs_dve = sem("x_fetch"), sem("xT_mm"), sem("xs_act"), sem("xs_dve")
        u_mm, u_act, u_dve = sem("u_mm"), sem("u_act"), sem("u_dve")
        g_mm, g_act = sem("g_mm"), sem("g_act")
        a_mul, a_fin, a_split_hi, a_split_lo = sem("a_mul"), sem("a_fin"), sem("a_split_hi"), sem("a_split_lo")
        d_mm, y_dve = sem("d_mm"), sem("y_dve")
        r_mm, r_dve, r_tanh, r_chain, r_ready, wT_mm, wT_act = (sem(n) for n in (
            "r_mm", "r_dve", "r_tanh", "r_chain", "r_ready", "wT_mm", "wT_act"))
        sq_act, ms_dve, ms_pool, y_norm = sem("sq_act"), sem("ms_dve"), sem("ms_pool"), sem("y_norm")
        ld_row, f_dve, e_w, e_scale = sem("ld_row"), sem("f_dve"), sem("e_w"), sem("e_scale")

        def f(ap):
            return ap.bitcast(F32)

        SCORE = [0, 1, 2, 3]
        TBANK = [4, 5]
        OBANK = 6
        HB, GB, DB, RB = [0, 1], [2, 3], [4, 5], 7
        XB = [6, 7]

        jobs = [("wqk", 0), ("wqk", 1), ("zb", 0)]
        jobs += [("T", 0, c) for c in range(C)]
        jobs += [("wvo", part) for part in (A, B, E)]
        jobs += [("T", 1, c) for c in range(C)]
        jobs += [("z", 0, part) for part in (A, B, E)] + [("z", 1, part) for part in (A, B, E)]
        jobs += [("T", 2, c) for c in range(C)]
        V_BLOCKS = (range(0, 7), range(7, KB))
        jobs += [("V", b) for b in V_BLOCKS[0]] + [("z", 2, part) for part in (A, B, E)]
        jobs += [("T", 3, c) for c in range(C)] + [("V", b) for b in V_BLOCKS[1]]
        Z3_BANKS = (6, 7, 5)

        freed = {"wqk": lambda m: (wqk_dve, m + 1), "zb": lambda m: (zb_dve, 1), "wvo": lambda part: (wvo_dve, part + 1),
                 "T": lambda g, c: (lnT_dve, C * g + c + 1), "z": lambda g, part: (z_act, 3 * g + part + 1),
                 "V": lambda b: (v_dve, b + 1)}

        def bank_of(*job):
            return Z3_BANKS[job[2]] if job[:2] == ("z", NG - 1) else jobs.index(job) % 8

        def bank_free(eng, *job):
            before = jobs.index(job) - 8
            if before >= 0:
                kind, *which = jobs[before]
                eng.wait_ge(*freed[kind](*which))

        def z_place(g, part):
            tiles = state[:, GROUP * C * g:GROUP * C * (g + 1)].rearrange("p (t s n) -> p s t n", t=TG, s=2)
            dst = z_e[:, GROUP * g:GROUP * g + GROUP].rearrange("p (t n) -> p t n", t=TG) if part == E else tiles[:, part]
            return dst, ps[:, bank_of("z", g, part), :].rearrange("p (t n) -> p t n", t=TG)

        block = ctx.enter_context(nc.Block())

        @block.sync
        def _(sp):
            xt = x.rearrange("(t p) d -> p t d", p=P)

            def load_x(g):
                sp.dma_start(x2[:, TG * g:TG * g + TG, :], xt[:, TG * g:TG * g + TG, :]).then_inc(ld_x[g], 16)

            sp.dma_start(wa_raw[:, WQ:WK], w_att[:, WQ:WK]).then_inc(ld_wq, 16)
            sp.dma_start(wa_raw[:, WK:WV], w_att[:, WK:WV]).then_inc(ld_wk, 16)
            load_x(0)
            sp.dma_start(colp[:], cols).then_inc(ld_cols, 16)
            sp.dma_start(wa_raw[:, WV:WA], w_att[:, WV:WA]).then_inc(ld_wvo, 16)
            sp.dma_start(bo_rows[:], b_o).then_inc(ld_bo, 16)
            load_x(1)
            for b, (lo, hi) in enumerate(SB):
                hi = min(hi, KEYS)
                sp.dma_start(y_raw[:, :, lo:hi], ctxT[:, :, lo:hi]).then_inc(ld_y[b], 16)
            load_x(2)
            load_x(3)
            sp.dma_start(rowp[:], rows.broadcast_to([P, NROW])).then_inc(ld_rows, 16)
            sp.dma_start(w_rows[:], norm_rows.broadcast_to([P, ROUNDS * D])).then_inc(ld_row, 16)
            sp.dma_start(wr_raw[:], w_router).then_inc(ld_small, 16)
            sp.wait_ge(zeroed, 1)
            for p0 in (W_HI, W_LO, W_HI2):
                sp.dma_start(bd_raw[p0:p0 + NE, :], b_down[0:NE, :]).then_inc(ld_small, 16)
            for p0 in (TWO_HI, TWO_LO):
                sp.dma_start(bd_raw[p0:p0 + 1, :], b_down[NE:NE + 1, :]).then_inc(ld_small, 16)
            sp.dma_start(stage[:], w_ffn[:, 0:WCHUNK]).then_inc(ld_w, 16)
            with sp.Fori(1, TILES) as m:
                sp.wait_ge(w_done, m)
                sp.dma_start(stage[:], w_ffn[:, bass.ds(m * WCHUNK, WCHUNK)]).then_inc(ld_w, 16)
            ot = out.rearrange("(t p) d -> p t d", p=P)
            for g in range(NG - 1):
                sp.wait_ge(f_dve, g + 1)
                sp.dma_start(ot[:, TG * g:TG * g + TG, :], x2[:, TG * g:TG * g + TG, :]).then_inc(out_done, 16)
            for i in range(2):
                sp.wait_ge(f_dve, NG + i)
                t = TILES - TG + 2 * i
                sp.dma_start(ot[:, t:t + 2, :], x2[:, t:t + 2, :]).then_inc(out_done, 16)
            sp.wait_ge(out_done, 16 * (NG + 1))

        @block.gpsimd
        def _(pool):
            nc.gpsimd.memset(bd_raw[:], 0.0).then_inc(zeroed, 1)
            nc.gpsimd.memset(y_raw[:, :, KEYS:KPAD], 0.0).then_inc(zeroed, 1)
            nc.gpsimd.memset(ident[:], 0.0).then_inc(zeroed, 1)
            nc.gpsimd.memset(tri[:], 0.0).then_inc(zeroed, 1)
            nc.gpsimd.memset(wp[:], 0.0).then_inc(zeroed, 1)
            nc.gpsimd.memset(half[:], -0.5).then_inc(const, 1)
            pool.wait_ge(zeroed, 5)
            nc.gpsimd.affine_select(out=ident[:], in_=ident[:], compare_op=ALU.not_equal, fill=1.0,
                                    base=0, pattern=[[-1, P]], channel_multiplier=1).then_inc(const, 1)
            nc.gpsimd.affine_select(out=tri[:], in_=tri[:], compare_op=ALU.is_ge, fill=1.0,
                                    base=0, pattern=[[-1, NE], [1, NE]], channel_multiplier=0).then_inc(const, 1)

            def ln_root(g):
                pool.wait_ge(ln_var, g + 1)
                t = slice(TG * g, TG * g + TG)
                nc.gpsimd.tensor_tensor(rstd[:, t], var[:, t], half[:].broadcast_to([P, TG]), ALU.pow).then_inc(ln_rs, 1)

            pool.wait_ge(const, 2)
            nc.gpsimd.tensor_tensor(ones_col[:], ident[:, ONE_HI:ONE_HI + 1], ident[:, ONE_LO:ONE_LO + 1], ALU.add).then_inc(ye_one, 1)
            pool.wait_ge(ye_one, 1)
            pool.wait_ge(const, 3)
            nc.gpsimd.tensor_copy(yk[DR:P, YE, :], ones_col[DR:P, :].broadcast_to([DR, KPAD])).then_inc(y_ones, 1)
            pool.wait_ge(y_ones, 1)
            ln_root(0)
            pool.wait_ge(wa_split_hi, 4)
            nc.gpsimd.tensor_tensor(wa_lo[:, WO:WA], wa_raw[:, WO:WA], f(wa_hi[:, WO:WA]), ALU.subtract).then_inc(wo_split_lo, 1)
            for g in range(1, NG):
                ln_root(g)
                if g == 1:
                    pool.wait_ge(ln_rs, 2)
                    for b, (lo, hi) in enumerate(SB):
                        pool.wait_ge(y_split_hi, 2 * b + 2)
                        wait(pool, ye_low, b)
                        nc.gpsimd.tensor_tensor(yk[0:DR, YE, lo:hi], y_raw[0:DR, 1, lo:hi], f(yk[0:DR, YB, lo:hi]),
                                                ALU.subtract).then_inc(ye_low, 1)
                    pool.wait_ge(ye_low, len(SB))

            def attention_rstd(t):
                pool.wait_ge(o_var, t + 1)
                nc.gpsimd.tensor_tensor(rstd[:, bass.ds(t, 1)], var[:, bass.ds(t, 1)], half[:], ALU.pow).then_inc(o_rs, 1)

            def split_z(t):
                nc.gpsimd.tensor_copy(z32[:, A:B + 1, :].rearrange("p s n -> p (s n)"), state[:, bass.ds(t * D, D)]).then_inc(zs_32, 1)
                nc.gpsimd.tensor_copy(z32[:, E, :], z_e[:, bass.ds(t * P, P)]).then_inc(zs_32, 1)
                pool.wait_ge(zs_32, 2 * t + 2)
                pool.wait_ge(zs_hi, 2 * t + 2)
                nc.gpsimd.tensor_tensor(zt[:, A_LO, :], z32[:, A, :], f(zt[:, A, :]), ALU.subtract).then_inc(zs_lo, 1)
                pool.wait_ge(zs_lo, 3 * t + 1)
                nc.gpsimd.tensor_tensor(zt[DR:P, B, :], z32[DR:P, B, :], f(zt[DR:P, B, :]), ALU.subtract).then_inc(zs_lo, 1)
                pool.wait_ge(zs_lo, 3 * t + 2)
                row = slice(ONE_LO, ONE_LO + 1)
                nc.gpsimd.tensor_tensor(zt[row, E, :], z32[row, E, :], f(zt[row, E, :]), ALU.subtract).then_inc(zs_lo, 1)
                pool.wait_ge(zs_lo, 3 * t + 3)

            pool.wait_ge(z_act, 3)
            split_z(0)
            pool.wait_ge(ld_small, 96)
            by_half = wr[:].rearrange("p u c h e -> p h (u c) e")
            raw = wr_raw[:].rearrange("p (n e) -> p n e", e=NE)
            nc.gpsimd.tensor_copy(by_half[:, 0], raw).then_inc(wh_done, 1)
            nc.gpsimd.tensor_copy(bd_hi[:], bd_raw[:]).then_inc(wh_done, 1)
            pool.wait_ge(wh_done, 2)
            nc.gpsimd.tensor_tensor(by_half[:, 1], raw, f(wr[:]).rearrange("p u c h e -> p h (u c) e")[:, 0],
                                    ALU.subtract).then_inc(const, 1)
            nc.gpsimd.tensor_copy(bd[0:W_HI2, :], f(bd_hi[0:W_HI2, :])).then_inc(const, 1)
            pool.wait_ge(const, 5)
            nc.gpsimd.tensor_tensor(bd[W_HI2:P, :], bd_raw[W_HI2:P, :], f(bd_hi[W_HI2:P, :]), ALU.subtract).then_inc(const, 1)
            pool.wait_ge(const, 6)
            split_z(1)
            split_z(2)
            pool.wait_ge(z_dve, 3)
            with pool.Fori(1, TILES - 2) as t:
                attention_rstd(t - 1)
                split_z(t + 2)
            for t in range(TILES - 3, TILES):
                attention_rstd(t)

            def norm_root(u):
                pool.wait_ge(ms_dve, u + 1)
                nc.gpsimd.tensor_tensor(root[:], msum[:], half[:].broadcast_to([P, TG]), ALU.pow).then_inc(ms_pool, 1)

            def fetch_input(u):
                wait(pool, xT_mm, C * u)
                wait(pool, y_norm, TG * (u - 1))
                nc.gpsimd.tensor_copy(x_in[:], state[:, bass.ds((u % NG) * TG * D, TG * D)]).then_inc(x_fetch, 1)

            pool.wait_ge(o_n, TILES)
            fetch_input(1)
            with pool.Fori(1, GROUPS - 1) as u:
                norm_root(u - 1)
                fetch_input(u + 1)
            norm_root(GROUPS - 2)
            norm_root(GROUPS - 1)

        @block.scalar
        def _(act):
            for n, part in enumerate((slice(WQ, WK), slice(WK, WV), slice(WV, WO), slice(WO, WA))):
                act.wait_ge((ld_wq, ld_wk, ld_wvo, ld_wvo)[n], 16)
                nc.scalar.copy(wa_hi[:, part], wa_raw[:, part]).then_inc(wa_split_hi, 1)
            for m in range(C):
                act.wait_ge(wqk_mm, m + 1)
                nc.scalar.copy(wqk_hi[:, m, :], ps[:, bank_of("wqk", m), 0:3 * P]).then_inc(wqk_act, 1)

            def ln_high(g):
                for c in range(C):
                    act.wait_ge(lnT_mm, C * g + c + 1)
                    nc.scalar.copy(ln_hi[:, g % 2, c, :], ps[:, bank_of("T", g, c), :]).then_inc(lnT_act, 1)

            def z_out(g):
                for part in (A, B, E):
                    act.wait_ge(z_mm, 3 * g + part + 1)
                    dst, source = z_place(g, part)
                    nc.scalar.activation(dst, source, ACT.Identity, bias=zbias[:, part:part + 1]).then_inc(z_act, 1)

            def y_high(b):
                lo, hi = SB[b]
                act.wait_ge(ld_y[b], 16)
                nc.scalar.copy(yk[:, Y, lo:hi], y_raw[:, 0, lo:hi]).then_inc(y_split_hi, 1)
                nc.scalar.copy(yk[:, YB, lo:hi], y_raw[:, 1, lo:hi]).then_inc(y_split_hi, 1)

            def z_high(t):
                wait(act, s_mm, 4 * t)
                wait(act, zs_lo, 3 * t)
                nc.scalar.copy(zt[:, A:B + 1, :].rearrange("p s n -> p (s n)"), state[:, bass.ds(t * D, D)]).then_inc(zs_hi, 1)
                nc.scalar.copy(zt[:, E, :], z_e[:, bass.ds(t * P, P)]).then_inc(zs_hi, 1)

            def v_high(blocks):
                for b in blocks:
                    r = KROWS[b]
                    act.wait_ge(v_mm, b + 1)
                    nc.scalar.copy(v_hi[0:r, b, :], ps[0:r, bank_of("V", b), 0:D]).then_inc(v_act, 1)

            act.wait_ge(zeroed, 2)
            y_high(0)
            y_high(1)
            ln_high(0)
            y_high(2)
            y_high(3)
            for part in (A, B):
                act.wait_ge(wvo_mm, part + 1)
                nc.scalar.copy(wvo[:, part, :], ps[:, bank_of("wvo", part), 0:D]).then_inc(wvo_act, 1)
            ln_high(1)
            act.wait_ge(zb_dve, 1)
            z_out(0)
            act.wait_ge(z_act, 3)
            z_high(0)
            z_out(1)
            ln_high(2)
            v_high(V_BLOCKS[0])
            z_out(2)
            ln_high(3)
            act.wait_ge(ld_rows, 16)
            nc.scalar.activation(tanh_g[:], rowp[:, R_G:R_G + 2], ACT.Tanh).then_inc(tg_done, 1)
            v_high(V_BLOCKS[1])

            def exponent(t):
                act.wait_ge(s_neg, t + 1)
                wait(act, t_mm, 4 * t)
                nc.scalar.activation(prob[:, 0:3 * SW].rearrange("p (b n) -> p b n", b=3), ps[:, 0:3, 0:SW], ACT.Exp,
                                     bias=negm[:, 0:1], scale=SCALE, accum_out=rsum[:, bass.ds(t, 1)]).then_inc(s_exp, 1)
                nc.scalar.activation(prob[:, 3 * SW:KEYS], ps[:, 3, 0:KEYS - 3 * SW], ACT.Exp,
                                     bias=negm[:, 0:1], scale=SCALE, accum_out=rsum2[:, bass.ds(t, 1)]).then_inc(s_exp, 1)

            def high_halves(t):
                for i, grp in enumerate(TGRP):
                    act.wait_ge(t_mm, 4 * t + i + 1)
                    n, k0 = len(grp) * P, grp[0] * P
                    rows = KROWS[grp[0]]
                    nc.scalar.copy(pT_hi[0:rows, k0:k0 + n], ps[0:rows, TBANK[i % 2], 0:n]).then_inc(t_act, 1)

            def weights_high(t):
                act.wait_ge(ld_w, 16 * (t + 1))
                nc.scalar.copy(w_hi[:, bass.ds(t * WCHUNK, WCHUNK)], stage[:]).then_inc(wh_act, 1)

            act.wait_ge(v_dve, KB)
            act.wait_ge(const, 6)
            z_high(1)
            exponent(0)
            high_halves(0)
            weights_high(0)
            z_high(2)
            exponent(1)
            act.wait_ge(z_dve, 3)
            with act.Fori(1, TILES - 2) as t:
                high_halves(t)
                weights_high(t)
                z_high(t + 2)
                exponent(t + 1)
            high_halves(TILES - 2)
            weights_high(TILES - 2)
            exponent(TILES - 1)
            high_halves(TILES - 1)
            weights_high(TILES - 1)

            def input_high(u, banks=XB):
                wait(act, u_mm, 2 * UNITS * u)
                for c in range(C):
                    act.wait_ge(xT_mm, C * u + c + 1)
                    nc.scalar.copy(xs_hi[:, c, :], ps[:, banks[c], :]).then_inc(xs_act, 1)

            input_high(0, GB)

            def after_up(u, k):
                for c in range(C):
                    n = 2 * UNITS * u + 2 * k + c
                    act.wait_ge(u_mm, n + 1)
                    wait(act, a_mul, n + 1 - 4)
                    wait(act, g_mm, 2 * UNITS * u + 2 * (k - 2) + 2)
                    bias = colp[:, BU + 2 * k + c:BU + 2 * k + c + 1]
                    nc.scalar.activation(h32[:, k % 2, c, :], ps[:, HB[c], :], ACT.Identity, bias=bias).then_inc(u_act, 1)
                    nc.scalar.activation(h_hi[:, k % 2, c, :], ps[:, HB[c], :], ACT.Identity, bias=bias).then_inc(u_act, 1)

            def after_gate(u, k):
                for c in range(C):
                    n = 2 * UNITS * u + 2 * k + c
                    act.wait_ge(g_mm, n + 1)
                    wait(act, a_mul, n + 1 - 2)
                    nc.scalar.activation(sg[:, c, :], ps[:, GB[c], :], ACT.Silu,
                                         bias=colp[:, BG + 2 * k + c:BG + 2 * k + c + 1]).then_inc(g_act, 1)

            def squares(u):
                for i in range(TG):
                    if i % 2 == 0:
                        act.wait_ge(y_dve, 2 * (UNITS - 1) * (u + 1) - 1 + i // 2)
                    nc.scalar.activation(sq[:, i, :], acc[:, i, :], ACT.Square, accum_out=sums[:, i:i + 1]).then_inc(sq_act, 1)

            def group(u, first=False, last=False):
                for k in range(UNITS):
                    if k == UNITS - 2 and not last:
                        input_high(u + 1)
                    if k < UNITS - 1:
                        after_up(u, k + 1)
                    elif not last:
                        after_up(u + 1, 0)
                    after_gate(u, k)
                    if k == 0:
                        act.wait_ge(r_tanh, 2 * u + 1)
                        nc.scalar.activation(rt_w[:], rt_w[:], ACT.Tanh, scale=0.5).then_inc(r_tanh, 1)
                    if k == 1:
                        act.wait_ge(wT_mm, u + 1)
                        wait(act, d_mm, 2 * (UNITS - 1) * u)
                        nc.scalar.copy(wT[:], ps[:, RB, :]).then_inc(wT_act, 1)
                    if k == 1 and not first:
                        squares(u - 1)

            act.wait_ge(o_mm, TILES)
            act.wait_ge(w_done, TILES)
            after_up(0, 0)
            group(0, first=True)
            with act.Fori(1, GROUPS - 1) as u:
                group(u)
            group(GROUPS - 1, last=True)
            squares(GROUPS - 1)

        @block.vector
        def _(dve):
            dve.wait_ge(const, 3)
            dve.wait_ge(zeroed, 5)
            for column in (TWO_HI, TWO_LO):
                nc.vector.tensor_scalar(wp[:, :, column:column + 1], wp[:, :, column:column + 1], 2.0, None, ALU.add).then_inc(twos, 1)

            def weights_low_att(parts):
                for n, part in parts:
                    dve.wait_ge(wa_split_hi, n + 1)
                    nc.vector.tensor_tensor(wa_lo[:, part], wa_raw[:, part], f(wa_hi[:, part]), ALU.subtract).then_inc(wa_split_lo, 1)

            weights_low_att(((0, slice(WQ, WK)), (1, slice(WK, WV))))

            def stats(g):
                dve.wait_ge(ld_x[g], 16)
                for t in range(TG * g, TG * g + TG):
                    nc.vector.bn_stats(bn6[:, t, :], x2[:, t, :]).then_inc(ln_st, 1)
                dve.wait_ge(ln_st, TG * (g + 1))
                for t in range(TG * g, TG * g + TG):
                    nc.vector.bn_aggr(mv[:, t, :], bn6[:, t, :]).then_inc(ln_ag, 1)
                dve.wait_ge(ln_ag, TG * (g + 1))
                nc.vector.tensor_scalar(var[:, TG * g:TG * g + TG], mv[:, TG * g:TG * g + TG, 1], LN_EPS, None,
                                        ALU.add).then_inc(ln_var, 1)

            def normalize(g):
                dve.wait_ge(ln_rs, g + 1)
                wait(dve, lnT_mm, C * g)
                for i in range(TG):
                    t = TG * g + i
                    nc.vector.tensor_scalar(ln_xn[:, i, :], x2[:, t, :], mv[:, t, 0:1], rstd[:, t:t + 1],
                                            ALU.subtract, ALU.mult).then_inc(ln_done, 1)

            def ln_low(g):
                for c in range(C):
                    dve.wait_ge(lnT_act, C * g + c + 1)
                    nc.vector.tensor_tensor(ln_lo[:, g % 2, c, :], ps[:, bank_of("T", g, c), :], f(ln_hi[:, g % 2, c, :]),
                                            ALU.subtract).then_inc(lnT_dve, 1)

            dve.wait_ge(ld_cols, 16)
            bq = colp[:, BQ:BQ + C].unsqueeze(2)
            nc.vector.tensor_copy(bq2[:, :, 0:1], bq).then_inc(bq_hi, 1)
            dve.wait_ge(bq_hi, 1)
            nc.vector.tensor_tensor(bq2[:, :, 1:2], bq, f(bq2[:, :, 0:1]), ALU.subtract).then_inc(bq_lo, 1)
            stats(0)
            for m in range(C):
                dve.wait_ge(wqk_act, m + 1)
                nc.vector.tensor_tensor(wqk_lo[:, m, :], ps[:, bank_of("wqk", m), 0:3 * P], f(wqk_hi[:, m, :]),
                                        ALU.subtract).then_inc(wqk_dve, 1)
                if m == 0:
                    normalize(0)
            dve.wait_ge(zb_mm, 1)
            nc.vector.tensor_reduce(zbias[:], ps[:, bank_of("zb", 0), 0:6].rearrange("p (s n) -> p s n", n=2), AX.X,
                                    ALU.add).then_inc(zb_dve, 1)
            weights_low_att(((2, slice(WV, WO)),))
            stats(1)
            ln_low(0)

            def y_low(b):
                lo, hi = SB[b]
                dve.wait_ge(y_split_hi, 2 * b + 1)
                nc.vector.tensor_tensor(yk[:, Y_LO, lo:hi], y_raw[:, 0, lo:hi], f(yk[:, Y, lo:hi]),
                                        ALU.subtract).then_inc(y_split_lo, 1)

            normalize(1)
            y_low(0)
            dve.wait_ge(wvo_act, 1)
            nc.vector.tensor_tensor(wvo[:, A_LO, :], ps[:, bank_of("wvo", A), 0:D], f(wvo[:, A, :]), ALU.subtract).then_inc(wvo_dve, 1)
            dve.wait_ge(wvo_act, 2)
            nc.vector.tensor_tensor(wvo[DR:P, B, :], ps[DR:P, bank_of("wvo", B), 0:D], f(wvo[DR:P, B, :]),
                                    ALU.subtract).then_inc(wvo_dve, 1)
            dve.wait_ge(wvo_mm, 3)
            dve.wait_ge(ld_bo, 16)
            nc.vector.tensor_tensor(vo[:], ps[:, bank_of("wvo", E), 0:D], bo_rows[:], ALU.add).then_inc(wvo_sum, 1)
            dve.wait_ge(wvo_sum, 1)
            nc.vector.tensor_copy(wvo[:, E, :], vo[:]).then_inc(wvo_e, 1)
            dve.wait_ge(wvo_e, 1)
            row = slice(ONE_LO, ONE_LO + 1)
            nc.vector.tensor_tensor(wvo[row, E, :], vo[row, :], f(wvo[row, E, :]), ALU.subtract).then_inc(wvo_dve, 1)
            ln_low(1)
            stats(2)
            normalize(2)
            for b in range(1, len(SB)):
                y_low(b)
            stats(3)
            def v_low(blocks):
                for b in blocks:
                    r = KROWS[b]
                    dve.wait_ge(v_act, b + 1)
                    nc.vector.tensor_tensor(v_lo[0:r, b, :], ps[0:r, bank_of("V", b), 0:D], f(v_hi[0:r, b, :]),
                                            ALU.subtract).then_inc(v_dve, 1)

            ln_low(2)
            normalize(3)
            v_low(V_BLOCKS[0])
            ln_low(3)
            v_low(V_BLOCKS[1])

            def weights_low(t):
                part = bass.ds(t * WCHUNK, WCHUNK)
                dve.wait_ge(wh_act, t + 1)
                nc.vector.tensor_tensor(w_lo[:, part], stage[:], f(w_hi[:, part]), ALU.subtract).then_inc(w_done, 1)

            def bank_max(t, b):
                lo, hi = SB[b]
                dve.wait_ge(s_mm, 4 * t + b + 1)
                nc.vector.tensor_reduce(bmax[:, b:b + 1], ps[:, SCORE[b], 0:min(hi, KEYS) - lo], AX.X,
                                        ALU.max).then_inc(s_max, 1)

            def neg_max(t):
                dve.wait_ge(s_max, 4 * t + 4)
                nc.vector.tensor_reduce(bmax[:, 0:1], bmax[:, 0:4], AX.X, ALU.max).then_inc(s_max4, 1)
                dve.wait_ge(s_max4, t + 1)
                nc.vector.tensor_scalar(negm[:], bmax[:, 0:1], -SCALE, None, ALU.mult).then_inc(s_neg, 1)

            def low_half(t, i):
                grp = TGRP[i]
                n, k0, rows = len(grp) * P, grp[0] * P, KROWS[grp[0]]
                dve.wait_ge(t_act, 4 * t + i + 1)
                nc.vector.tensor_tensor(pT_lo[0:rows, k0:k0 + n], ps[0:rows, TBANK[i % 2], 0:n],
                                        f(pT_hi[0:rows, k0:k0 + n]), ALU.subtract).then_inc(t_dve, 1)

            def residual(t):
                one = bass.ds(t, 1)
                dve.wait_ge(s_exp, 2 * t + 2)
                nc.vector.tensor_tensor(rsum[:, one], rsum[:, one], rsum2[:, one], ALU.add).then_inc(o_sum, 1)
                dve.wait_ge(o_sum, t + 1)
                nc.vector.reciprocal(rinv[:, one], rsum[:, one]).then_inc(o_inv, 1)
                dve.wait_ge(o_inv, t + 1)
                nc.vector.tensor_tensor(rinv[:, one], rinv[:, one], tanh_g[:, 0:1], ALU.mult).then_inc(o_sc, 1)
                dve.wait_ge(o_sc, t + 1)
                dve.wait_ge(o_mm, t + 1)
                row = x2[:, one, :].rearrange("p a n -> p (a n)")
                nc.vector.scalar_tensor_tensor(out=o_row[:], in0=ps[:, OBANK, 0:D], scalar=rinv[:, one], in1=row,
                                               op0=ALU.mult, op1=ALU.add).then_inc(o_x2, 1)
                dve.wait_ge(o_x2, t + 1)
                nc.vector.bn_stats(bn6[:, 0, :], o_row[:]).then_inc(o_bn, 1)

            def residual_end(t):
                one = bass.ds(t, 1)
                row = x2[:, one, :].rearrange("p a n -> p (a n)")
                dve.wait_ge(o_bn, t + 1)
                nc.vector.tensor_scalar(row, o_row[:], 1.0, None, ALU.mult).then_inc(o_keep, 1)
                nc.vector.bn_aggr(mv[:, 0, :], bn6[:, 0, :]).then_inc(o_ag, 1)
                dve.wait_ge(o_ag, t + 1)
                nc.vector.tensor_scalar(var[:, one], mv[:, 0, 1:2], LN_EPS, None, ALU.add).then_inc(o_var, 1)

            def normed(t):
                one = bass.ds(t, 1)
                dve.wait_ge(o_rs, t + 1)
                nc.vector.tensor_scalar(state[:, bass.ds(t * D, D)], o_row[:], mv[:, 0, 0:1],
                                        rstd[:, one], ALU.subtract, ALU.mult).then_inc(o_n, 1)

            dve.wait_ge(tg_done, 1)
            for b in range(4):
                bank_max(0, b)
            neg_max(0)
            for part in (A, B, E):
                dve.wait_ge(z_mm, 3 * (NG - 1) + part + 1)
                dst, source = z_place(NG - 1, part)
                nc.vector.tensor_scalar(dst, source, zbias[:, part:part + 1], None, ALU.add).then_inc(z_dve, 1)

            def attention_tile(t, first=False, last=False):
                if not (first or last):
                    residual(t - 1)
                low_half(t, 0)
                low_half(t, 1)
                if not (first or last):
                    residual_end(t - 1)
                if last:
                    residual(t - 1)
                    residual_end(t - 1)
                if not last:
                    bank_max(t + 1, 0)
                    bank_max(t + 1, 1)
                low_half(t, 2)
                low_half(t, 3)
                if not last:
                    bank_max(t + 1, 2)
                    bank_max(t + 1, 3)
                    neg_max(t + 1)
                if not first:
                    normed(t - 1)
                weights_low(t)

            attention_tile(0, first=True)
            with dve.Fori(1, TILES - 1) as t:
                attention_tile(t)
            attention_tile(TILES - 1, last=True)

            def input_low(u, banks=XB):
                for c in range(C):
                    dve.wait_ge(xs_act, C * u + c + 1)
                    nc.vector.tensor_tensor(xs_lo[:, c, :], ps[:, banks[c], :], f(xs_hi[:, c, :]), ALU.subtract).then_inc(xs_dve, 1)

            input_low(0, GB)
            residual(TILES - 1)
            residual_end(TILES - 1)
            normed(TILES - 1)

            def h_low(u, k):
                for c in range(C):
                    n = 2 * UNITS * u + 2 * k + c
                    dve.wait_ge(u_act, 2 * n + 2)
                    nc.vector.tensor_tensor(h_lo[:, k % 2, c, :], h32[:, k % 2, c, :], f(h_hi[:, k % 2, c, :]),
                                            ALU.subtract).then_inc(u_dve, 1)

            def activated(u, k):
                for c in range(C):
                    n = 2 * UNITS * u + 2 * k + c
                    m = 2 * (UNITS - 1) * u + 2 * (k - 1) + c
                    dve.wait_ge(g_act, n + 1)
                    if k == 0:
                        nc.vector.tensor_tensor(as0[:, c, :], sg[:, c, :], h32[:, 0, c, :], ALU.mult).then_inc(a_mul, 1)
                        continue
                    nc.vector.tensor_tensor(aa[:, c, :], sg[:, c, :], h32[:, k % 2, c, :], ALU.mult).then_inc(a_mul, 1)
                    dve.wait_ge(a_mul, n + 1)
                    if k == 1:
                        nc.vector.tensor_tensor(aa[:, c, :], aa[:, c, :], as0[:, c, :], ALU.add).then_inc(a_fin, 1)
                        dve.wait_ge(a_fin, C * u + c + 1)
                    wait(dve, d_mm, 2 * (UNITS - 1) * u + 2 * (k - 2 if k > 2 else 0))
                    nc.vector.tensor_copy(a_hi[:, k % 2, c, :], aa[:, c, :]).then_inc(a_split_hi, 1)
                    dve.wait_ge(a_split_hi, m + 1)
                    nc.vector.tensor_tensor(a_lo[:, k % 2, c, :], aa[:, c, :], f(a_hi[:, k % 2, c, :]),
                                            ALU.subtract).then_inc(a_split_lo, 1)

            CHAIN = 13

            def route_a(u):
                step = [0]

                def link(instruction):
                    step[0] += 1
                    instruction.then_inc(r_chain, 1)
                    dve.wait_ge(r_chain, CHAIN * u + step[0])

                def per_tile(row):
                    return rowp[:, bass.ds(row + (u // NG) * NE, NE)].unsqueeze(1).broadcast_to([P, TG, NE])

                dve.wait_ge(r_mm, u + 1)
                gates = ps[:, RB, 0:TG * P].rearrange("p (t n) -> p t n", t=TG)
                link(nc.vector.tensor_tensor(rt_g[:], gates[:, :, 0:NE], per_tile(R_RB), ALU.add))
                link(nc.vector.tensor_tensor(rt_g[:], gates[:, :, NE:2 * NE], rt_g[:], ALU.add))
                link(nc.vector.tensor_tensor(rt_b[:], rt_g[:], per_tile(R_GB), ALU.add))
                mine = rt_b[:].unsqueeze(3).broadcast_to([P, TG, NE, NE])
                other = rt_b[:].unsqueeze(2).broadcast_to([P, TG, NE, NE])
                nc.vector.tensor_tensor(rt_gt[:], other, mine, ALU.is_gt).then_inc(r_dve, 1)
                link(nc.vector.tensor_tensor(rt_eq[:], other, mine, ALU.is_equal))
                link(nc.vector.tensor_tensor(rt_eq[:], rt_eq[:], tri[:].unsqueeze(1).broadcast_to([P, TG, NE, NE]), ALU.mult))
                dve.wait_ge(r_dve, 2 * u + 1)
                link(nc.vector.tensor_tensor(rt_gt[:], rt_gt[:], rt_eq[:], ALU.add))
                link(nc.vector.tensor_reduce(rt_c[:], rt_gt[:], AX.X, ALU.add))
                link(nc.vector.tensor_scalar(rt_c[:], rt_c[:], 2.0, None, ALU.is_lt))
                link(nc.vector.tensor_tensor(rt_w[:], rt_g[:], rt_c[:], ALU.mult))
                link(nc.vector.tensor_reduce(rt_s[:], rt_w[:], AX.X, ALU.add))
                link(nc.vector.tensor_scalar(rt_w[:], rt_g[:], 2.0, None, ALU.mult))
                nc.vector.tensor_tensor(rt_w[:], rt_w[:], rt_s[:].unsqueeze(2).broadcast_to([P, TG, NE]),
                                        ALU.subtract).then_inc(r_tanh, 1)

            def route_b(u):
                dve.wait_ge(r_tanh, 2 * u + 2)
                nc.vector.tensor_scalar(rt_w[:], rt_w[:], 0.5, 0.5, ALU.mult, ALU.add).then_inc(r_chain, 1)
                dve.wait_ge(r_chain, CHAIN * u + CHAIN - 1)
                wait(dve, y_dve, 2 * (UNITS - 1) * u)
                nc.vector.tensor_tensor(rt_wf[:], rt_w[:], rt_c[:], ALU.mult).then_inc(r_chain, 1)
                dve.wait_ge(r_chain, CHAIN * u + CHAIN)
                nc.vector.tensor_copy(rt_h[:], rt_wf[:]).then_inc(r_dve, 1)
                dve.wait_ge(r_dve, 2 * u + 2)
                nc.vector.tensor_copy(wp[:, :, W_HI:W_HI + NE], f(rt_h[:])).then_inc(r_ready, 1)
                nc.vector.tensor_copy(wp[:, :, W_HI2:W_HI2 + NE], f(rt_h[:])).then_inc(r_ready, 1)
                nc.vector.tensor_tensor(wp[:, :, W_LO:W_LO + NE], rt_wf[:], f(rt_h[:]), ALU.subtract).then_inc(r_ready, 1)

            def accumulate(u, k, banks=DB):
                n = (UNITS - 1) * u + k - 1
                if k == 1:
                    wait(dve, y_norm, TG * u)
                for b in range(2):
                    dve.wait_ge(d_mm, 2 * n + b + 1)
                    if k == 1:
                        rows = acc[:, 2 * b:2 * b + 2, :].rearrange("p t d -> p (t d)")
                        nc.vector.tensor_tensor(rows, ps[:, DB[b], :], state[:, bass.ds(((u % NG) * TG + 2 * b) * D, 2 * D)],
                                                ALU.add).then_inc(y_dve, 1)
                        continue
                    dve.wait_ge(y_dve, 2 * (n - 1) + b + 1)
                    for i in (2 * b, 2 * b + 1):
                        m = nc.vector.scalar_tensor_tensor(out=acc[:, i, :], in0=ps[:, banks[b], (i % 2) * D:(i % 2) * D + D],
                                                           scalar=rt_wf[:, i, k - 2:k - 1], in1=acc[:, i, :],
                                                           op0=ALU.mult, op1=ALU.add)
                    m.then_inc(y_dve, 1)

            def mean_square(u):
                dve.wait_ge(sq_act, TG * (u + 1))
                nc.vector.tensor_scalar(msum[:], sums[:], 1.0 / D, RMS_EPS, ALU.mult, ALU.add).then_inc(ms_dve, 1)

            def rms(u):
                dve.wait_ge(ms_pool, u + 1)
                for i in range(TG):
                    nc.vector.scalar_tensor_tensor(out=state[:, bass.ds(((u % NG) * TG + i) * D, D)], in0=acc[:, i, :],
                                                   scalar=root[:, i:i + 1], in1=w_rows[:, bass.ds((u // NG) * D, D)],
                                                   op0=ALU.mult, op1=ALU.mult).then_inc(y_norm, 1)

            def out_group(g):
                dve.wait_ge(y_norm, TG * (NG + g + 1))
                rows = x2[:, TG * g:TG * g + TG, :].rearrange("p t d -> p (t d)")
                nc.vector.scalar_tensor_tensor(out=rows, in0=state[:, TG * D * g:TG * D * (g + 1)], scalar=tanh_g[:, 1:2],
                                               in1=rows, op0=ALU.mult, op1=ALU.add).then_inc(f_dve, 1)

            def group(u, first=False, last=False):
                for k in range(UNITS):
                    if k == 0:
                        route_a(u)
                    if k == UNITS - 2 and not last:
                        input_low(u + 1)
                    if k < UNITS - 1:
                        h_low(u, k + 1)
                    elif not last:
                        h_low(u + 1, 0)
                    if k == 2 and not first:
                        mean_square(u - 1)
                    activated(u, k)
                    if k == 0 and not first:
                        accumulate(u - 1, UNITS - 1)
                    if k == 0:
                        route_b(u)
                    if k == 2 and not first:
                        rms(u - 1)
                    if k >= 2:
                        accumulate(u, k - 1)
                    if last and 3 <= k < 3 + NG - 1:
                        out_group(k - 3)

            dve.wait_ge(o_mm, TILES)
            dve.wait_ge(w_done, TILES)
            h_low(0, 0)
            dve.wait_ge(twos, 2)
            group(0, first=True)
            dve.wait_ge(ld_row, 16)
            with dve.Fori(1, GROUPS - 1) as u:
                group(u)
            group(GROUPS - 1, last=True)
            accumulate(GROUPS - 1, UNITS - 1, XB)
            dve.wait_ge(y_dve, 2 * (UNITS - 1) * GROUPS)
            for b in range(2):
                if b:
                    mean_square(GROUPS - 1)
                nc.vector.tensor_tensor(aa[:, b, :].rearrange("p (t d) -> p t d", d=D), acc[:, 2 * b:2 * b + 2, :],
                                        w_rows[:, (ROUNDS - 1) * D:ROUNDS * D].unsqueeze(1).broadcast_to([P, 2, D]),
                                        ALU.mult).then_inc(e_w, 1)
            dve.wait_ge(ms_pool, GROUPS)
            nc.vector.tensor_scalar(root[:], root[:], tanh_g[:, 1:2], None, ALU.mult).then_inc(e_scale, 1)
            dve.wait_ge(e_scale, 1)
            dve.wait_ge(e_w, 2)
            for i in range(TG):
                row = x2[:, TILES - TG + i, :]
                m = nc.vector.scalar_tensor_tensor(out=row, in0=aa[:, i // 2, (i % 2) * D:(i % 2) * D + D],
                                                   scalar=root[:, i:i + 1], in1=row, op0=ALU.mult, op1=ALU.add)
                if i % 2:
                    m.then_inc(f_dve, 1)

        @block.tensor
        def _(pe):
            def product(dst, terms):
                last = None
                n = 3 * len(terms)
                i = 0
                for wh, wl, xh, xl in terms:
                    for w, v in ((wh, xh), (wh, xl), (wl, xh)):
                        last = nc.tensor.matmul(dst, w, v, start=(i == 0), stop=(i == n - 1))
                        i += 1
                return last

            def halves(start, n):
                return wa_hi[:, start:start + n], wa_lo[:, start:start + n]

            pe.wait_ge(wa_split_lo, 2)
            for m in range(C):
                product(ps[:, bank_of("wqk", m), 0:3 * P],
                        [halves(WQ + c * D + m * P, P) + halves(WK + c * 3 * P, 3 * P) for c in range(C)]).then_inc(wqk_mm, 1)
            pe.wait_ge(bq_lo, 1)
            for part in (A, B, E):
                for c in range(C):
                    for n, w in enumerate(halves(WK + c * 3 * P + part * P, P)):
                        m = nc.tensor.matmul(ps[:, bank_of("zb", 0), 2 * part:2 * part + 2], w, bq2[:, c, :],
                                             start=(c == 0 and n == 0), stop=(c == C - 1 and n == 1))
            m.then_inc(zb_mm, 1)
            pe.wait_ge(const, 3)
            def x_transposes(g):
                pe.wait_ge(ln_done, TG * (g + 1))
                for c in range(C):
                    bank_free(pe, "T", g, c)
                    for i in range(TG):
                        m = nc.tensor.transpose(ps[:, bank_of("T", g, c), i * P:i * P + P], ln_xn[:, i, c * P:c * P + P], ident[:])
                    m.then_inc(lnT_mm, 1)

            x_transposes(0)
            pe.wait_ge(wa_split_lo, 3)
            pe.wait_ge(wo_split_lo, 1)
            for part in (A, B, E):
                bank_free(pe, "wvo", part)
                product(ps[:, bank_of("wvo", part), 0:D],
                        [halves(WV + c * 3 * P + part * P, P) + halves(WO + c * D, D) for c in range(C)]).then_inc(wvo_mm, 1)
            x_transposes(1)
            pe.wait_ge(wqk_dve, C)

            def make_z(g):
                pe.wait_ge(lnT_dve, C * (g + 1))
                for part in (A, B, E):
                    if g < NG - 1:
                        bank_free(pe, "z", g, part)
                    columns = slice(part * P, part * P + P)
                    product(ps[:, bank_of("z", g, part), :],
                            [(wqk_hi[:, c, columns], wqk_lo[:, c, columns], ln_hi[:, g % 2, c, :], ln_lo[:, g % 2, c, :])
                             for c in range(C)]).then_inc(z_mm, 1)

            def make_v(blocks):
                for b in blocks:
                    r = KROWS[b]
                    bank_free(pe, "V", b)
                    for n, (left, right) in enumerate(PASSES):
                        m = nc.tensor.matmul(ps[0:r, bank_of("V", b), 0:D], yk[:, right, b * P:b * P + r], wvo[:, left, :],
                                             start=(n == 0), stop=(n == len(PASSES) - 1))
                    m.then_inc(v_mm, 1)

            make_z(0)
            make_z(1)
            x_transposes(2)
            pe.wait_ge(y_split_lo, len(SB))
            pe.wait_ge(ye_low, len(SB))
            pe.wait_ge(y_ones, 1)
            pe.wait_ge(wvo_dve, 3)
            make_v(V_BLOCKS[0])
            make_z(2)
            x_transposes(3)
            make_v(V_BLOCKS[1])

            def scores(t, b):
                lo, hi = SB[b]
                if b == 0:
                    pe.wait_ge(zs_lo, 3 * (t + 1))
                    wait(pe, s_exp, 2 * t)
                for n, (left, right) in enumerate(PASSES):
                    m = nc.tensor.matmul(ps[:, SCORE[b], 0:hi - lo], zt[:, left, :], yk[:, right, lo:hi],
                                         start=(n == 0), stop=(n == len(PASSES) - 1))
                m.then_inc(s_mm, 1)

            def transposes(t, i):
                if i in (0, 2):
                    assert TGRP[1][-1] * P + P <= 3 * SW
                    pe.wait_ge(s_exp, 2 * t + 1 + i // 2)
                wait(pe, t_dve, 4 * t + i - 1)
                for n, kb in enumerate(TGRP[i]):
                    r = KROWS[kb]
                    m = nc.tensor.transpose(ps[0:r, TBANK[i % 2], n * P:n * P + P], prob[:, kb * P:kb * P + r], ident[:])
                m.then_inc(t_mm, 1)

            def values(t):
                wait(pe, o_x2, t)
                for i, grp in enumerate(TGRP):
                    pe.wait_ge(t_dve, 4 * t + i + 1)
                    for kb in grp:
                        r = KROWS[kb]
                        ph, pl = pT_hi[0:r, kb * P:kb * P + P], pT_lo[0:r, kb * P:kb * P + P]
                        for n, (p, v) in enumerate(((ph, v_hi), (ph, v_lo), (pl, v_hi))):
                            m = nc.tensor.matmul(ps[:, OBANK, 0:D], p, v[0:r, kb, :], start=(kb == 0 and n == 0),
                                                 stop=(kb == KB - 1 and n == 2))
                m.then_inc(o_mm, 1)

            def input_transposes(u, banks=XB):
                wait(pe, x_fetch, u)
                source = state if isinstance(u, int) and u == 0 else x_in
                for c in range(C):
                    for i in range(TG):
                        m = nc.tensor.transpose(ps[:, banks[c], i * P:i * P + P], source[:, i * D + c * P:i * D + c * P + P], ident[:])
                    m.then_inc(xT_mm, 1)

            def attention_tile(t, first=False, last=False):
                transposes(t, 0)
                if first:
                    pe.wait_ge(z_dve, 3)
                transposes(t, 1)
                if not last:
                    scores(t + 1, 0)
                    scores(t + 1, 1)
                if last:
                    pe.wait_ge(o_n, TG)
                    pe.wait_ge(s_exp, 2 * TILES)
                    input_transposes(0, GB)
                transposes(t, 2)
                transposes(t, 3)
                if not last:
                    scores(t + 1, 2)
                    scores(t + 1, 3)
                values(t)

            pe.wait_ge(z_act, 3 * (NG - 1))
            pe.wait_ge(lnT_dve, C * NG)
            for b in range(4):
                assert bank_of("V", KB - 4 + b) == SCORE[b]
                pe.wait_ge(v_dve, KB - 4 + b + 1)
                scores(0, b)
            make_z(NG - 1)
            attention_tile(0, first=True)
            with pe.Fori(1, TILES - 1) as t:
                attention_tile(t)
            attention_tile(TILES - 1, last=True)

            def w(m, c, e):
                start = (m * C + c) * D + e * P
                return w_hi[:, start:start + P], w_lo[:, start:start + P]

            def up(u, k):
                if k == 0:
                    pe.wait_ge(xs_dve, C * (u + 1))
                for e in range(C):
                    n = 2 * UNITS * u + 2 * k + e
                    wait(pe, u_act, 2 * (n - 1))
                    product(ps[:, HB[e], :], [w(up_index(k), c, e) + (xs_hi[:, c, :], xs_lo[:, c, :])
                                              for c in range(C)]).then_inc(u_mm, 1)

            def gate(u, k):
                pe.wait_ge(u_dve, 2 * UNITS * u + 2 * k + 2)
                for e in range(C):
                    n = 2 * UNITS * u + 2 * k + e
                    wait(pe, g_act, n - 1)
                    product(ps[:, GB[e], :], [w(gate_index(k), c, e) + (h_hi[:, k % 2, c, :], h_lo[:, k % 2, c, :])
                                              for c in range(C)]).then_inc(g_mm, 1)

            def down(u, k, banks=DB):
                n = (UNITS - 1) * u + k - 1
                pe.wait_ge(a_split_lo, 2 * n + 2)
                if k == 1:
                    pe.wait_ge(wT_act, u + 1)
                for i in range(TG):
                    b = i // 2
                    if i % 2 == 0 and banks is DB:
                        wait(pe, y_dve, 2 * (n - 1) + b + 1)
                    dst = ps[:, banks[b], (i % 2) * D:(i % 2) * D + D]
                    j = 0
                    for c in range(C):
                        start = (down_index(k) * C + c) * D
                        wh, wl = w_hi[:, start:start + D], w_lo[:, start:start + D]
                        ah, al = (v[:, k % 2, c, i * P:i * P + P] for v in (a_hi, a_lo))
                        for a, ww in ((ah, wh), (ah, wl), (al, wh)):
                            m = nc.tensor.matmul(dst, a, ww, start=(j == 0), stop=(j == 5 and k > 1))
                            j += 1
                    if k == 1:
                        m = nc.tensor.matmul(dst, wT[:, i * P:i * P + P], bd[:], start=False, stop=True)
                    if i % 2:
                        m.then_inc(d_mm, 1)

            def router_weights(u):
                pe.wait_ge(r_ready, 3 * u + 3)
                for i in range(TG):
                    m = nc.tensor.transpose(ps[:, RB, i * P:i * P + P], wp[:, i, :], ident[:])
                m.then_inc(wT_mm, 1)

            def group(u, first=False, last=False):
                for k in range(UNITS):
                    if k < UNITS - 1:
                        up(u, k + 1)
                    elif not last:
                        up(u + 1, 0)
                    gate(u, k)
                    if k == UNITS - 1 and not last:
                        router_gates(u + 1)
                    if k >= 2:
                        down(u, k - 1)
                    if k == 0 and not first:
                        down(u - 1, UNITS - 1)
                    if k == 1:
                        router_weights(u)
                    if k == 5 and not last:
                        input_transposes(u + 1)

            def router_gates(u):
                for i in range(TG):
                    for c in range(C):
                        xh, xl = xs_hi[:, c, i * P:i * P + P], xs_lo[:, c, i * P:i * P + P]
                        w_both = wr[:, bass.ds(u // NG, 1), c, :, :].rearrange("p a h e -> p (a h e)")
                        w_high = wr[:, bass.ds(u // NG, 1), c, 0, :].rearrange("p a e -> p (a e)")
                        nc.tensor.matmul(ps[:, RB, i * P:i * P + 2 * NE], xh, w_both, start=(c == 0), stop=False)
                        m = nc.tensor.matmul(ps[:, RB, i * P:i * P + NE], xl, w_high, start=False, stop=(c == C - 1))
                m.then_inc(r_mm, 1)

            pe.wait_ge(w_done, TILES)
            up(0, 0)
            router_gates(0)
            group(0, first=True)
            with pe.Fori(1, GROUPS - 1) as u:
                group(u)
            group(GROUPS - 1, last=True)

            down(GROUPS - 1, UNITS - 1, XB)


def kernel(**inputs):
    import concourse.bacc as bacc
    from concourse.bass_utils import run_bass_kernel_spmd as run

    a = {k: np.asarray(v) for k, v in inputs.items()}

    def rows_by_partition(w, p):
        k = w.shape[0] // p
        return w.reshape(k, p, w.shape[1]).transpose(1, 0, 2).reshape(p, k * w.shape[1])

    def columns(v):
        return v.reshape(-1, C, P).transpose(2, 0, 1).reshape(P, -1)

    y = a["ctx_768"][0].T
    ctxT = np.stack([y[:P], np.concatenate([y[P:], y[P:]])], axis=1)

    def parts(w, bias):
        e = np.zeros((D, P), w.dtype)
        e[:, :DR], e[:, ONE_HI], e[:, ONE_LO] = w[:, P:], bias, bias
        return np.concatenate([w[:, :P], w[:, P:], w[:, P:], e], axis=1)

    w_att = np.concatenate([rows_by_partition(w, P) for w in (
        a["L0_xattn_Wq"].T, parts(a["L0_xattn_Wk"].T, a["L0_xattn_bk"]), parts(a["L0_xattn_Wv"].T, a["L0_xattn_bv"]),
        a["L0_xattn_Wo"])], axis=1)
    b_o = np.zeros((P, D), np.float32)
    b_o[[ONE_HI, ONE_LO]] = a["L0_xattn_bo"]
    ws = [a["L0_ffn_share_Wup"][:, 0:D], a["L0_ffn_share_Wup"][:, D:2 * D], a["L0_ffn_share_Wg"], a["L0_ffn_share_Wdown"]]
    for e in range(NE):
        ws += [a["L0_ffn_exp_Wup"][e], a["L0_ffn_exp_Wg"][e], a["L0_ffn_exp_Wdown"][e]]
    w_ffn = np.concatenate([rows_by_partition(m, P) for m in ws], axis=1)
    sbg = a["L0_ffn_share_bg"]
    cols = np.concatenate([columns(v) for v in (
        a["L0_xattn_bq"], a["L0_ffn_share_bup"], a["L0_ffn_exp_bup"],
        sbg, sbg, a["L0_ffn_exp_bg"])], axis=1)
    rows = np.concatenate([a["L0_ffn_router_b"].reshape(-1),
                           a["L0_ffn_gate_bias"].reshape(-1), a["g_xattn"], a["g_ffn"]])[None, :]
    w_router = a["L0_ffn_router_W"].reshape(ROUNDS, C, P, NE).transpose(2, 0, 1, 3).reshape(P, -1)
    arrays = {"x": a["x"][0], "ctxT": ctxT, "w_att": w_att, "b_o": b_o, "w_ffn": w_ffn, "cols": cols, "rows": rows,
              "w_router": w_router, "b_down": np.concatenate([a["L0_ffn_exp_bdown"], a["L0_ffn_share_bdown"][None]]),
              "norm_rows": a["L0_ffn_norm_w"].reshape(1, -1)}
    arrays = {k: np.ascontiguousarray(v) for k, v in arrays.items()}
    assert arrays["cols"].shape == (P, NCOL) and arrays["rows"].shape == (1, NROW)

    nc = bacc.Bacc("TRN2", target_bir_lowering=False, num_devices=1)
    args = [nc.dram_tensor(k, v.shape, mybir.dt.from_np(v.dtype), kind="ExternalInput").ap() for k, v in arrays.items()]
    o = nc.dram_tensor("out", (NTOK, D), F32, kind="ExternalOutput").ap()
    build(nc, *args, o)
    r = run(nc, [arrays], core_ids=[0])
    return r.results[0]["out"].reshape(1, NTOK, D)
```
